# Optimizing a Trainium2 kernel written in Bass

```python
import numpy as np
import jax
import jax.numpy as jnp

def _softmax(x, axis=-1):
    return jax.nn.softmax(x, axis=axis)

def _gelu(x):
    return jax.nn.gelu(x, approximate=True)

def _silu(x):
    return jax.nn.silu(x)

def _sigmoid(x):
    return jax.nn.sigmoid(x)

def _layernorm(x, axis=-1, eps=1e-05):
    m = jnp.mean(x, axis=axis, keepdims=True)
    v = jnp.var(x, axis=axis, keepdims=True)
    return (x - m) / jnp.sqrt(v + eps)

def _scatter_add(tgt, idx, src, axis=0):
    return tgt.at[idx].add(src)

def _segment_sum(src, seg, n):
    return jax.ops.segment_sum(src, seg, n)
kernel_name = 'mk_cond_seq_d2_seqx_r2_dc1fb7'

def setup_inputs(seed: int=0):
    np.random.seed(seed)
    _w = jnp.asarray

    def _rec_inputs():
        import jax
        import jax.numpy as jnp
        _rk = jax.random.key(seed)
        x = -0.000125 + 0.9999 * jax.random.normal(jax.random.fold_in(_rk, 1), (8, 512, 512), jnp.float32)
        _lenS = 512 - jax.random.randint(jax.random.fold_in(_rk, 7), (8,), 0, max(1, 512 // 4) + 1, jnp.int32)
        _lenS2 = 512 - jax.random.randint(jax.random.fold_in(_rk, 8), (8,), 0, max(1, 512 // 4) + 1, jnp.int32)
        condB_vol = -0.363024 + 1.06491 * jax.random.normal(jax.random.fold_in(_rk, 11), (8,), jnp.float32)
        itok_B_34_63 = jax.random.randint(jax.random.fold_in(_rk, 13), (8,), 34, 64, jnp.int32)
        fside_Bx16xSxS_0 = -1.47943e-05 + 1.00017 * jax.random.normal(jax.random.fold_in(_rk, 14), (8, 16, 512, 512), jnp.float32)
        _validS = jnp.arange(512)[None, :] < _lenS[:, None]
        _validS2 = jnp.arange(512)[None, :] < _lenS2[:, None]
        _causal = jnp.tril(jnp.ones((512, 512), dtype=bool))
        mask_Bx1xSxS_bk0 = jnp.logical_not(jnp.broadcast_to(_validS[:, None, None, :], (8, 1, 512, 512)))
        return (x, condB_vol, itok_B_34_63, fside_Bx16xSxS_0, mask_Bx1xSxS_bk0)
    x, condB_vol, itok_B_34_63, fside_Bx16xSxS_0, mask_Bx1xSxS_bk0 = _rec_inputs()

    def _L0_cond_setup():
        import jax, jax.numpy as jnp
        import numpy as np
        N_Q = 4
        N_LAYERS = 2
        PI = 3.141592653589793
        DIM = 2 ** N_Q

        def _cnot_mat(c, t, n=N_Q):
            M = np.zeros((2 ** n, 2 ** n), dtype=np.complex64)
            for b in range(2 ** n):
                bits = [b >> n - 1 - w & 1 for w in range(n)]
                if bits[c]:
                    bits[t] ^= 1
                nb = sum((bit << n - 1 - w for w, bit in enumerate(bits)))
                M[nb, b] = 1.0
            return M
        _CNOTS = [[_cnot_mat(i, (i + r) % N_Q) for i in range(N_Q)] for r in (1, 2)]
        _ZSIGN = np.array([[1.0 - 2.0 * (b >> N_Q - 1 - w & 1) for w in range(N_Q)] for b in range(DIM)], dtype=np.float32)

        def _rot(p, t, o):
            c = jnp.cos(t / 2).astype(jnp.complex64)
            s = jnp.sin(t / 2).astype(jnp.complex64)
            e = lambda a: jnp.exp(1j * a).astype(jnp.complex64)
            return jnp.stack([jnp.stack([e(-(o + p) / 2) * c, -e((p - o) / 2) * s]), jnp.stack([e((o - p) / 2) * s, e((o + p) / 2) * c])])

        def _vqc(angles, weights):
            half = angles / 2
            c = jnp.cos(half).astype(jnp.complex64)
            s = jnp.sin(half).astype(jnp.complex64)
            v = jnp.stack([c, -1j * s], axis=-1)
            state = v[:, 0]
            for w in range(1, N_Q):
                state = (state[:, :, None] * v[:, w][:, None, :]).reshape(state.shape[0], -1)
            U = jnp.eye(DIM, dtype=jnp.complex64)
            for l in range(N_LAYERS):
                R = _rot(*weights[l, 0])
                for w in range(1, N_Q):
                    R = jnp.kron(R, _rot(*weights[l, w]))
                U = R @ U
                for C in _CNOTS[l]:
                    U = jnp.asarray(C) @ U
            state = state @ U.T
            probs = state.real ** 2 + state.imag ** 2
            return probs @ jnp.asarray(_ZSIGN)
        key = jax.random.key(seed)
        ks = jax.random.split(key, 8)
        B, T, C, H = (64, 256, 512, 2048)
        return {'x': jax.random.normal(ks[0], (B, T, C), jnp.float32), 'vol': jax.random.normal(ks[1], (B,), jnp.float32), 'w1': jax.random.normal(ks[2], (C, H), jnp.float32) * 0.02, 'b1': jnp.zeros((H,), jnp.float32), 'w2': jax.random.normal(ks[3], (H, C), jnp.float32) * 0.02, 'b2': jnp.zeros((C,), jnp.float32), 'pd_w': jax.random.normal(ks[4], (C, N_Q), jnp.float32) * 0.02, 'pd_b': jnp.zeros((N_Q,), jnp.float32), 'vqc_w': jax.random.uniform(ks[5], (N_LAYERS, N_Q, 3), jnp.float32, 0.0, 2 * PI), 'pu_w': jax.random.normal(ks[6], (N_Q, C), jnp.float32) * 0.02, 'pu_b': jnp.zeros((C,), jnp.float32), 'q_scale': jnp.full((1,), 0.1, jnp.float32), 'ln_g': jnp.ones((C,), jnp.float32), 'ln_b': jnp.zeros((C,), jnp.float32)}
    _L0_cond_all = _L0_cond_setup()
    _L0_cond_in = {k: v for k, v in _L0_cond_all.items() if k in ('w1', 'b1', 'w2', 'b2', 'pd_w', 'pd_b', 'vqc_w', 'pu_w', 'pu_b', 'q_scale', 'ln_g', 'ln_b')}
    del _L0_cond_all

    def _L1_cond_setup():
        import jax, jax.numpy as jnp
        import numpy as np
        import math
        D_MODEL = 512
        N_HEAD = 16
        HEAD_DIM = D_MODEL // N_HEAD
        D_FF = 2048
        NUM_STEPS = 100.0
        RESCALE = 4000.0
        EPS = 1e-05

        def _sin_emb(t):
            half = D_MODEL // 2
            x = t.astype(jnp.float32) / NUM_STEPS * RESCALE
            freqs = jnp.exp(jnp.arange(half, dtype=jnp.float32) * (-math.log(10000.0) / (half - 1)))
            e = x[:, None] * freqs[None, :]
            return jnp.concatenate([jnp.sin(e), jnp.cos(e)], axis=-1)

        def _ln(x):
            m = jnp.mean(x, axis=-1, keepdims=True)
            v = jnp.var(x, axis=-1, keepdims=True)
            return (x - m) / jnp.sqrt(v + EPS)

        def _gelu2(x):
            return x * jax.nn.sigmoid(1.702 * x)
        key = jax.random.key(seed)
        ks = jax.random.split(key, 24)
        B, S, D, F = (4, 256, D_MODEL, D_FF)
        std = 0.02
        inp = {'src': jax.random.normal(ks[0], (B, S, D), dtype=jnp.float32), 'src_mask': jax.random.randint(ks[1], (B, 1, S, S), 0, 2).astype(bool), 'timestep': jax.random.randint(ks[2], (B,), 0, 100, dtype=jnp.int32), 'attention_bias': jax.random.normal(ks[3], (B, N_HEAD, S, S), dtype=jnp.float32), 'W_ada': jax.random.normal(ks[4], (D, 2 * D), dtype=jnp.float32) * std, 'b_ada': jnp.zeros((2 * D,), dtype=jnp.float32), 'Wq': jax.random.normal(ks[5], (D, D), dtype=jnp.float32) * std, 'bq': jnp.zeros((D,), dtype=jnp.float32), 'Wk': jax.random.normal(ks[6], (D, D), dtype=jnp.float32) * std, 'bk': jnp.zeros((D,), dtype=jnp.float32), 'Wv': jax.random.normal(ks[7], (D, D), dtype=jnp.float32) * std, 'bv': jnp.zeros((D,), dtype=jnp.float32), 'Wo': jax.random.normal(ks[8], (D, D), dtype=jnp.float32) * std, 'bo': jnp.zeros((D,), dtype=jnp.float32), 'W1': jax.random.normal(ks[9], (D, F), dtype=jnp.float32) * std, 'b1': jnp.zeros((F,), dtype=jnp.float32), 'W2': jax.random.normal(ks[10], (F, D), dtype=jnp.float32) * std, 'b2': jnp.zeros((D,), dtype=jnp.float32), 'g2': jnp.ones((D,), dtype=jnp.float32), 'beta2': jnp.zeros((D,), dtype=jnp.float32)}
        return inp
    _L1_cond_all = _L1_cond_setup()
    _L1_cond_in = {k: v for k, v in _L1_cond_all.items() if k in ('W_ada', 'b_ada', 'Wq', 'bq', 'Wk', 'bk', 'Wv', 'bv', 'Wo', 'bo', 'W1', 'b1', 'W2', 'b2', 'g2', 'beta2')}
    del _L1_cond_all
    return {'x': x, 'condB_vol': condB_vol, 'itok_B_34_63': itok_B_34_63, 'fside_Bx16xSxS_0': fside_Bx16xSxS_0, 'mask_Bx1xSxS_bk0': mask_Bx1xSxS_bk0, 'L0_cond_w1': _L0_cond_in['w1'], 'L0_cond_b1': _L0_cond_in['b1'], 'L0_cond_w2': _L0_cond_in['w2'], 'L0_cond_b2': _L0_cond_in['b2'], 'L0_cond_pd_w': _L0_cond_in['pd_w'], 'L0_cond_pd_b': _L0_cond_in['pd_b'], 'L0_cond_vqc_w': _L0_cond_in['vqc_w'], 'L0_cond_pu_w': _L0_cond_in['pu_w'], 'L0_cond_pu_b': _L0_cond_in['pu_b'], 'L0_cond_q_scale': _L0_cond_in['q_scale'], 'L0_cond_ln_g': _L0_cond_in['ln_g'], 'L0_cond_ln_b': _L0_cond_in['ln_b'], 'L1_cond_W_ada': _L1_cond_in['W_ada'], 'L1_cond_b_ada': _L1_cond_in['b_ada'], 'L1_cond_Wq': _L1_cond_in['Wq'], 'L1_cond_bq': _L1_cond_in['bq'], 'L1_cond_Wk': _L1_cond_in['Wk'], 'L1_cond_bk': _L1_cond_in['bk'], 'L1_cond_Wv': _L1_cond_in['Wv'], 'L1_cond_bv': _L1_cond_in['bv'], 'L1_cond_Wo': _L1_cond_in['Wo'], 'L1_cond_bo': _L1_cond_in['bo'], 'L1_cond_W1': _L1_cond_in['W1'], 'L1_cond_b1': _L1_cond_in['b1'], 'L1_cond_W2': _L1_cond_in['W2'], 'L1_cond_b2': _L1_cond_in['b2'], 'L1_cond_g2': _L1_cond_in['g2'], 'L1_cond_beta2': _L1_cond_in['beta2']}

def reference(x, condB_vol, itok_B_34_63, fside_Bx16xSxS_0, mask_Bx1xSxS_bk0, L0_cond_w1, L0_cond_b1, L0_cond_w2, L0_cond_b2, L0_cond_pd_w, L0_cond_pd_b, L0_cond_vqc_w, L0_cond_pu_w, L0_cond_pu_b, L0_cond_q_scale, L0_cond_ln_g, L0_cond_ln_b, L1_cond_W_ada, L1_cond_b_ada, L1_cond_Wq, L1_cond_bq, L1_cond_Wk, L1_cond_bk, L1_cond_Wv, L1_cond_bv, L1_cond_Wo, L1_cond_bo, L1_cond_W1, L1_cond_b1, L1_cond_W2, L1_cond_b2, L1_cond_g2, L1_cond_beta2):
    import jax
    import jax.numpy as jnp

    def _L0_cond_ref(x, vol, w1, b1, w2, b2, pd_w, pd_b, vqc_w, pu_w, pu_b, q_scale, ln_g, ln_b):
        import jax, jax.numpy as jnp
        import numpy as np
        N_Q = 4
        N_LAYERS = 2
        PI = 3.141592653589793
        DIM = 2 ** N_Q

        def _cnot_mat(c, t, n=N_Q):
            M = np.zeros((2 ** n, 2 ** n), dtype=np.complex64)
            for b in range(2 ** n):
                bits = [b >> n - 1 - w & 1 for w in range(n)]
                if bits[c]:
                    bits[t] ^= 1
                nb = sum((bit << n - 1 - w for w, bit in enumerate(bits)))
                M[nb, b] = 1.0
            return M
        _CNOTS = [[_cnot_mat(i, (i + r) % N_Q) for i in range(N_Q)] for r in (1, 2)]
        _ZSIGN = np.array([[1.0 - 2.0 * (b >> N_Q - 1 - w & 1) for w in range(N_Q)] for b in range(DIM)], dtype=np.float32)

        def _rot(p, t, o):
            c = jnp.cos(t / 2).astype(jnp.complex64)
            s = jnp.sin(t / 2).astype(jnp.complex64)
            e = lambda a: jnp.exp(1j * a).astype(jnp.complex64)
            return jnp.stack([jnp.stack([e(-(o + p) / 2) * c, -e((p - o) / 2) * s]), jnp.stack([e((o - p) / 2) * s, e((o + p) / 2) * c])])

        def _vqc(angles, weights):
            half = angles / 2
            c = jnp.cos(half).astype(jnp.complex64)
            s = jnp.sin(half).astype(jnp.complex64)
            v = jnp.stack([c, -1j * s], axis=-1)
            state = v[:, 0]
            for w in range(1, N_Q):
                state = (state[:, :, None] * v[:, w][:, None, :]).reshape(state.shape[0], -1)
            U = jnp.eye(DIM, dtype=jnp.complex64)
            for l in range(N_LAYERS):
                R = _rot(*weights[l, 0])
                for w in range(1, N_Q):
                    R = jnp.kron(R, _rot(*weights[l, w]))
                U = R @ U
                for C in _CNOTS[l]:
                    U = jnp.asarray(C) @ U
            state = state @ U.T
            probs = state.real ** 2 + state.imag ** 2
            return probs @ jnp.asarray(_ZSIGN)
        B, T, C = x.shape
        ffn_out = x + jax.nn.gelu(x @ w1 + b1, approximate=False) @ w2 + b2
        p = jnp.clip(x @ pd_w + pd_b, -10.0, 10.0)
        q_in = jax.nn.sigmoid(p) * PI
        q_out = _vqc(q_in.reshape(-1, N_Q), vqc_w).reshape(B, T, N_Q)
        xq = x + (q_out @ pu_w + pu_b) * jnp.abs(q_scale)
        mask = (vol > 0.5)[:, None, None]
        out = jnp.where(mask, xq, ffn_out)
        mu = out.mean(-1, keepdims=True)
        var = out.var(-1, keepdims=True)
        return (out - mu) * jax.lax.rsqrt(var + 1e-05) * ln_g + ln_b

    def _L1_cond_ref(src, src_mask, timestep, attention_bias, W_ada, b_ada, Wq, bq, Wk, bk, Wv, bv, Wo, bo, W1, b1, W2, b2, g2, beta2):
        import jax, jax.numpy as jnp
        import numpy as np
        import math
        D_MODEL = 512
        N_HEAD = 16
        HEAD_DIM = D_MODEL // N_HEAD
        D_FF = 2048
        NUM_STEPS = 100.0
        RESCALE = 4000.0
        EPS = 1e-05

        def _sin_emb(t):
            half = D_MODEL // 2
            x = t.astype(jnp.float32) / NUM_STEPS * RESCALE
            freqs = jnp.exp(jnp.arange(half, dtype=jnp.float32) * (-math.log(10000.0) / (half - 1)))
            e = x[:, None] * freqs[None, :]
            return jnp.concatenate([jnp.sin(e), jnp.cos(e)], axis=-1)

        def _ln(x):
            m = jnp.mean(x, axis=-1, keepdims=True)
            v = jnp.var(x, axis=-1, keepdims=True)
            return (x - m) / jnp.sqrt(v + EPS)

        def _gelu2(x):
            return x * jax.nn.sigmoid(1.702 * x)
        B, S, D = src.shape
        emb = jax.nn.silu(_sin_emb(timestep)) @ W_ada + b_ada
        scale, shift = jnp.split(emb[:, None, :], 2, axis=-1)
        x = _ln(src) * (1.0 + scale) + shift
        q = (x @ Wq + bq).reshape(B, S, N_HEAD, HEAD_DIM).transpose(0, 2, 1, 3)
        k = (x @ Wk + bk).reshape(B, S, N_HEAD, HEAD_DIM).transpose(0, 2, 1, 3)
        v = (x @ Wv + bv).reshape(B, S, N_HEAD, HEAD_DIM).transpose(0, 2, 1, 3)
        scores = jnp.einsum('bhqd,bhkd->bhqk', q / math.sqrt(HEAD_DIM), k)
        scores = scores + attention_bias
        scores = jnp.where(src_mask, -jnp.inf, scores.astype(jnp.float32))
        probs = jax.nn.softmax(scores, axis=-1).astype(v.dtype)
        ctx = jnp.einsum('bhqk,bhkd->bhqd', probs, v)
        ctx = ctx.transpose(0, 2, 1, 3).reshape(B, S, D)
        x = x + (ctx @ Wo + bo)
        h = _ln(x) * g2 + beta2
        ff = _gelu2(h @ W1 + b1) @ W2 + b2
        return x + ff
    x = _L0_cond_ref(x, condB_vol, L0_cond_w1, L0_cond_b1, L0_cond_w2, L0_cond_b2, L0_cond_pd_w, L0_cond_pd_b, L0_cond_vqc_w, L0_cond_pu_w, L0_cond_pu_b, L0_cond_q_scale, L0_cond_ln_g, L0_cond_ln_b)
    x = _L1_cond_ref(x, mask_Bx1xSxS_bk0, itok_B_34_63, fside_Bx16xSxS_0, L1_cond_W_ada, L1_cond_b_ada, L1_cond_Wq, L1_cond_bq, L1_cond_Wk, L1_cond_bk, L1_cond_Wv, L1_cond_bv, L1_cond_Wo, L1_cond_bo, L1_cond_W1, L1_cond_b1, L1_cond_W2, L1_cond_b2, L1_cond_g2, L1_cond_beta2)
    return x

_drawn_inputs = setup_inputs


def setup_inputs(seed=0):
    import zlib

    import numpy as np

    out = dict(_drawn_inputs(seed))
    spreads = {'L0_cond_b1': (0.0, 0.1),
     'L0_cond_b2': (0.0, 0.1),
     'L0_cond_pd_b': (0.0, 2.0),
     'L0_cond_pu_b': (0.0, 0.8),
     'L0_cond_ln_g': (1.0, 0.2),
     'L0_cond_ln_b': (0.0, 0.1),
     'L1_cond_b_ada': (0.0, 0.1),
     'L1_cond_bq': (0.0, 0.8),
     'L1_cond_bk': (0.0, 2.0),
     'L1_cond_bv': (0.0, 0.1),
     'L1_cond_bo': (0.0, 0.1),
     'L1_cond_b1': (0.0, 0.1),
     'L1_cond_b2': (0.0, 0.1),
     'L1_cond_g2': (1.0, 0.2),
     'L1_cond_beta2': (0.0, 0.332)}
    factors = {'fside_Bx16xSxS_0': 4.567,
     'L0_cond_pd_w': 189.131,
     'L0_cond_vqc_w': 64.0,
     'L0_cond_pu_w': 184.519,
     'L1_cond_Wq': 8.0,
     'L1_cond_Wk': 8.0}
    for name, (base, spread) in spreads.items():
        noise = np.random.default_rng([zlib.crc32(name.encode()), seed]).standard_normal(out[name].shape)
        drawn = base * np.exp(spread * noise) if base else spread * noise
        out[name] = jnp.asarray(drawn.astype(out[name].dtype))
    for name, factor in factors.items():
        out[name] = (out[name] * factor).astype(out[name].dtype)
    return out
```

```python
from contextlib import ExitStack

import numpy as np

import concourse.bass as bass
from concourse import mybir

F32 = mybir.dt.float32
F32R = mybir.dt.float32r
BF16 = mybir.dt.bfloat16
U8 = mybir.dt.uint8
I32 = mybir.dt.int32
ALU = mybir.AluOpType
ACT = mybir.ActivationFunctionType
AX = mybir.AxisListType

P = 128
B, S, D, F, H = 8, 512, 512, 2048, 16
HD = D // H
KT = D // P
TT = S // P
FT = F // P
WIRES, LAYERS = 4, 2
DIM = 2 ** WIRES
EPS = 1e-5
PI = float(np.pi)
INV_2PI = float(1 / (2 * np.pi))
ROUND = 1.5 * 2.0 ** 23
C1 = 6.28125
C2 = float(np.floor((2 * np.pi - C1) * 2 ** 20) / 2 ** 20)
C3 = float(2 * np.pi - C1 - C2)
PI_BELOW = 3.1415925
MASKED = -3e38
Q_SCALE = float(HD) ** -0.5

DENSE = ["w1", "b1", "w2", "b2"]


def each_batch(eng, body):
    body(0, True, False)
    with eng.Fori(1, B - 1) as b:
        body(b, False, False)
    body(B - 1, False, True)


def rows(t):
    return t.rearrange("(t p) n -> p t n", p=P)


def wait_apart(eng, passed, *waits):
    for sem, value in waits:
        eng.wait_ge(sem, value)
    eng.sem_inc(passed, 1)


class Chain:

    def __init__(self, eng, sem):
        self.eng, self.sem, self.base, self.n = eng, sem, 0, 0

    def at(self, base):
        self.base, self.n = base, 0

    def step(self, ins):
        self.n += 1
        ins.then_inc(self.sem, 1)

    def wait(self):
        self.eng.wait_ge(self.sem, self.base + self.n)

    def __call__(self, ins):
        self.step(ins)
        self.wait()


def setup_stage(nc, keep, t, C, scratch):
    with ExitStack() as ctx:
        sb = lambda n, s, d=F32: ctx.enter_context(nc.sbuf_tensor(n, s, d))
        ps = lambda n: ctx.enter_context(nc.psum_tensor(n, [P, 512], F32))
        sem = lambda n: ctx.enter_context(nc.semaphore(n))
        NE = 2 * KT // 2 * B
        NV = LAYERS * WIRES * DIM + 4
        steps_i = sb("steps_i", [P, B], I32)
        steps = sb("steps", [P, B])
        freq = sb("freq", [P, 2])
        ang, off, turns, sine = (sb(f"emb_{n}", [P, KT, B]) for n in ("ang", "off", "turns", "sine"))
        sig = sb("emb_sig", [P, KT, B])
        wada = sb("wada", [P, KT, 2 * D])
        bada = sb("bada", [B, 2 * D])
        ada = sb("ada", [B, 2 * D])
        vol = sb("vol", [P, B])
        qs = sb("qs", [P, 1])
        vw = sb("vw", [DIM, LAYERS * WIRES * 3])
        vcoef = sb("vcoef", [DIM, 2, LAYERS * WIRES * 3])
        voff = sb("voff", [DIM, NV])
        vprod = sb("vprod", [DIM, 2, LAYERS * WIRES * 3])
        vang, vturn, vsin = (sb(f"v_{n}", [DIM, NV]) for n in ("ang", "turn", "sin"))
        pair = sb("vpair", [DIM, LAYERS, 2, DIM])
        gates = sb("vgates", [DIM, LAYERS, DIM])
        rot2 = sb("vrot2", [DIM, 2, DIM])
        part = sb("vpart", [DIM, 2, DIM])
        zs = sb("zs", [WIRES, 2 * DIM])
        puw = sb("puw", [WIRES, D])
        ps_a, ps_b, ps_v, ps_z = ps("ps_a"), ps("ps_b"), ps("ps_v"), ps("ps_z")
        s_in, s_chain, s_x, s_sin, s_sig, s_silu, s_ada, s_rows, s_out = map(
            sem, ("setup_in", "setup_chain", "angles", "sines", "sigmoids", "silu", "ada_mm", "ada_rows", "ada_out"))
        s_vw, s_vmm, s_z = map(sem, ("v_ready", "v_mm", "z_mm"))
        block = ctx.enter_context(nc.Block())

        @block.sync
        def _(sp):
            loads = [
                (keep.ident[:, :], C["ident"]), (freq[:, :], C["freqs"]), (voff[:, :], C["voff"]),
                (vcoef[:, :, :], C["vcoef"]), (zs[:, :], C["zsign"]),
                (steps_i[:, :], t["itok_B_34_63"].partition_broadcast(P)),
                (vol[:, :], t["condB_vol"].partition_broadcast(P)),
                (qs[:, :], t["L0_cond_q_scale"].partition_broadcast(P)),
                (vw[:, :], t["L0_cond_vqc_w"].rearrange("l w a -> (l w a)").partition_broadcast(DIM)),
                (puw[:, :], t["L0_cond_pu_w"]),
                (wada[:, :, :], t["L1_cond_W_ada"].rearrange("(k p) n -> p k n", p=P)),
                (bada[:, :], t["L1_cond_b_ada"].partition_broadcast(B)),
            ]
            for dst, src in loads:
                sp.dma_start(dst, src).then_inc(s_in, 16)
            sp.wait_ge(s_rows, 2)
            sp.dma_start(scratch["ada"], ada[:, :]).then_inc(s_out, 16)
            sp.wait_ge(s_out, 16)

        all_in = 16 * 12

        @block.vector
        def _(dve):
            link = Chain(dve, s_chain)

            def reduce_angle(ang, off, turns):
                link(nc.vector.tensor_tensor(turns, ang, off, ALU.add))
                link(nc.vector.tensor_scalar(turns, turns, INV_2PI, None, ALU.mult))
                link(nc.vector.tensor_scalar(turns, turns, ROUND, None, ALU.add))
                link(nc.vector.tensor_scalar(turns, turns, ROUND, None, ALU.subtract))
                for c in (C1, C2, C3):
                    link(nc.vector.scalar_tensor_tensor(ang, turns, -c, ang, ALU.mult, ALU.add))
                link(nc.vector.tensor_tensor(ang, ang, off, ALU.add))
                link(nc.vector.tensor_scalar(ang, ang, PI_BELOW, -PI_BELOW, ALU.min, ALU.max))

            dve.wait_ge(s_in, all_in)
            link(nc.vector.tensor_copy(steps[:, :], steps_i[:, :]))
            link(nc.vector.tensor_scalar(steps[:, :], steps[:, :], 4000.0 / 100.0, None, ALU.mult))
            for k in range(KT):
                link(nc.vector.tensor_scalar(ang[:, k, :], steps[:, :], freq[:, k % 2:k % 2 + 1], None, ALU.mult))
            link(nc.vector.memset(off[:, 0:2, :], 0.0))
            link(nc.vector.memset(off[:, 2:4, :], PI / 2))
            reduce_angle(ang[:, :, :], off[:, :, :], turns[:, :, :])
            n = LAYERS * WIRES * DIM
            theta = vw[:, :].rearrange("p (g a) -> p g a", a=3)[:, :, 1:2].to_broadcast([DIM, LAYERS * WIRES, DIM])
            link(nc.vector.tensor_scalar(vang[:, 0:n].rearrange("p (g b) -> p g b", b=DIM), theta, 0.5, None, ALU.mult))
            for c in range(2):
                link(nc.vector.tensor_tensor(vprod[:, c, :], vcoef[:, c, :], vw[:, :], ALU.mult))
            for c in range(2):
                for d in range(2):
                    link(nc.vector.tensor_reduce(vang[:, n + 2 * c + d:n + 2 * c + d + 1], vprod[:, c, :], AX.X, ALU.add))
            reduce_angle(vang[:, :], voff[:, :], vturn[:, :])
            link(nc.vector.tensor_scalar(keep.take_q[:, :], vol[:, :], 0.5, None, ALU.is_gt))
            link(nc.vector.tensor_scalar(keep.take_f[:, :], keep.take_q[:, :], -1.0, 1.0, ALU.mult, ALU.add))
            link(nc.vector.scalar_tensor_tensor(qs[:, :], qs[:, :], -1.0, qs[:, :], ALU.mult, ALU.max))
            nc.vector.tensor_scalar(keep.q_factor[:, :], keep.take_q[:, :], qs[:, 0:1], None, ALU.mult).then_inc(s_x, 1)
            dve.wait_ge(s_sig, 1)
            nc.vector.tensor_tensor(sig[:, :, :], sig[:, :, :], sine[:, :, :], ALU.mult).then_inc(s_silu, 1)
            dve.wait_ge(s_sin, 2)
            g = vsin[:, 0:n].rearrange("p (l u v b) -> p l u v b", l=LAYERS, u=2, v=2)
            for l in range(LAYERS):
                link(nc.vector.tensor_tensor(pair[:, l, :, :], g[:, l, :, 0, :], g[:, l, :, 1, :], ALU.mult))
            link(nc.vector.tensor_tensor(gates[:, :, :], pair[:, :, 0, :], pair[:, :, 1, :], ALU.mult))
            for c in range(2):
                link(nc.vector.tensor_scalar(rot2[:, c, :], gates[:, 1, :], vsin[:, n + 1 - c:n + 2 - c], None, ALU.mult))
            nc.vector.tensor_copy(gates[:, 0, :], gates[:, 0, :]).then_inc(s_vw, 1)
            dve.wait_ge(s_vmm, 1)
            re, im = ps_v[0:DIM, 0:DIM], ps_v[0:DIM, DIM:2 * DIM]
            sin_b, cos_b = vsin[:, n + 2:n + 3], vsin[:, n + 3:n + 4]
            link(nc.vector.tensor_scalar(part[:, 0, :], im, sin_b, None, ALU.mult))
            link(nc.vector.tensor_scalar(part[:, 1, :], im, cos_b, None, ALU.mult))
            link(nc.vector.scalar_tensor_tensor(keep.circuit[:, 0:DIM], re, cos_b, part[:, 0, :], ALU.mult, ALU.subtract))
            link(nc.vector.scalar_tensor_tensor(keep.circuit[:, DIM:], re, sin_b, part[:, 1, :], ALU.mult, ALU.add))
            dve.wait_ge(s_z, 1)
            link(nc.vector.tensor_copy(keep.zpu[:, :], ps_z[0:2 * DIM, :]))
            dve.wait_ge(s_ada, 1)
            scale = slice(0, D)
            link(nc.vector.tensor_tensor(ada[:, scale], ps_a[0:B, :], bada[:, scale], ALU.add))
            nc.vector.tensor_scalar(ada[:, scale], ada[:, scale], 1.0, None, ALU.add).then_inc(s_rows, 1)
            nc.vector.tensor_tensor(ada[:, D:], ps_b[0:B, :], bada[:, D:], ALU.add).then_inc(s_rows, 1)

        @block.scalar
        def _(act):
            act.wait_ge(s_x, 1)
            nc.scalar.activation(sine[:, :, :], ang[:, :, :], ACT.Sin).then_inc(s_sin, 1)
            nc.scalar.activation(vsin[:, :], vang[:, :], ACT.Sin).then_inc(s_sin, 1)
            act.wait_ge(s_sin, 1)
            nc.scalar.activation(sig[:, :, :], sine[:, :, :], ACT.Sigmoid).then_inc(s_sig, 1)

        @block.tensor
        def _(pe):
            pe.wait_ge(s_silu, 1)
            pe.wait_ge(s_in, all_in)
            for half, bank in ((0, ps_a), (1, ps_b)):
                for k in range(KT):
                    mm = nc.tensor.matmul(bank[0:B, :], sig[:, k, :], wada[:, k, half * D:(half + 1) * D],
                                          start=k == 0, stop=k == KT - 1)
            mm.then_inc(s_ada, 1)
            pe.wait_ge(s_vw, 1)
            nc.tensor.matmul(ps_v[0:DIM, 0:2 * DIM], gates[:, 0, :], rot2[:, :, :].rearrange("p c j -> p (c j)"),
                             start=True, stop=True).then_inc(s_vmm, 1)
            nc.tensor.matmul(ps_z[0:2 * DIM, :], zs[:, :], puw[:, :], start=True, stop=True).then_inc(s_z, 1)


def split_product(pe, out, pairs, last_stop=True):
    n = len(pairs)
    for i, (ah, al, bh, bl) in enumerate(pairs):
        nc_mm = pe.matmul(out, ah, bh, start=i == 0, stop=False)
        nc_mm = pe.matmul(out, al, bh, start=False, stop=False)
        nc_mm = pe.matmul(out, ah, bl, start=False, stop=i == n - 1)
    return nc_mm


def ffn_stage(nc, keep, t, scratch, l0, out):
    L = "L0" if l0 else "L1"
    name = (lambda n: f"L0_cond_{n}") if l0 else (lambda n: f"L1_cond_{n.replace('w', 'W')}")
    w1, b1, w2, b2 = (t[name(n)] for n in ("w1", "b1", "w2", "b2"))
    func = ACT.Gelu if l0 else ACT.Gelu_apprx_sigmoid
    x_src = t["x"] if l0 else scratch["x2"]
    with ExitStack() as ctx:
        sb = lambda n, s, d=F32: ctx.enter_context(nc.sbuf_tensor(f"{L}_{n}", s, d))
        ps = lambda n: ctx.enter_context(nc.psum_tensor(f"{L}_{n}", [P, 512], F32))
        sem = lambda n: ctx.enter_context(nc.semaphore(f"{L}_{n}"))
        w1h, w1l = sb("w1h", [P, KT, F], F32R), sb("w1l", [P, KT, F], F32R)
        w2h, w2l = sb("w2h", [P, FT, D], F32R), sb("w2l", [P, FT, D], F32R)
        xin = sb("xin", [P, TT, D])
        xres = sb("xres", [P, TT, D])
        xth, xtl = sb("xth", [P, KT, S], F32R), sb("xtl", [P, KT, S], F32R)
        hid = [sb(f"hid{i}", [P, S]) for i in range(2)]
        hh = [sb(f"hh{i}", [P, S], F32R) for i in range(2)]
        hl = [sb(f"hl{i}", [P, S], F32R) for i in range(2)]
        b1c = sb("b1c", [P, FT])
        b2r = sb("b2r", [P, D])
        gain, offset = sb("gain", [P, D]), sb("offset", [P, D])
        stat, mv = sb("stat", [P, TT, 6]), sb("mv", [P, TT, 2])
        power, rstd, shift = sb("power", [P, TT]), sb("rstd", [P, TT]), sb("shift", [P, TT])
        turn = [ps(f"turn{i}") for i in range(2)]
        acc = [ps(f"acc{i}") for i in range(TT)]

        consts_in, w_hi, w_lo, power_set = map(sem, ("consts_in", "w_hi", "w_lo", "power_set"))
        w_in = [sem(f"w_in{i}") for i in range(2)]
        x_in, xres_in, stored = map(sem, ("x_in", "xres_in", "stored"))
        turned, xt_hi, xt_lo = map(sem, ("turned", "xt_hi", "xt_lo"))
        h_mm, h_act, h_hi, h_lo, y_mm, y_out = map(sem, ("h_mm", "h_act", "h_hi", "h_lo", "y_mm", "y_out"))
        row_added, n_var, n_rstd, n_shift, normed = map(sem, ("row_added", "n_var", "n_rstd", "n_shift", "normed"))
        gained, affine_done, dve_chain = map(sem, ("gained", "affine_done", "dve_chain"))
        passed_dve, passed_pe = sem("passed_dve"), sem("passed_pe")
        if l0:
            pub_row, row = sb("pub_row", [P, D]), sb("row", [P, D])
            ada_row = sb("ada_row", [P, 2, D])
            pdw = sb("pdw", [P, KT, WIRES])
            pd = sb("pd", [P, KT, P], F32R)
            pd_zero = sb("pd_zero", [P, KT, P])
            pdb = sb("pdb", [P, WIRES])
            pt = sb("pt", [2 * WIRES, S])
            angle = sb("angle", [P, TT, WIRES])
            cos_sin = sb("cos_sin", [P, 2, TT, WIRES])
            pairs = sb("pairs", [P, 2, TT, 4])
            amp = sb("amp", [P, TT, DIM])
            ampt = sb("ampt", [DIM, S])
            prob = sb("prob", [2 * DIM, S])
            misc = [ps(f"misc{i}") for i in range(2)]
            pd_set, p_mm, pt_out, p_turned, p_out, p_sig, halved, cs_out, amp_out, amp_turned, ampt_out, state_mm, \
                prob_out, up_mm, up_added, row_set, ada_in = map(sem, (
                    "pd_set", "p_mm", "pt_out", "p_turned", "p_out", "p_sig", "halved", "cs_out", "amp_out", "amp_turned",
                    "ampt_out", "state_mm", "prob_out", "up_mm", "up_added", "row_set", "ada_in"))
        across = lambda n: t[n].partition_broadcast(P)
        consts = [(b1c[:, :], b1.rearrange("(m p) -> p m", p=P)), (b2r[:, :], b2.partition_broadcast(P)),
                  (gain[:, :], across("L0_cond_ln_g" if l0 else "L1_cond_g2")),
                  (offset[:, :], across("L0_cond_ln_b" if l0 else "L1_cond_beta2"))]
        if l0:
            consts += [(pub_row[:, :], across("L0_cond_pu_b")), (pdb[:, :], across("L0_cond_pd_b")),
                       (pdw[:, :, :], t["L0_cond_pd_w"].rearrange("(k p) n -> p k n", p=P))]
        passing = [xin, xres]
        chunks = [(w1[k * P:(k + 1) * P, :].rearrange("p (a n) -> p a n", n=D),
                   w1h[:, k, :].rearrange("p (a n) -> p a n", n=D), w1l[:, k, :].rearrange("p (a n) -> p a n", n=D))
                  for k in range(KT)]
        chunks += [(w2[m * P:(m + TT) * P, :].rearrange("(m p) n -> p m n", p=P), w2h[:, m:m + TT, :], w2l[:, m:m + TT, :])
                   for m in range(0, FT, TT)]
        CH = len(chunks)
        block = ctx.enter_context(nc.Block())

        @block.sync
        def _(sp):
            for dst, src in consts:
                sp.dma_start(dst, src).then_inc(consts_in, 16)
            for c, (src, _, _) in enumerate(chunks):
                if c >= 2:
                    sp.wait_ge(w_lo, c - 1)
                sp.dma_start(passing[c % 2][:, :, :], src).then_inc(w_in[c % 2], 16)
            sp.wait_ge(w_lo, CH - 1)
            sp.dma_start(xin[:, :, :], rows(x_src[0])).then_inc(x_in, 16)
            sp.wait_ge(w_lo, CH)

            def body(b, first, last):
                if not last:
                    sp.wait_ge(turned, b * KT + KT)
                    sp.dma_start(xin[:, :, :], rows(x_src[b + 1])).then_inc(x_in, 16)
                if not first:
                    store(b - 1)
                    sp.wait_ge(stored, b * 16)
                sp.dma_start(xres[:, :, :], rows(x_src[b])).then_inc(xres_in, 16)
                if l0:
                    sp.dma_start(ada_row[:, :, :].rearrange("p a n -> p (a n)"),
                                 scratch["ada"][b].partition_broadcast(P)).then_inc(ada_in, 16)

            def store(b):
                if l0:
                    sp.wait_ge(affine_done, b * 2 * TT + 2 * TT)
                else:
                    sp.wait_ge(y_out, b * TT + TT)
                sp.dma_start(rows(out[b]), xres[:, :, :]).then_inc(stored, 16)

            each_batch(sp, body)
            store(B - 1)
            sp.wait_ge(stored, 16 * B)

        @block.gpsimd
        def _(pool):
            nc.gpsimd.memset(power[:, :], -0.5).then_inc(power_set, 1)
            pool.wait_ge(power_set, 1)
            pool.wait_ge(consts_in, 16 * len(consts))

            def norm(buf, n, g, o):
                pool.wait_ge(n_var, n + 1)
                nc.gpsimd.tensor_tensor(rstd[:, :], mv[:, :, 1], power[:, :], ALU.pow).then_inc(n_rstd, 1)
                for i in range(TT):
                    pool.wait_ge(normed, n * TT + i + 1)
                    nc.gpsimd.tensor_tensor(buf[:, i, :], buf[:, i, :], g, ALU.mult).then_inc(gained, 1)
                    pool.wait_ge(gained, n * TT + i + 1)
                    nc.gpsimd.tensor_tensor(buf[:, i, :], buf[:, i, :], o, ALU.add).then_inc(affine_done, 1)

            def tail(b):
                norm(xres, 2 * b, gain[:, :], offset[:, :])
                pool.wait_ge(ada_in, b * 16 + 16)
                norm(xres, 2 * b + 1, ada_row[:, 0, :], ada_row[:, 1, :])

            def body(b, first, last):
                if l0 and not first:
                    tail(b - 1)
                pool.wait_ge(xres_in, b * 16 + 16)
                if l0:
                    pool.wait_ge(row_set, b + 1)
                for i in range(TT):
                    nc.gpsimd.tensor_tensor(xres[:, i, :], xres[:, i, :], (row if l0 else b2r)[:, :], ALU.add)\
                        .then_inc(row_added, 1)
                if not l0 and not last:
                    norm(xin, b + 1, gain[:, :], offset[:, :])

            if not l0:
                norm(xin, 0, gain[:, :], offset[:, :])
            each_batch(pool, body)
            if l0:
                tail(B - 1)

        @block.scalar
        def _(act):
            for c, (_, hi, _) in enumerate(chunks):
                act.wait_ge(w_in[c % 2], 16 * (c // 2 + 1))
                nc.scalar.activation(hi, passing[c % 2][:, :, :], ACT.Copy).then_inc(w_hi, 1)

            def norm(buf, n):
                act.wait_ge(n_shift, n + 1)
                for i in range(TT):
                    nc.scalar.activation(buf[:, i, :], buf[:, i, :], ACT.Identity, bias=shift[:, i:i + 1],
                                         scale=rstd[:, i:i + 1]).then_inc(normed, 1)

            def turn_out(b):
                for k in range(KT):
                    act.wait_ge(turned, b * KT + k + 1)
                    nc.scalar.activation(xth[:, k, :], turn[k % 2][:, :], ACT.Copy).then_inc(xt_hi, 1)

            def body(b, first, last):
                if l0:
                    act.wait_ge(p_mm, b + 1)
                    nc.scalar.activation(pt[:, :], misc[0][0:2 * WIRES, :], ACT.Copy).then_inc(pt_out, 1)
                for m in range(FT):
                    act.wait_ge(h_mm, b * FT + m + 1)
                    if not (first and m < 2):
                        act.wait_ge(h_lo, b * FT + m - 1)
                    nc.scalar.activation(hid[m % 2][:, :], turn[m % 2][:, :], func, bias=b1c[:, m:m + 1]).then_inc(h_act, 1)
                    if l0 and not first and m == 3:
                        norm(xres, 2 * b - 2)
                    if l0 and not first and m == 7:
                        norm(xres, 2 * b - 1)
                    if l0 and m == 5:
                        act.wait_ge(p_out, b + 1)
                        nc.scalar.activation(angle[:, :, :], angle[:, :, :], ACT.Sigmoid).then_inc(p_sig, 1)
                    if l0 and m == 6:
                        act.wait_ge(halved, b + 1)
                        nc.scalar.activation(cos_sin[:, :, :, :], cos_sin[:, :, :, :], ACT.Sin).then_inc(cs_out, 1)
                    if l0 and m == 10:
                        act.wait_ge(amp_turned, b + 1)
                        nc.scalar.activation(ampt[:, :], misc[0][0:DIM, :], ACT.Copy).then_inc(ampt_out, 1)
                    if l0 and m == 11:
                        act.wait_ge(state_mm, b + 1)
                        nc.scalar.activation(prob[:, :], misc[1][0:2 * DIM, :], ACT.Square).then_inc(prob_out, 1)
                    if not l0 and not last and m == 6:
                        norm(xin, b + 1)
                if not last:
                    turn_out(b + 1)

            if not l0:
                norm(xin, 0)
            turn_out(0)
            each_batch(act, body)
            if l0:
                norm(xres, 2 * B - 2)
                norm(xres, 2 * B - 1)

        @block.vector
        def _(dve):
            link = Chain(dve, dve_chain)
            for c, (_, hi, lo) in enumerate(chunks):
                dve.wait_ge(w_hi, c + 1)
                nc.vector.tensor_tensor(lo, passing[c % 2][:, :, :], hi.bitcast(F32), ALU.subtract).then_inc(w_lo, 1)
            dve.wait_ge(consts_in, 16 * len(consts))
            if l0:
                link(nc.vector.memset(pd_zero[:, :, :], 0.0))
                link(nc.vector.tensor_copy(pd[:, :, :], pd_zero[:, :, :]))
                link(nc.vector.tensor_copy(pd[:, :, 0:WIRES], pdw[:, :, :]))
                nc.vector.tensor_tensor(pd[:, :, WIRES:2 * WIRES], pdw[:, :, :], pd[:, :, 0:WIRES].bitcast(F32),
                                        ALU.subtract).then_inc(pd_set, 1)
            ahead = link.n

            def norm_stats(buf, n):
                for i in range(TT):
                    link.step(nc.vector.bn_stats(stat[:, i, :], buf[:, i, :]))
                wait_apart(dve, passed_dve, (dve_chain, link.base + link.n))
                for i in range(TT):
                    link.step(nc.vector.bn_aggr(mv[:, i, :], stat[:, i, :]))
                link.wait()
                nc.vector.tensor_scalar(mv[:, :, 1], mv[:, :, 1], EPS, None, ALU.add).then_inc(n_var, 1)

            def norm_shift(n):
                dve.wait_ge(n_rstd, n + 1)
                nc.vector.scalar_tensor_tensor(shift[:, :], mv[:, :, 0], -1.0, rstd[:, :], ALU.mult, ALU.mult)\
                    .then_inc(n_shift, 1)

            def turn_out(b):
                for k in range(KT):
                    dve.wait_ge(xt_hi, b * KT + k + 1)
                    nc.vector.tensor_tensor(xtl[:, k, :], turn[k % 2][:, :], xth[:, k, :].bitcast(F32), ALU.subtract)\
                        .then_inc(xt_lo, 1)

            def circuit_row(b, first):
                if not first:
                    dve.wait_ge(row_added, b * TT)
                link(nc.vector.tensor_scalar(row[:, :], b2r[:, :], keep.take_f[:, bass.ds(b, 1)], None, ALU.mult))
                nc.vector.scalar_tensor_tensor(row[:, :], pub_row[:, :], keep.q_factor[:, bass.ds(b, 1)], row[:, :],
                                               ALU.mult, ALU.add).then_inc(row_set, 1)

            def circuit_inputs(b):
                dve.wait_ge(p_turned, b + 1)
                halves = misc[1][:, 0:TT * 2 * WIRES].rearrange("p (t a w) -> p t w a", t=TT, a=2)
                link(nc.vector.tensor_reduce(angle[:, :, :], halves, AX.X, ALU.add))
                link(nc.vector.tensor_tensor(angle[:, :, :], angle[:, :, :],
                                             pdb[:, :].unsqueeze(1).to_broadcast([P, TT, WIRES]), ALU.add))
                nc.vector.tensor_scalar(angle[:, :, :], angle[:, :, :], 10.0, -10.0, ALU.min, ALU.max).then_inc(p_out, 1)

            def circuit_angles(b):
                dve.wait_ge(p_sig, b + 1)
                link(nc.vector.tensor_scalar(cos_sin[:, 1, :, :], angle[:, :, :], PI, 0.5, ALU.mult, ALU.mult))
                nc.vector.tensor_scalar(cos_sin[:, 0, :, :], cos_sin[:, 1, :, :], -1.0, PI / 2, ALU.mult, ALU.add)\
                    .then_inc(halved, 1)

            def circuit_amplitudes(b):
                dve.wait_ge(cs_out, b + 1)
                for h in range(2):
                    for i in range(2):
                        one = cos_sin[:, i, :, 2 * h:2 * h + 1].to_broadcast([P, TT, 2])
                        two = cos_sin[:, :, :, 2 * h + 1].rearrange("p c t -> p t c")
                        link(nc.vector.tensor_tensor(pairs[:, h, :, 2 * i:2 * i + 2], one, two, ALU.mult))
                for i in range(4):
                    ins = nc.vector.tensor_tensor(amp[:, :, 4 * i:4 * i + 4],
                                                  pairs[:, 0, :, i:i + 1].to_broadcast([P, TT, 4]),
                                                  pairs[:, 1, :, :], ALU.mult)
                    ins.then_inc(amp_out, 1)

            def circuit_add(b, i):
                dve.wait_ge(up_mm, b * TT + i + 1)
                dve.wait_ge(row_added, b * TT + i + 1)
                nc.vector.scalar_tensor_tensor(xres[:, i, :], misc[i % 2][:, :], keep.q_factor[:, bass.ds(b, 1)],
                                               xres[:, i, :], ALU.mult, ALU.add).then_inc(up_added, 1)

            def body(b, first, last):
                if l0:
                    links = 1 + 2 + 1 + 4 + (0 if first else 4 * TT)
                    link.at(ahead if first else ahead + 8 + (b - 1) * (8 + 4 * TT))
                else:
                    links = 0 if last else 2 * TT
                    link.at(ahead + b * 2 * TT + 2 * TT)
                if l0:
                    circuit_row(b, first)
                for m in range(FT):
                    dve.wait_ge(h_act, b * FT + m + 1)
                    if not (first and m < 2):
                        dve.wait_ge(y_mm, b * FT + m - 1)
                    nc.vector.tensor_copy(hh[m % 2][:, :], hid[m % 2][:, :]).then_inc(h_hi, 1)
                    dve.wait_ge(h_hi, b * FT + m + 1)
                    nc.vector.tensor_tensor(hl[m % 2][:, :], hid[m % 2][:, :], hh[m % 2][:, :].bitcast(F32), ALU.subtract)\
                        .then_inc(h_lo, 1)
                    if l0 and not first:
                        if m == 0:
                            dve.wait_ge(y_out, b * TT)
                            norm_stats(xres, 2 * b - 2)
                        if m == 2:
                            norm_shift(2 * b - 2)
                        if m == 5:
                            dve.wait_ge(affine_done, b * 2 * TT - TT)
                            norm_stats(xres, 2 * b - 1)
                        if m == 6:
                            norm_shift(2 * b - 1)
                    if l0:
                        if m == 3:
                            circuit_inputs(b)
                        if m == 5:
                            circuit_angles(b)
                        if m == 7:
                            circuit_amplitudes(b)
                        if m >= 12:
                            circuit_add(b, m - 12)
                    if not l0 and not last:
                        if m == 3:
                            dve.wait_ge(x_in, b * 16 + 32)
                            norm_stats(xin, b + 1)
                        if m == 5:
                            norm_shift(b + 1)
                if not last:
                    turn_out(b + 1)
                dve.wait_ge(y_mm, b * FT + FT)
                for i in range(TT):
                    if l0:
                        dve.wait_ge(up_added, b * TT + i + 1)
                        nc.vector.scalar_tensor_tensor(xres[:, i, :], acc[i][:, :], keep.take_f[:, bass.ds(b, 1)],
                                                       xres[:, i, :], ALU.mult, ALU.add).then_inc(y_out, 1)
                    else:
                        dve.wait_ge(row_added, b * TT + i + 1)
                        nc.vector.tensor_tensor(xres[:, i, :], acc[i][:, :], xres[:, i, :], ALU.add).then_inc(y_out, 1)
                assert link.n == links, (link.n, links)

            if not l0:
                dve.wait_ge(x_in, 16)
                norm_stats(xin, 0)
                norm_shift(0)
            turn_out(0)
            each_batch(dve, body)
            if l0:
                link.at(ahead + 8 + (B - 1) * (8 + 4 * TT))
                dve.wait_ge(y_out, B * TT)
                norm_stats(xres, 2 * B - 2)
                norm_shift(2 * B - 2)
                dve.wait_ge(affine_done, 2 * B * TT - TT)
                norm_stats(xres, 2 * B - 1)
                norm_shift(2 * B - 1)

        @block.tensor
        def _(pe):
            def turn_in(b, k, ahead):
                if k == 0:
                    if l0:
                        pe.wait_ge(x_in, b * 16 + 16)
                    else:
                        pe.wait_ge(affine_done, b * TT + TT)
                if ahead and k < 2:
                    pe.wait_ge(h_act, b * FT - 1 + k)
                if k >= 2:
                    pe.wait_ge(xt_lo, b * KT + k - 1)
                for i in range(TT):
                    mm = pe.transpose(turn[k % 2][:, i * P:(i + 1) * P], xin[:, i, k * P:(k + 1) * P], keep.ident[:, :])
                mm.then_inc(turned, 1)

            def up(b, m, first):
                if m >= 2:
                    pe.wait_ge(h_act, b * FT + m - 1)
                cut = slice(m * P, (m + 1) * P)
                split_product(pe, turn[m % 2][:, :], [(w1h[:, k, cut], w1l[:, k, cut], xth[:, k, :], xtl[:, k, :])
                                                      for k in range(KT)]).then_inc(h_mm, 1)

            def down(b, m, first):
                pe.wait_ge(h_lo, b * FT + m + 1)
                if m == 0 and not first:
                    pe.wait_ge(y_out, b * TT)
                for i in range(TT):
                    cut = slice(i * P, (i + 1) * P)
                    pe.matmul(acc[i][:, :], hh[m % 2][:, cut], w2h[:, m, :], start=m == 0, stop=False)
                    pe.matmul(acc[i][:, :], hl[m % 2][:, cut], w2h[:, m, :], start=False, stop=False)
                    mm = pe.matmul(acc[i][:, :], hh[m % 2][:, cut], w2l[:, m, :], start=False, stop=m == FT - 1)
                mm.then_inc(y_mm, 1)

            def circuit(b, m, first):
                if m == 2:
                    if not first:
                        pe.wait_ge(up_added, b * TT)
                    wait_apart(pe, passed_pe, (pt_out, b + 1))
                    for i in range(TT):
                        mm = pe.transpose(misc[1][:, i * 2 * WIRES:(i + 1) * 2 * WIRES], pt[:, i * P:(i + 1) * P],
                                          keep.ident[0:2 * WIRES, 0:2 * WIRES])
                    mm.then_inc(p_turned, 1)
                if m == 9:
                    pe.wait_ge(amp_out, b * 4 + 4)
                    for i in range(TT):
                        mm = pe.transpose(misc[0][0:DIM, i * P:(i + 1) * P], amp[:, i, :], keep.ident[:, :])
                    mm.then_inc(amp_turned, 1)
                if m == 11:
                    wait_apart(pe, passed_pe, (ampt_out, b + 1))
                    pe.matmul(misc[1][0:2 * DIM, :], keep.circuit[:, :], ampt[:, :], start=True, stop=True)\
                        .then_inc(state_mm, 1)
                if m >= 12:
                    i = m - 12
                    if i == 0:
                        pe.wait_ge(prob_out, b + 1)
                    if i >= 2:
                        pe.wait_ge(up_added, b * TT + i - 1)
                    pe.matmul(misc[i % 2][:, :], prob[:, i * P:(i + 1) * P], keep.zpu[:, :], start=True, stop=True)\
                        .then_inc(up_mm, 1)

            def body(b, first, last):
                pe.wait_ge(xt_lo, b * KT + KT)
                if l0:
                    if first:
                        pe.wait_ge(pd_set, 1)
                    else:
                        pe.wait_ge(up_added, b * TT)
                    for k in range(KT):
                        pe.matmul(misc[0][:, :], pd[:, k, :], xth[:, k, :], start=k == 0, stop=False)
                        mm = pe.matmul(misc[0][:, :], pd[:, k, :], xtl[:, k, :], start=False, stop=k == KT - 1)
                    mm.then_inc(p_mm, 1)
                for m in range(FT):
                    up(b, m, first)
                    if m >= 2:
                        down(b, m - 2, first)
                    if l0:
                        circuit(b, m, first)
                for half in range(2):
                    if not last:
                        turn_in(b + 1, 2 * half, True)
                        turn_in(b + 1, 2 * half + 1, True)
                    down(b, FT - 2 + half, first)

            pe.wait_ge(w_lo, CH)
            for k in range(KT):
                turn_in(0, k, False)
            each_batch(pe, body)


def attention_stage(nc, keep, t, scratch):
    UNITS = H * TT
    SLOTS = 8
    ITEMS = 6 * TT
    IT_Q, IT_K, IT_V, IT_C, IT_O = (TT * i for i in range(1, 6))
    VB = TT * H
    ORDER = [4 * (pair // 4 * 2 + i) + pair % 4 for pair in range(H // 2) for i in range(2)]
    PAIR = 2 * TT
    with ExitStack() as ctx:
        sb = lambda n, s, d=F32: ctx.enter_context(nc.sbuf_tensor(f"at_{n}", s, d))
        ps = lambda n: ctx.enter_context(nc.psum_tensor(f"at_{n}", [P, 512], F32))
        sem = lambda n: ctx.enter_context(nc.semaphore(f"at_{n}"))
        weight = {n: (sb(f"w{n}h", [P, KT, D], F32R), sb(f"w{n}l", [P, KT, D], F32R)) for n in "qkvo"}
        xin = sb("xin", [P, TT, D])
        qk = sb("qk", [P, 4, KT, S])
        QH, KH, QL, KL = range(4)
        xres = qk[:, KL, :, :]
        flat = [sb(f"flat{i}", [P, S]) for i in range(2)]
        stack = [sb(f"stack{i}", [P, 2, 2, S], F32R) for i in range(2)]
        v = sb("v", [P, VB + 1, 2 * HD], F32R)
        v_tiles = v[:, 0:VB, :].rearrange("p (t h) c -> p t h c", t=TT)
        bias = sb("bias", [P, SLOTS, S])
        pt_hi = [sb(f"pt_hi{i}", [P, KT, S], F32R) for i in range(2)]
        pt_lo = [sb(f"pt_lo{i}", [P, KT, S], F32R) for i in range(2)]
        xth, xtl = pt_hi[1], pt_lo[1]
        ctx_flat = sb("ctx_flat", [P, S])
        head_sum = sb("head_sum", [P, TT, HD])
        inv_sum = sb("inv_sum", [P, TT])
        mask8 = sb("mask8", [P, TT, S], U8)
        mask = sb("mask", [P, TT, S], BF16)
        neg_top = sb("neg_top", [P, SLOTS])
        bqc, bkc = sb("bqc", [P, KT]), sb("bkc", [P, KT])
        bvr, bor = sb("bvr", [P, D]), sb("bor", [P, D])
        zeros = sb("zeros", [P, 2 * HD])
        row_sum = sb("row_sum", [P, 4 * TT])
        score = [ps(f"score{i}") for i in range(4)]
        turn = [ps(f"turn{i}") for i in range(2)]
        head_ps, head_turn = ps("head"), ps("head_turn")

        consts_in, w_hi, w_lo, ones_set = map(sem, ("consts_in", "w_hi", "w_lo", "ones_set"))
        w_in = [sem(f"w_in{i}") for i in range(2)]
        x_in, xres_in, stored, mask_in, mask_set = map(sem, ("x_in", "xres_in", "stored", "mask_in", "mask_set"))
        item_mm, item_flat, item_hi, item_out, res_ready = map(sem, ("item_mm", "item_flat", "item_hi", "item_out", "res_ready"))
        bias_in = [sem(f"bias_in{i}") for i in range(SLOTS // 2)]
        stack_in = [sem(f"stack_in{i}") for i in range(2)]
        masked, score_mm, scored, exped, turned, p_hi, p_lo = map(sem, (
            "masked", "score_mm", "scored", "exped", "turned", "p_hi", "p_lo"))
        head_mm, head_flat, head_turned, head_out, dve_chain = map(sem, (
            "head_mm", "head_flat", "head_turned", "head_out", "dve_chain"))
        passed_dve, passed_sp = sem("passed_dve"), sem("passed_sp")
        consts = [(bqc[:, :], t["L1_cond_bq"].rearrange("(m p) -> p m", p=P)),
                  (bkc[:, :], t["L1_cond_bk"].rearrange("(m p) -> p m", p=P)),
                  (bvr[:, :], t["L1_cond_bv"].partition_broadcast(P)), (bor[:, :], t["L1_cond_bo"].partition_broadcast(P))]
        passing = [bias[:, 0:TT, :], bias[:, TT:SLOTS, :]]
        chunks = [(t[f"L1_cond_W{n}"].rearrange("(k p) n -> p k n", p=P), *weight[n]) for n in "qkvo"]
        bias_src = t["fside_Bx16xSxS_0"]
        block = ctx.enter_context(nc.Block())

        @block.sync
        def _(sp):
            for dst, src in consts:
                sp.dma_start(dst, src).then_inc(consts_in, 16)
            sp.dma_start(xin[:, :, :], rows(scratch["x1"][0])).then_inc(x_in, 16)
            sp.dma_start(mask8[:, :, :], rows(t["mask_Bx1xSxS_bk0"][0, 0])).then_inc(mask_in, 16)
            for c, (src, _, _) in enumerate(chunks):
                if c >= 2:
                    sp.wait_ge(w_lo, c - 1)
                sp.dma_start(passing[c % 2], src).then_inc(w_in[c % 2], 16)

            def load_bias(b, two, first):
                if two >= SLOTS // 2 or not first:
                    sp.wait_ge(turned, b * UNITS + 2 * two + 2 - SLOTS)
                elif two % 2 == 0:
                    sp.wait_ge(w_lo, 3 + two // 2)
                h, u = divmod(2 * two, TT)
                slot = 2 * two % SLOTS
                sp.dma_start(bias[:, slot:slot + 2, :],
                             bias_src[b, ORDER[h], u * P:(u + 2) * P, :].rearrange("(t p) n -> p t n", p=P))\
                    .then_inc(bias_in[two % (SLOTS // 2)], 16)

            def load_stack(b, pair):
                if pair == 0:
                    sp.wait_ge(item_out, b * ITEMS + IT_V)
                if pair >= 2:
                    sp.wait_ge(score_mm, b * UNITS + (pair - 1) * PAIR)
                j, k = ORDER[2 * pair] % 4, ORDER[2 * pair] // 4
                src, to = slice(j * HD, (j + 1) * HD), stack[pair % 2][:, :, :, :].bitcast(F32)
                two = slice(k, k + 2)
                for block, dst, part in ((0, slice(0, 2), slice(QH, KH + 1)), (1, slice(0, 2), slice(QH, KL + 1, KL - QH)),
                                         (2, slice(0, 1), slice(QL, QL + 1)), (2, slice(1, 2), slice(KH, KH + 1)),
                                         (3, slice(0, 2), slice(QL, KL + 1))):
                    sp.dma_start(to[block * HD:(block + 1) * HD, dst, :, :], qk[src, part, two, :])\
                        .then_inc(stack_in[pair % 2], 16)

            def body(b, first, last):
                for two in range(SLOTS // 2):
                    load_bias(b, two, first)
                load_stack(b, 0)
                load_stack(b, 1)
                for two in range(SLOTS // 2, UNITS // 2):
                    load_bias(b, two, first)
                    if two % 4 == 2 and two // 4 + 1 < H // 2:
                        load_stack(b, two // 4 + 1)
                if not last:
                    wait_apart(sp, passed_sp, (mask_set, b + 1))
                    sp.dma_start(mask8[:, :, :], rows(t["mask_Bx1xSxS_bk0"][b + 1, 0])).then_inc(mask_in, 16)
                sp.wait_ge(score_mm, b * UNITS + UNITS)
                sp.dma_start(xres, rows(scratch["x1"][b])).then_inc(xres_in, 16)
                if not last:
                    wait_apart(sp, passed_sp, (item_mm, b * ITEMS + IT_O))
                    sp.dma_start(xin[:, :, :], rows(scratch["x1"][b + 1])).then_inc(x_in, 16)
                sp.wait_ge(item_out, b * ITEMS + ITEMS)
                sp.dma_start(rows(scratch["x2"][b]), xres).then_inc(stored, 16)

            each_batch(sp, body)
            sp.wait_ge(stored, 16 * B)

        @block.gpsimd
        def _(pool):
            pool.wait_ge(consts_in, 16 * len(consts))

            def body(b, first, last):
                pool.wait_ge(mask_set, b + 1)
                for n in range(UNITS):
                    if n % 2 == 0:
                        pair = n // 2
                        pool.wait_ge(bias_in[pair % 4], b * (UNITS // SLOTS * 16) + 16 * (pair // 4 + 1))
                    tile = bias[:, n % SLOTS, :]
                    nc.gpsimd.tensor_tensor(tile, tile, mask[:, n % TT, :], ALU.add).then_inc(masked, 1)
                pool.wait_ge(xres_in, b * 16 + 16)
                for i in range(TT):
                    nc.gpsimd.tensor_tensor(xres[:, i, :], xres[:, i, :], bor[:, :], ALU.add).then_inc(res_ready, 1)

            each_batch(pool, body)

        @block.scalar
        def _(act):
            def split_weights(c):
                act.wait_ge(w_in[c % 2], 16 * (c // 2 + 1))
                nc.scalar.activation(chunks[c][1][:, :, :], passing[c % 2], ACT.Copy).then_inc(w_hi, 1)

            split_weights(0)
            split_weights(1)

            def body(b, first, last):
                def item(i):
                    if first and i in (IT_Q, IT_K):
                        split_weights(i // TT + 1)
                    """The hi part of item i, from PSUM (transposes) or behind its bias (q, k, v)."""
                    k = i % TT
                    if i < IT_Q or i >= IT_C:
                        act.wait_ge(item_mm, b * ITEMS + i + 1)
                        nc.scalar.activation(xth[:, k, :], score[k][:, :], ACT.Copy).then_inc(item_hi, 1)
                    else:
                        act.wait_ge(item_flat, b * 3 * TT + i - IT_Q + 1)
                        if i < IT_V:
                            if not first:
                                act.wait_ge(stored, b * 16)
                            dst, src = qk[:, QH if i < IT_K else KH, k, :].bitcast(F32R), flat[k % 2][:, :]
                        else:
                            dst = v_tiles[:, k, :, 0:HD]
                            src = flat[k % 2][:, :].rearrange("p (h d) -> p h d", h=H)
                        nc.scalar.activation(dst, src, ACT.Copy).then_inc(item_hi, 1)

                def exp(n):
                    act.wait_ge(scored, b * UNITS + n + 1)
                    tile = bias[:, n % SLOTS, :]
                    nc.scalar.activation(tile, tile, ACT.Exp, bias=neg_top[:, n % SLOTS:n % SLOTS + 1], scale=-1.0,
                                         accum_out=row_sum[:, n % (4 * TT):n % (4 * TT) + 1])\
                        .then_inc(exped, 1)

                def hi(n):
                    h, u = divmod(n, TT)
                    act.wait_ge(turned, b * UNITS + n + 1)
                    if h >= 2 and u == 0:
                        act.wait_ge(head_mm, b * H + h - 1)
                    nc.scalar.activation(pt_hi[h % 2][:, :, u * P:(u + 1) * P],
                                         turn[n % 2][:, :].rearrange("p (k q) -> p k q", k=KT), ACT.Copy).then_inc(p_hi, 1)

                def head(h):
                    act.wait_ge(head_mm, b * H + h + 1)
                    if h >= 1:
                        act.wait_ge(head_turned, b * H + h)
                    nc.scalar.activation(ctx_flat[:, :], head_ps[:, :], ACT.Copy).then_inc(head_flat, 1)

                for i in range(IT_C):
                    item(i)
                for n in range(UNITS + 8):
                    if n < UNITS:
                        exp(n)
                    if 1 <= n <= UNITS:
                        hi(n - 1)
                    if n >= 7 and (n - 7) % TT == 0 and (n - 7) // TT < H:
                        head((n - 7) // TT)
                for i in range(IT_C, IT_O):
                    item(i)

            each_batch(act, body)

        @block.vector
        def _(dve):
            link = Chain(dve, dve_chain)
            dve.wait_ge(consts_in, 16 * len(consts))
            link(nc.vector.memset(zeros[:, :], 0.0))
            link(nc.vector.tensor_copy(v[:, VB, :], zeros[:, :]))
            ahead = link.n

            def split_weights(c):
                _, hi, lo = chunks[c]
                dve.wait_ge(w_hi, c + 1)
                nc.vector.tensor_tensor(lo[:, :, :], passing[c % 2], hi[:, :, :].bitcast(F32), ALU.subtract).then_inc(w_lo, 1)

            split_weights(0)
            split_weights(1)

            def body(b, first, last):
                link.at(ahead + b * 2 * H)

                def item(i):
                    k = i % TT
                    if first and i in (IT_Q, IT_K):
                        split_weights(i // TT + 1)
                    if i < IT_Q or IT_C <= i < IT_O:
                        dve.wait_ge(item_hi, b * 5 * TT + i + 1)
                        nc.vector.tensor_tensor(xtl[:, k, :], score[k][:, :], xth[:, k, :].bitcast(F32), ALU.subtract)\
                            .then_inc(item_out, 1)
                        return
                    dve.wait_ge(item_mm, b * ITEMS + i + 1)
                    if i >= IT_O:
                        dve.wait_ge(res_ready, b * TT + k + 1)
                        nc.vector.tensor_tensor(xres[:, k, :], score[k][:, :], xres[:, k, :], ALU.add).then_inc(item_out, 1)
                        return
                    tile = flat[k % 2][:, :]
                    if i < IT_K:
                        ins = nc.vector.tensor_scalar(tile, score[k][:, :], bqc[:, k:k + 1], Q_SCALE, ALU.add, ALU.mult)
                    elif i < IT_V:
                        ins = nc.vector.tensor_scalar(tile, score[k][:, :], bkc[:, k:k + 1], None, ALU.add)
                    else:
                        ins = nc.vector.tensor_tensor(tile, score[k][:, :], bvr[:, :], ALU.add)
                    ins.then_inc(item_flat, 1)
                    dve.wait_ge(item_hi, b * 5 * TT + i + 1)
                    if i < IT_V:
                        hi, lo = (QH, QL) if i < IT_K else (KH, KL)
                        hi, lo = qk[:, hi, k, :], qk[:, lo, k, :].bitcast(F32R)
                    else:
                        hi, lo = v_tiles[:, k, :, 0:HD].bitcast(F32), v_tiles[:, k, :, HD:2 * HD]
                        tile = tile.rearrange("p (h d) -> p h d", h=H)
                    nc.vector.tensor_tensor(lo, tile, hi, ALU.subtract).then_inc(item_out, 1)

                def scores(n):
                    slot = n % SLOTS
                    wait_apart(dve, passed_dve, (masked, b * UNITS + n + 1), (score_mm, b * UNITS + n + 1))
                    nc.vector.tensor_tensor_reduce(bias[:, slot, :], score[n % 4][:, :], bias[:, slot, :], -1.0, -MASKED,
                                                   ALU.add, ALU.min, neg_top[:, slot:slot + 1]).then_inc(scored, 1)

                def lo(n):
                    h, u = divmod(n, TT)
                    dve.wait_ge(p_hi, b * UNITS + n + 1)
                    cut = slice(u * P, (u + 1) * P)
                    nc.vector.tensor_tensor(pt_lo[h % 2][:, :, cut], turn[n % 2][:, :].rearrange("p (k q) -> p k q", k=KT),
                                            pt_hi[h % 2][:, :, cut].bitcast(F32), ALU.subtract).then_inc(p_lo, 1)

                def head(h):
                    dve.wait_ge(head_turned, b * H + h + 1)
                    tiles = head_turn[:, :].rearrange("p (t c) -> p t c", t=TT)[:, :, 0:2 * HD]
                    parts = tiles.rearrange("p t (a d) -> p t d a", a=2)
                    link.step(nc.vector.reciprocal(inv_sum[:, :], row_sum[:, h % 4 * TT:(h % 4 + 1) * TT]))
                    link(nc.vector.tensor_reduce(head_sum[:, :, :], parts, AX.X, ALU.add))
                    nc.vector.tensor_tensor(xin[:, :, ORDER[h] * HD:(ORDER[h] + 1) * HD], head_sum[:, :, :],
                                            inv_sum[:, :].unsqueeze(2).to_broadcast([P, TT, HD]), ALU.mult).then_inc(head_out, 1)

                dve.wait_ge(mask_in, b * 16 + 16)
                if not first:
                    dve.wait_ge(masked, b * UNITS)
                nc.vector.tensor_scalar(mask[:, :, :], mask8[:, :, :], MASKED, None, ALU.mult).then_inc(mask_set, 1)
                for i in range(IT_C):
                    item(i)
                for n in range(UNITS + 10):
                    if n < UNITS:
                        scores(n)
                    if 2 <= n <= UNITS + 1:
                        lo(n - 2)
                    if n >= 9 and (n - 9) % TT == 0 and (n - 9) // TT < H:
                        head((n - 9) // TT)
                for i in range(IT_C, ITEMS):
                    item(i)

            each_batch(dve, body)

        @block.tensor
        def _(pe):
            def body(b, first, last):
                def item(i):
                    k = i % TT
                    bank = score[k]
                    if i == 0:
                        pe.wait_ge(x_in, b * 16 + 16)
                        if not first:
                            pe.wait_ge(item_out, b * ITEMS)
                    elif i == IT_C:
                        pe.wait_ge(head_out, b * H + H)
                    elif i in (IT_Q, IT_O):
                        pe.wait_ge(item_out, b * ITEMS + i)
                    elif i >= TT:
                        pe.wait_ge(item_out, b * ITEMS + i - TT + 1)
                    if first and k == 0 and IT_Q <= i < IT_C or i == IT_O:
                        pe.wait_ge(w_lo, TT if i == IT_O else i // TT)
                    if i < IT_Q or IT_C <= i < IT_O:
                        for j in range(TT):
                            mm = pe.transpose(bank[:, j * P:(j + 1) * P], xin[:, j, k * P:(k + 1) * P], keep.ident[:, :])
                    elif i < IT_V:
                        wh, wl = weight["q" if i < IT_K else "k"]
                        cut = slice(k * P, (k + 1) * P)
                        mm = split_product(pe, bank[:, :], [(wh[:, j, cut], wl[:, j, cut], xth[:, j, :], xtl[:, j, :])
                                                            for j in range(KT)])
                    else:
                        wh, wl = weight["v" if i < IT_C else "o"]
                        cut = slice(k * P, (k + 1) * P)
                        mm = split_product(pe, bank[:, :], [(xth[:, j, cut], xtl[:, j, cut], wh[:, j, :], wl[:, j, :])
                                                            for j in range(KT)])
                    mm.then_inc(item_mm, 1)

                def scores(n):
                    h, u = divmod(n, TT)
                    pair = h // 2
                    if n % PAIR == 0:
                        pe.wait_ge(stack_in[pair % 2], b * (H // 4 * 5 * 16) + (pair // 2 + 1) * 5 * 16)
                    if n >= 4:
                        pe.wait_ge(scored, b * UNITS + n - 3)
                    pe.matmul(score[n % 4][:, :], stack[pair % 2][:, 0, h % 2, u * P:(u + 1) * P], stack[pair % 2][:, 1, h % 2, :],
                              start=True, stop=True).then_inc(score_mm, 1)

                def turn_unit(n):
                    pe.wait_ge(exped, b * UNITS + n + 1)
                    if n >= 2:
                        pe.wait_ge(p_lo, b * UNITS + n - 1)
                    for k in range(KT):
                        mm = pe.transpose(turn[n % 2][:, k * P:(k + 1) * P], bias[:, n % SLOTS, k * P:(k + 1) * P],
                                          keep.ident[:, :])
                    mm.then_inc(turned, 1)

                def head(h):
                    pe.wait_ge(p_lo, b * UNITS + (h + 1) * TT)
                    if h >= 1:
                        pe.wait_ge(head_flat, b * H + h)
                    for k in range(KT):
                        block = k * H + ORDER[h]
                        vk = v[:, block:block + 2, :].rearrange("p a c -> p (a c)")
                        pe.matmul(head_ps[:, :], vk, pt_hi[h % 2][:, k, :], start=k == 0, stop=False)
                        mm = pe.matmul(head_ps[:, :], vk, pt_lo[h % 2][:, k, :], start=False, stop=k == KT - 1)
                    mm.then_inc(head_mm, 1)

                def turn_head(h):
                    pe.wait_ge(head_flat, b * H + h + 1)
                    if h >= 1:
                        pe.wait_ge(head_out, b * H + h)
                    for i in range(TT):
                        mm = pe.transpose(head_turn[:, i * P:(i + 1) * P], ctx_flat[:, i * P:(i + 1) * P], keep.ident[:, :])
                    mm.then_inc(head_turned, 1)

                for i in range(IT_C):
                    item(i)
                pe.wait_ge(item_out, b * ITEMS + IT_C)
                for n in range(3):
                    scores(n)
                for n in range(UNITS + 8):
                    if n + 3 < UNITS:
                        scores(n + 3)
                    if n < UNITS:
                        turn_unit(n)
                    if n >= 5 and (n - 5) % TT == 0 and (n - 5) // TT < H:
                        head((n - 5) // TT)
                    if n >= 7 and (n - 7) % TT == 0 and (n - 7) // TT < H:
                        turn_head((n - 7) // TT)
                for i in range(IT_C, ITEMS):
                    item(i)

            each_batch(pe, body)


class Keep:

    def __init__(self, nc, ctx):
        sb = lambda n, s: ctx.enter_context(nc.sbuf_tensor(n, s, F32))
        self.ident = sb("ident", [P, P])
        self.circuit = sb("circuit", [DIM, 2 * DIM])
        self.zpu = sb("zpu", [2 * DIM, D])
        self.take_q = sb("take_q", [P, B])
        self.take_f = sb("take_f", [P, B])
        self.q_factor = sb("q_factor", [P, B])


def build(nc, t, consts, out):
    scratch = {"x1": nc.dram_tensor("x1_scratch", (B, S, D), F32, kind="Internal").ap(),
               "x2": nc.dram_tensor("x2_scratch", (B, S, D), F32, kind="Internal").ap(),
               "ada": nc.dram_tensor("ada_scratch", (B, 2 * D), F32, kind="Internal").ap()}
    with ExitStack() as ctx, nc.allow_non_contiguous_dma(reason="small bias vectors as columns"):
        keep = Keep(nc, ctx)
        setup_stage(nc, keep, t, consts, scratch)
        ffn_stage(nc, keep, t, scratch, True, scratch["x1"])
        attention_stage(nc, keep, t, scratch)
        ffn_stage(nc, keep, t, scratch, False, out)


def circuit_constants():
    bit = lambda i, w: i >> (WIRES - 1 - w) & 1

    def permuted(l):
        to = []
        for i in range(DIM):
            v = [bit(i, w) for w in range(WIRES)]
            for c in range(WIRES):
                if v[c]:
                    v[(c + l + 1) % WIRES] ^= 1
            to.append(sum(x << (WIRES - 1 - w) for w, x in enumerate(v)))
        return to

    to1, to2 = permuted(0), permuted(1)
    from1 = [to1.index(k) for k in range(DIM)]
    entry = {(0, 0): np.pi / 2, (0, 1): np.pi, (1, 0): 0.0, (1, 1): np.pi / 2}
    voff = np.zeros((DIM, LAYERS * WIRES * DIM + 4), np.float64)
    vcoef = np.zeros((DIM, 2, LAYERS * WIRES * 3), np.float64)
    for k in range(DIM):
        for w in range(WIRES):
            for i in range(DIM):
                voff[k, w * DIM + i] = entry[bit(from1[k], w), bit(i, w)]
                voff[k, (WIRES + w) * DIM + i] = entry[bit(i, w), bit(k, w)]
            vcoef[k, 0, w * 3 + 2] = 0.5 if bit(from1[k], w) else -0.5
            vcoef[k, 0, (WIRES + w) * 3] = 0.5 if bit(k, w) else -0.5
            vcoef[k, 1, w * 3] = 0.5 if bit(k, w) else -0.5
        n = LAYERS * WIRES * DIM
        ones = bin(k).count("1")
        voff[k, n:] = [0.0, np.pi / 2, -np.pi / 2 * ones, np.pi / 2 - np.pi / 2 * ones]
    sign = np.array([[1.0 - 2.0 * bit(to2[j], w) for j in range(DIM)] for w in range(WIRES)])
    return voff, vcoef, np.concatenate([sign, sign], axis=1)


def constants():
    voff, vcoef, zsign = circuit_constants()
    half = D // 2
    freqs = np.exp(np.arange(half) * (-np.log(10000.0) / (half - 1)))
    c = {"ident": np.eye(P), "freqs": freqs.reshape(2, P).T, "voff": voff, "vcoef": vcoef, "zsign": zsign}
    return {k: np.ascontiguousarray(v, dtype=np.float32) for k, v in c.items()}


_INS = ["x", "condB_vol", "itok_B_34_63", "fside_Bx16xSxS_0", "mask_Bx1xSxS_bk0"] + [
    f"L0_cond_{n}" for n in ("w1", "b1", "w2", "b2", "pd_w", "pd_b", "vqc_w", "pu_w", "pu_b", "q_scale", "ln_g", "ln_b")] + [
    f"L1_cond_{n}" for n in ("W_ada", "b_ada", "Wq", "bq", "Wk", "bk", "Wv", "bv", "Wo", "bo", "W1", "b1", "W2", "b2",
                             "g2", "beta2")]


def kernel(**inputs):
    import concourse.bacc as _bacc
    from concourse.bass_utils import run_bass_kernel_spmd as _run

    nc = _bacc.Bacc("TRN2", target_bir_lowering=False, num_devices=1)
    arrays, t, consts = {}, {}, {}
    for name in _INS:
        a = np.ascontiguousarray(inputs[name])
        arrays[f"in_{name}"] = a
        t[name] = nc.dram_tensor(f"in_{name}", a.shape, mybir.dt.from_np(a.dtype), kind="ExternalInput").ap()
    for name, a in constants().items():
        arrays[f"const_{name}"] = a
        consts[name] = nc.dram_tensor(f"const_{name}", a.shape, mybir.dt.from_np(a.dtype), kind="ExternalInput").ap()
    out = nc.dram_tensor("out", (B, S, D), F32, kind="ExternalOutput").ap()
    build(nc, t, consts, out)
    r = _run(nc, [arrays], core_ids=[0])
    return r.results[0]["out"]
```

```python
from contextlib import ExitStack

import numpy as np

import concourse.bass as bass
from concourse import mybir

F32 = mybir.dt.float32
F32R = mybir.dt.float32r
BF16 = mybir.dt.bfloat16
U8 = mybir.dt.uint8
I32 = mybir.dt.int32
ALU = mybir.AluOpType
ACT = mybir.ActivationFunctionType
AX = mybir.AxisListType

P = 128
B, S, D, F, H = 8, 512, 512, 2048, 16
HD = D // H
KT = D // P
TT = S // P
FT = F // P
WIRES, LAYERS = 4, 2
DIM = 2 ** WIRES
EPS = 1e-5
PI = float(np.pi)
INV_2PI = float(1 / (2 * np.pi))
ROUND = 1.5 * 2.0 ** 23
C1 = 6.28125
C2 = float(np.floor((2 * np.pi - C1) * 2 ** 20) / 2 ** 20)
C3 = float(2 * np.pi - C1 - C2)
PI_BELOW = 3.1415925
MASKED = -3e38
Q_SCALE = float(HD) ** -0.5

DENSE = ["w1", "b1", "w2", "b2"]


def each_batch(eng, body):
    body(0, True, False)
    with eng.Fori(1, B - 1) as b:
        body(b, False, False)
    body(B - 1, False, True)


def rows(t):
    return t.rearrange("(t p) n -> p t n", p=P)


def wait_apart(eng, passed, *waits):
    for sem, value in waits:
        eng.wait_ge(sem, value)
    eng.sem_inc(passed, 1)


class Chain:

    def __init__(self, eng, sem):
        self.eng, self.sem, self.base, self.n = eng, sem, 0, 0

    def at(self, base):
        self.base, self.n = base, 0

    def step(self, ins):
        self.n += 1
        ins.then_inc(self.sem, 1)

    def wait(self):
        self.eng.wait_ge(self.sem, self.base + self.n)

    def __call__(self, ins):
        self.step(ins)
        self.wait()


def setup_stage(nc, keep, t, C, scratch):
    with ExitStack() as ctx:
        sb = lambda n, s, d=F32: ctx.enter_context(nc.sbuf_tensor(n, s, d))
        ps = lambda n: ctx.enter_context(nc.psum_tensor(n, [P, 512], F32))
        sem = lambda n: ctx.enter_context(nc.semaphore(n))
        NE = 2 * KT // 2 * B
        NV = LAYERS * WIRES * DIM + 4
        steps_i = sb("steps_i", [P, B], I32)
        steps = sb("steps", [P, B])
        freq = sb("freq", [P, 2])
        ang, off, turns, sine = (sb(f"emb_{n}", [P, KT, B]) for n in ("ang", "off", "turns", "sine"))
        sig = sb("emb_sig", [P, KT, B])
        wada = sb("wada", [P, KT, 2 * D])
        bada = sb("bada", [B, 2 * D])
        ada = sb("ada", [B, 2 * D])
        vol = sb("vol", [P, B])
        qs = sb("qs", [P, 1])
        vw = sb("vw", [DIM, LAYERS * WIRES * 3])
        vcoef = sb("vcoef", [DIM, 2, LAYERS * WIRES * 3])
        voff = sb("voff", [DIM, NV])
        vprod = sb("vprod", [DIM, 2, LAYERS * WIRES * 3])
        vang, vturn, vsin = (sb(f"v_{n}", [DIM, NV]) for n in ("ang", "turn", "sin"))
        pair = sb("vpair", [DIM, LAYERS, 2, DIM])
        gates = sb("vgates", [DIM, LAYERS, DIM])
        rot2 = sb("vrot2", [DIM, 2, DIM])
        part = sb("vpart", [DIM, 2, DIM])
        zs = sb("zs", [WIRES, 2 * DIM])
        puw = sb("puw", [WIRES, D])
        ps_a, ps_b, ps_v, ps_z = ps("ps_a"), ps("ps_b"), ps("ps_v"), ps("ps_z")
        s_in, s_chain, s_x, s_sin, s_sig, s_silu, s_ada, s_rows, s_out = map(
            sem, ("setup_in", "setup_chain", "angles", "sines", "sigmoids", "silu", "ada_mm", "ada_rows", "ada_out"))
        s_vw, s_vmm, s_z = map(sem, ("v_ready", "v_mm", "z_mm"))
        block = ctx.enter_context(nc.Block())

        @block.sync
        def _(sp):
            loads = [
                (keep.ident[:, :], C["ident"]), (freq[:, :], C["freqs"]), (voff[:, :], C["voff"]),
                (vcoef[:, :, :], C["vcoef"]), (zs[:, :], C["zsign"]),
                (steps_i[:, :], t["itok_B_34_63"].partition_broadcast(P)),
                (vol[:, :], t["condB_vol"].partition_broadcast(P)),
                (qs[:, :], t["L0_cond_q_scale"].partition_broadcast(P)),
                (vw[:, :], t["L0_cond_vqc_w"].rearrange("l w a -> (l w a)").partition_broadcast(DIM)),
                (puw[:, :], t["L0_cond_pu_w"]),
                (wada[:, :, :], t["L1_cond_W_ada"].rearrange("(k p) n -> p k n", p=P)),
                (bada[:, :], t["L1_cond_b_ada"].partition_broadcast(B)),
            ]
            for dst, src in loads:
                sp.dma_start(dst, src).then_inc(s_in, 16)
            sp.wait_ge(s_rows, 2)
            sp.dma_start(scratch["ada"], ada[:, :]).then_inc(s_out, 16)
            sp.wait_ge(s_out, 16)

        all_in = 16 * 12

        @block.vector
        def _(dve):
            link = Chain(dve, s_chain)

            def reduce_angle(ang, off, turns):
                link(nc.vector.tensor_tensor(turns, ang, off, ALU.add))
                link(nc.vector.tensor_scalar(turns, turns, INV_2PI, None, ALU.mult))
                link(nc.vector.tensor_scalar(turns, turns, ROUND, None, ALU.add))
                link(nc.vector.tensor_scalar(turns, turns, ROUND, None, ALU.subtract))
                for c in (C1, C2, C3):
                    link(nc.vector.scalar_tensor_tensor(ang, turns, -c, ang, ALU.mult, ALU.add))
                link(nc.vector.tensor_tensor(ang, ang, off, ALU.add))
                link(nc.vector.tensor_scalar(ang, ang, PI_BELOW, -PI_BELOW, ALU.min, ALU.max))

            dve.wait_ge(s_in, all_in)
            link(nc.vector.tensor_copy(steps[:, :], steps_i[:, :]))
            link(nc.vector.tensor_scalar(steps[:, :], steps[:, :], 4000.0 / 100.0, None, ALU.mult))
            for k in range(KT):
                link(nc.vector.tensor_scalar(ang[:, k, :], steps[:, :], freq[:, k % 2:k % 2 + 1], None, ALU.mult))
            link(nc.vector.memset(off[:, 0:2, :], 0.0))
            link(nc.vector.memset(off[:, 2:4, :], PI / 2))
            reduce_angle(ang[:, :, :], off[:, :, :], turns[:, :, :])
            n = LAYERS * WIRES * DIM
            theta = vw[:, :].rearrange("p (g a) -> p g a", a=3)[:, :, 1:2].to_broadcast([DIM, LAYERS * WIRES, DIM])
            link(nc.vector.tensor_scalar(vang[:, 0:n].rearrange("p (g b) -> p g b", b=DIM), theta, 0.5, None, ALU.mult))
            for c in range(2):
                link(nc.vector.tensor_tensor(vprod[:, c, :], vcoef[:, c, :], vw[:, :], ALU.mult))
            for c in range(2):
                for d in range(2):
                    link(nc.vector.tensor_reduce(vang[:, n + 2 * c + d:n + 2 * c + d + 1], vprod[:, c, :], AX.X, ALU.add))
            reduce_angle(vang[:, :], voff[:, :], vturn[:, :])
            link(nc.vector.tensor_scalar(keep.take_q[:, :], vol[:, :], 0.5, None, ALU.is_gt))
            link(nc.vector.tensor_scalar(keep.take_f[:, :], keep.take_q[:, :], -1.0, 1.0, ALU.mult, ALU.add))
            link(nc.vector.scalar_tensor_tensor(qs[:, :], qs[:, :], -1.0, qs[:, :], ALU.mult, ALU.max))
            nc.vector.tensor_scalar(keep.q_factor[:, :], keep.take_q[:, :], qs[:, 0:1], None, ALU.mult).then_inc(s_x, 1)
            dve.wait_ge(s_sig, 1)
            nc.vector.tensor_tensor(sig[:, :, :], sig[:, :, :], sine[:, :, :], ALU.mult).then_inc(s_silu, 1)
            dve.wait_ge(s_sin, 2)
            g = vsin[:, 0:n].rearrange("p (l u v b) -> p l u v b", l=LAYERS, u=2, v=2)
            for l in range(LAYERS):
                link(nc.vector.tensor_tensor(pair[:, l, :, :], g[:, l, :, 0, :], g[:, l, :, 1, :], ALU.mult))
            link(nc.vector.tensor_tensor(gates[:, :, :], pair[:, :, 0, :], pair[:, :, 1, :], ALU.mult))
            for c in range(2):
                link(nc.vector.tensor_scalar(rot2[:, c, :], gates[:, 1, :], vsin[:, n + 1 - c:n + 2 - c], None, ALU.mult))
            nc.vector.tensor_copy(gates[:, 0, :], gates[:, 0, :]).then_inc(s_vw, 1)
            dve.wait_ge(s_vmm, 1)
            re, im = ps_v[0:DIM, 0:DIM], ps_v[0:DIM, DIM:2 * DIM]
            sin_b, cos_b = vsin[:, n + 2:n + 3], vsin[:, n + 3:n + 4]
            link(nc.vector.tensor_scalar(part[:, 0, :], im, sin_b, None, ALU.mult))
            link(nc.vector.tensor_scalar(part[:, 1, :], im, cos_b, None, ALU.mult))
            link(nc.vector.scalar_tensor_tensor(keep.circuit[:, 0:DIM], re, cos_b, part[:, 0, :], ALU.mult, ALU.subtract))
            link(nc.vector.scalar_tensor_tensor(keep.circuit[:, DIM:], re, sin_b, part[:, 1, :], ALU.mult, ALU.add))
            dve.wait_ge(s_z, 1)
            link(nc.vector.tensor_copy(keep.zpu[:, :], ps_z[0:2 * DIM, :]))
            dve.wait_ge(s_ada, 1)
            scale = slice(0, D)
            link(nc.vector.tensor_tensor(ada[:, scale], ps_a[0:B, :], bada[:, scale], ALU.add))
            nc.vector.tensor_scalar(ada[:, scale], ada[:, scale], 1.0, None, ALU.add).then_inc(s_rows, 1)
            nc.vector.tensor_tensor(ada[:, D:], ps_b[0:B, :], bada[:, D:], ALU.add).then_inc(s_rows, 1)

        @block.scalar
        def _(act):
            act.wait_ge(s_x, 1)
            nc.scalar.activation(sine[:, :, :], ang[:, :, :], ACT.Sin).then_inc(s_sin, 1)
            nc.scalar.activation(vsin[:, :], vang[:, :], ACT.Sin).then_inc(s_sin, 1)
            act.wait_ge(s_sin, 1)
            nc.scalar.activation(sig[:, :, :], sine[:, :, :], ACT.Sigmoid).then_inc(s_sig, 1)

        @block.tensor
        def _(pe):
            pe.wait_ge(s_silu, 1)
            pe.wait_ge(s_in, all_in)
            for half, bank in ((0, ps_a), (1, ps_b)):
                for k in range(KT):
                    mm = nc.tensor.matmul(bank[0:B, :], sig[:, k, :], wada[:, k, half * D:(half + 1) * D],
                                          start=k == 0, stop=k == KT - 1)
            mm.then_inc(s_ada, 1)
            pe.wait_ge(s_vw, 1)
            nc.tensor.matmul(ps_v[0:DIM, 0:2 * DIM], gates[:, 0, :], rot2[:, :, :].rearrange("p c j -> p (c j)"),
                             start=True, stop=True).then_inc(s_vmm, 1)
            nc.tensor.matmul(ps_z[0:2 * DIM, :], zs[:, :], puw[:, :], start=True, stop=True).then_inc(s_z, 1)


def split_product(pe, out, pairs, last_stop=True):
    n = len(pairs)
    for i, (ah, al, bh, bl) in enumerate(pairs):
        nc_mm = pe.matmul(out, ah, bh, start=i == 0, stop=False)
        nc_mm = pe.matmul(out, al, bh, start=False, stop=False)
        nc_mm = pe.matmul(out, ah, bl, start=False, stop=i == n - 1)
    return nc_mm


def ffn_stage(nc, keep, t, scratch, l0, out):
    L = "L0" if l0 else "L1"
    name = (lambda n: f"L0_cond_{n}") if l0 else (lambda n: f"L1_cond_{n.replace('w', 'W')}")
    w1, b1, w2, b2 = (t[name(n)] for n in ("w1", "b1", "w2", "b2"))
    func = ACT.Gelu if l0 else ACT.Gelu_apprx_sigmoid
    x_src = t["x"] if l0 else scratch["x2"]
    with ExitStack() as ctx:
        sb = lambda n, s, d=F32: ctx.enter_context(nc.sbuf_tensor(f"{L}_{n}", s, d))
        ps = lambda n: ctx.enter_context(nc.psum_tensor(f"{L}_{n}", [P, 512], F32))
        sem = lambda n: ctx.enter_context(nc.semaphore(f"{L}_{n}"))
        w1h, w1l = sb("w1h", [P, KT, F], F32R), sb("w1l", [P, KT, F], F32R)
        w2h, w2l = sb("w2h", [P, FT, D], F32R), sb("w2l", [P, FT, D], F32R)
        xin = sb("xin", [P, TT, D])
        xres = sb("xres", [P, TT, D])
        w_pass = sb("w_pass", [P, TT, D])
        xth, xtl = sb("xth", [P, KT, S], F32R), sb("xtl", [P, KT, S], F32R)
        hid = [sb(f"hid{i}", [P, S]) for i in range(2)]
        hh = [sb(f"hh{i}", [P, S], F32R) for i in range(2)]
        hl = [sb(f"hl{i}", [P, S], F32R) for i in range(2)]
        b1c = sb("b1c", [P, FT])
        b2r = sb("b2r", [P, D])
        gain, offset = sb("gain", [P, D]), sb("offset", [P, D])
        stat, mv = sb("stat", [P, TT, 6]), sb("mv", [P, TT, 2])
        power, rstd, shift = sb("power", [P, TT]), sb("rstd", [P, TT]), sb("shift", [P, TT])
        turn = [ps(f"turn{i}") for i in range(2)]
        acc = [ps(f"acc{i}") for i in range(TT)]

        consts_in, w_hi, w_lo, power_set = map(sem, ("consts_in", "w_hi", "w_lo", "power_set"))
        w_in = [sem(f"w_in{i}") for i in range(2)]
        x_in, xres_in, stored = map(sem, ("x_in", "xres_in", "stored"))
        turned, xt_hi, xt_lo = map(sem, ("turned", "xt_hi", "xt_lo"))
        h_mm, h_act, h_hi, h_lo, y_mm, y_out = map(sem, ("h_mm", "h_act", "h_hi", "h_lo", "y_mm", "y_out"))
        row_added, n_var, n_rstd, n_shift, normed = map(sem, ("row_added", "n_var", "n_rstd", "n_shift", "normed"))
        gained, affine_done, dve_chain = map(sem, ("gained", "affine_done", "dve_chain"))
        passed_dve, passed_pe = sem("passed_dve"), sem("passed_pe")
        if l0:
            pub_row, row = sb("pub_row", [P, D]), sb("row", [P, D])
            ada_row = sb("ada_row", [P, 2, D])
            pdw = sb("pdw", [P, KT, WIRES])
            pd = sb("pd", [P, KT, P], F32R)
            pd_zero = sb("pd_zero", [P, KT, P])
            pdb = sb("pdb", [P, WIRES])
            pt = sb("pt", [2 * WIRES, S])
            angle = sb("angle", [P, TT, WIRES])
            cos_sin = sb("cos_sin", [P, 2, TT, WIRES])
            pairs = sb("pairs", [P, 2, TT, 4])
            amp = sb("amp", [P, TT, DIM])
            ampt = sb("ampt", [DIM, S])
            prob = sb("prob", [2 * DIM, S])
            misc = [ps(f"misc{i}") for i in range(2)]
            pd_set, p_mm, pt_out, p_turned, p_out, p_sig, halved, cs_out, amp_out, amp_turned, ampt_out, state_mm, \
                prob_out, up_mm, up_added, row_set, ada_in = map(sem, (
                    "pd_set", "p_mm", "pt_out", "p_turned", "p_out", "p_sig", "halved", "cs_out", "amp_out", "amp_turned",
                    "ampt_out", "state_mm", "prob_out", "up_mm", "up_added", "row_set", "ada_in"))
        across = lambda n: t[n].partition_broadcast(P)
        consts = [(b1c[:, :], b1.rearrange("(m p) -> p m", p=P)), (b2r[:, :], b2.partition_broadcast(P)),
                  (gain[:, :], across("L0_cond_ln_g" if l0 else "L1_cond_g2")),
                  (offset[:, :], across("L0_cond_ln_b" if l0 else "L1_cond_beta2"))]
        if l0:
            consts += [(pub_row[:, :], across("L0_cond_pu_b")), (pdb[:, :], across("L0_cond_pd_b")),
                       (pdw[:, :, :], t["L0_cond_pd_w"].rearrange("(k p) n -> p k n", p=P))]
        passing = [w_pass, xres]
        chunks = []
        for m in range(0, FT, TT):
            cut = slice(m * P, (m + TT) * P)
            chunks.append((w1.rearrange("(k p) n -> p k n", p=P)[:, :, cut], w1h[:, :, cut], w1l[:, :, cut]))
            chunks.append((w2[cut, :].rearrange("(m p) n -> p m n", p=P), w2h[:, m:m + TT, :], w2l[:, m:m + TT, :]))
        CH = len(chunks)
        ALONE = 0 if l0 else 1
        block = ctx.enter_context(nc.Block())

        @block.sync
        def _(sp):
            sp.dma_start(xin[:, :, :], rows(x_src[0])).then_inc(x_in, 16)
            sp.dma_start(passing[0][:, :, :], chunks[0][0]).then_inc(w_in[0], 16)
            for dst, src in consts:
                sp.dma_start(dst, src).then_inc(consts_in, 16)
            for c, (src, _, _) in enumerate(chunks[1:], 1):
                if c >= 2:
                    sp.wait_ge(w_lo, c - 1)
                sp.dma_start(passing[c % 2][:, :, :], src).then_inc(w_in[c % 2], 16)

            def body(b, first, last):
                if not last:
                    sp.wait_ge(turned, b * KT + KT)
                    sp.dma_start(xin[:, :, :], rows(x_src[b + 1])).then_inc(x_in, 16)
                if not first:
                    store(b - 1)
                    sp.wait_ge(stored, b * 16)
                else:
                    sp.wait_ge(w_lo, CH)
                sp.dma_start(xres[:, :, :], rows(x_src[b])).then_inc(xres_in, 16)
                if l0:
                    sp.dma_start(ada_row[:, :, :].rearrange("p a n -> p (a n)"),
                                 scratch["ada"][b].partition_broadcast(P)).then_inc(ada_in, 16)

            def store(b):
                if l0:
                    sp.wait_ge(affine_done, b * 2 * TT + 2 * TT)
                else:
                    sp.wait_ge(y_out, b * TT + TT)
                sp.dma_start(rows(out[b]), xres[:, :, :]).then_inc(stored, 16)

            each_batch(sp, body)
            store(B - 1)
            sp.wait_ge(stored, 16 * B)

        @block.gpsimd
        def _(pool):
            nc.gpsimd.memset(power[:, :], -0.5).then_inc(power_set, 1)
            pool.wait_ge(power_set, 1)
            pool.wait_ge(consts_in, 16 * len(consts))

            def norm_rstd(n):
                pool.wait_ge(n_var, n + 1)
                nc.gpsimd.tensor_tensor(rstd[:, :], mv[:, :, 1], power[:, :], ALU.pow).then_inc(n_rstd, 1)

            def norm(buf, n, g, o):
                norm_rstd(n)
                n = n - ALONE
                for i in range(TT):
                    pool.wait_ge(normed, n * TT + i + 1)
                    nc.gpsimd.tensor_tensor(buf[:, i, :], buf[:, i, :], g, ALU.mult).then_inc(gained, 1)
                    pool.wait_ge(gained, n * TT + i + 1)
                    nc.gpsimd.tensor_tensor(buf[:, i, :], buf[:, i, :], o, ALU.add).then_inc(affine_done, 1)

            def tail(b):
                norm(xres, 2 * b, gain[:, :], offset[:, :])
                pool.wait_ge(ada_in, b * 16 + 16)
                norm(xres, 2 * b + 1, ada_row[:, 0, :], ada_row[:, 1, :])

            def body(b, first, last):
                if l0 and not first:
                    tail(b - 1)
                pool.wait_ge(xres_in, b * 16 + 16)
                if l0:
                    pool.wait_ge(row_set, b + 1)
                for i in range(TT):
                    nc.gpsimd.tensor_tensor(xres[:, i, :], xres[:, i, :], (row if l0 else b2r)[:, :], ALU.add)\
                        .then_inc(row_added, 1)
                if not l0 and not last:
                    norm(xin, b + 1, gain[:, :], offset[:, :])

            if not l0:
                norm_rstd(0)
            each_batch(pool, body)
            if l0:
                norm_rstd(2 * B - 2)
                norm_rstd(2 * B - 1)

        @block.scalar
        def _(act):
            def split_weights(c):
                act.wait_ge(w_in[c % 2], 16 * (c // 2 + 1))
                nc.scalar.activation(chunks[c][1], passing[c % 2][:, :, :], ACT.Copy).then_inc(w_hi, 1)

            def norm(buf, n):
                act.wait_ge(n_shift, n + 1 - ALONE)
                for i in range(TT):
                    nc.scalar.activation(buf[:, i, :], buf[:, i, :], ACT.Identity, bias=shift[:, i:i + 1],
                                         scale=rstd[:, i:i + 1]).then_inc(normed, 1)

            def turn_out(b):
                for k in range(KT):
                    act.wait_ge(turned, b * KT + k + 1)
                    nc.scalar.activation(xth[:, k, :], turn[k % 2][:, :], ACT.Copy).then_inc(xt_hi, 1)

            def body(b, first, last):
                if l0:
                    act.wait_ge(p_mm, b + 1)
                    nc.scalar.activation(pt[:, :], misc[0][0:2 * WIRES, :], ACT.Copy).then_inc(pt_out, 1)
                for m in range(FT):
                    act.wait_ge(h_mm, b * FT + m + 1)
                    if not (first and m < 2):
                        act.wait_ge(h_lo, b * FT + m - 1)
                    nc.scalar.activation(hid[m % 2][:, :], turn[m % 2][:, :], func, bias=b1c[:, m:m + 1]).then_inc(h_act, 1)
                    if first and m < CH - 2:
                        split_weights(m + 2)
                    if l0 and not first and m == 3:
                        norm(xres, 2 * b - 2)
                    if l0 and not first and m == 7:
                        norm(xres, 2 * b - 1)
                    if l0 and m == 5:
                        act.wait_ge(p_out, b + 1)
                        nc.scalar.activation(angle[:, :, :], angle[:, :, :], ACT.Sigmoid).then_inc(p_sig, 1)
                    if l0 and m == 6:
                        act.wait_ge(halved, b + 1)
                        nc.scalar.activation(cos_sin[:, :, :, :], cos_sin[:, :, :, :], ACT.Sin).then_inc(cs_out, 1)
                    if l0 and m == 10:
                        act.wait_ge(amp_turned, b + 1)
                        nc.scalar.activation(ampt[:, :], misc[0][0:DIM, :], ACT.Copy).then_inc(ampt_out, 1)
                    if l0 and m == 11:
                        act.wait_ge(state_mm, b + 1)
                        nc.scalar.activation(prob[:, :], misc[1][0:2 * DIM, :], ACT.Square).then_inc(prob_out, 1)
                    if not l0 and not last and m == 6:
                        norm(xin, b + 1)
                if not last:
                    turn_out(b + 1)

            split_weights(0)
            split_weights(1)
            turn_out(0)
            each_batch(act, body)

        @block.vector
        def _(dve):
            link = Chain(dve, dve_chain)
            dve.wait_ge(consts_in, 16 * len(consts))
            if l0:
                link(nc.vector.memset(pd_zero[:, :, :], 0.0))
                link(nc.vector.tensor_copy(pd[:, :, :], pd_zero[:, :, :]))
                link(nc.vector.tensor_copy(pd[:, :, 0:WIRES], pdw[:, :, :]))
                nc.vector.tensor_tensor(pd[:, :, WIRES:2 * WIRES], pdw[:, :, :], pd[:, :, 0:WIRES].bitcast(F32),
                                        ALU.subtract).then_inc(pd_set, 1)

            def split_weights(c):
                _, hi, lo = chunks[c]
                dve.wait_ge(w_hi, c + 1)
                nc.vector.tensor_tensor(lo, passing[c % 2][:, :, :], hi.bitcast(F32), ALU.subtract).then_inc(w_lo, 1)

            def norm_stats(buf, n):
                for i in range(TT):
                    link.step(nc.vector.bn_stats(stat[:, i, :], buf[:, i, :]))
                wait_apart(dve, passed_dve, (dve_chain, link.base + link.n))
                for i in range(TT):
                    link.step(nc.vector.bn_aggr(mv[:, i, :], stat[:, i, :]))
                link.wait()
                nc.vector.tensor_scalar(mv[:, :, 1], mv[:, :, 1], EPS, None, ALU.add).then_inc(n_var, 1)

            def norm_shift(n):
                dve.wait_ge(n_rstd, n + 1)
                nc.vector.scalar_tensor_tensor(shift[:, :], mv[:, :, 0], -1.0, rstd[:, :], ALU.mult, ALU.mult)\
                    .then_inc(n_shift, 1)

            def norm_alone(buf, n, g, o, written):
                norm_stats(buf, n)
                for i in range(TT):
                    link.step(nc.vector.scalar_tensor_tensor(buf[:, i, :], buf[:, i, :], mv[:, i, 0:1], g,
                                                             ALU.subtract, ALU.mult))
                dve.wait_ge(n_rstd, n + 1)
                link.wait()
                for i in range(TT):
                    nc.vector.scalar_tensor_tensor(buf[:, i, :], buf[:, i, :], rstd[:, i:i + 1], o,
                                                   ALU.mult, ALU.add).then_inc(affine_done, 1)
                if not written:
                    dve.wait_ge(affine_done, n * TT + TT)

            def turn_out(b):
                for k in range(KT):
                    dve.wait_ge(xt_hi, b * KT + k + 1)
                    nc.vector.tensor_tensor(xtl[:, k, :], turn[k % 2][:, :], xth[:, k, :].bitcast(F32), ALU.subtract)\
                        .then_inc(xt_lo, 1)

            def circuit_row(b, first):
                if not first:
                    dve.wait_ge(row_added, b * TT)
                link(nc.vector.tensor_scalar(row[:, :], b2r[:, :], keep.take_f[:, bass.ds(b, 1)], None, ALU.mult))
                nc.vector.scalar_tensor_tensor(row[:, :], pub_row[:, :], keep.q_factor[:, bass.ds(b, 1)], row[:, :],
                                               ALU.mult, ALU.add).then_inc(row_set, 1)

            def circuit_inputs(b):
                dve.wait_ge(p_turned, b + 1)
                halves = misc[1][:, 0:TT * 2 * WIRES].rearrange("p (t a w) -> p t w a", t=TT, a=2)
                link(nc.vector.tensor_reduce(angle[:, :, :], halves, AX.X, ALU.add))
                link(nc.vector.tensor_tensor(angle[:, :, :], angle[:, :, :],
                                             pdb[:, :].unsqueeze(1).to_broadcast([P, TT, WIRES]), ALU.add))
                nc.vector.tensor_scalar(angle[:, :, :], angle[:, :, :], 10.0, -10.0, ALU.min, ALU.max).then_inc(p_out, 1)

            def circuit_angles(b):
                dve.wait_ge(p_sig, b + 1)
                link(nc.vector.tensor_scalar(cos_sin[:, 1, :, :], angle[:, :, :], PI, 0.5, ALU.mult, ALU.mult))
                nc.vector.tensor_scalar(cos_sin[:, 0, :, :], cos_sin[:, 1, :, :], -1.0, PI / 2, ALU.mult, ALU.add)\
                    .then_inc(halved, 1)

            def circuit_amplitudes(b):
                dve.wait_ge(cs_out, b + 1)
                for h in range(2):
                    for i in range(2):
                        one = cos_sin[:, i, :, 2 * h:2 * h + 1].to_broadcast([P, TT, 2])
                        two = cos_sin[:, :, :, 2 * h + 1].rearrange("p c t -> p t c")
                        link(nc.vector.tensor_tensor(pairs[:, h, :, 2 * i:2 * i + 2], one, two, ALU.mult))
                for i in range(4):
                    ins = nc.vector.tensor_tensor(amp[:, :, 4 * i:4 * i + 4],
                                                  pairs[:, 0, :, i:i + 1].to_broadcast([P, TT, 4]),
                                                  pairs[:, 1, :, :], ALU.mult)
                    ins.then_inc(amp_out, 1)

            def circuit_add(b, i):
                dve.wait_ge(up_mm, b * TT + i + 1)
                dve.wait_ge(row_added, b * TT + i + 1)
                nc.vector.scalar_tensor_tensor(xres[:, i, :], misc[i % 2][:, :], keep.q_factor[:, bass.ds(b, 1)],
                                               xres[:, i, :], ALU.mult, ALU.add).then_inc(up_added, 1)

            def body(b, first, last):
                if l0:
                    links = 1 + 2 + 1 + 4 + (0 if first else 4 * TT)
                    link.at(ahead if first else ahead + 8 + (b - 1) * (8 + 4 * TT))
                else:
                    links = 0 if last else 2 * TT
                    link.at(ahead + b * 2 * TT)
                if l0:
                    circuit_row(b, first)
                for m in range(FT):
                    dve.wait_ge(h_act, b * FT + m + 1)
                    if not (first and m < 2):
                        dve.wait_ge(y_mm, b * FT + m - 1)
                    nc.vector.tensor_copy(hh[m % 2][:, :], hid[m % 2][:, :]).then_inc(h_hi, 1)
                    dve.wait_ge(h_hi, b * FT + m + 1)
                    nc.vector.tensor_tensor(hl[m % 2][:, :], hid[m % 2][:, :], hh[m % 2][:, :].bitcast(F32), ALU.subtract)\
                        .then_inc(h_lo, 1)
                    if first and m < CH - 2:
                        split_weights(m + 2)
                    if l0 and not first:
                        if m == 0:
                            dve.wait_ge(y_out, b * TT)
                            norm_stats(xres, 2 * b - 2)
                        if m == 2:
                            norm_shift(2 * b - 2)
                        if m == 5:
                            dve.wait_ge(affine_done, b * 2 * TT - TT)
                            norm_stats(xres, 2 * b - 1)
                        if m == 6:
                            norm_shift(2 * b - 1)
                    if l0:
                        if m == 3:
                            circuit_inputs(b)
                        if m == 5:
                            circuit_angles(b)
                        if m == 7:
                            circuit_amplitudes(b)
                        if m >= 12:
                            circuit_add(b, m - 12)
                    if not l0 and not last:
                        if m == 3:
                            dve.wait_ge(x_in, b * 16 + 32)
                            norm_stats(xin, b + 1)
                        if m == 5:
                            norm_shift(b + 1)
                if not last:
                    turn_out(b + 1)
                dve.wait_ge(y_mm, b * FT + FT)
                for i in range(TT):
                    if l0:
                        dve.wait_ge(up_added, b * TT + i + 1)
                        nc.vector.scalar_tensor_tensor(xres[:, i, :], acc[i][:, :], keep.take_f[:, bass.ds(b, 1)],
                                                       xres[:, i, :], ALU.mult, ALU.add).then_inc(y_out, 1)
                    else:
                        dve.wait_ge(row_added, b * TT + i + 1)
                        nc.vector.tensor_tensor(xres[:, i, :], acc[i][:, :], xres[:, i, :], ALU.add).then_inc(y_out, 1)
                assert link.n == links, (link.n, links)

            if not l0:
                dve.wait_ge(x_in, 16)
                norm_alone(xin, 0, gain[:, :], offset[:, :], True)
            ahead = link.n
            split_weights(0)
            split_weights(1)
            turn_out(0)
            each_batch(dve, body)
            if l0:
                link.at(ahead + 8 + (B - 1) * (8 + 4 * TT))
                dve.wait_ge(y_out, B * TT)
                norm_alone(xres, 2 * B - 2, gain[:, :], offset[:, :], False)
                dve.wait_ge(ada_in, B * 16)
                norm_alone(xres, 2 * B - 1, ada_row[:, 0, :], ada_row[:, 1, :], True)

        @block.tensor
        def _(pe):
            def turn_in(b, k, ahead):
                if k == 0:
                    if l0:
                        pe.wait_ge(x_in, b * 16 + 16)
                    else:
                        pe.wait_ge(affine_done, b * TT + TT)
                if ahead and k < 2:
                    pe.wait_ge(h_act, b * FT - 1 + k)
                if k >= 2:
                    pe.wait_ge(xt_lo, b * KT + k - 1)
                for i in range(TT):
                    mm = pe.transpose(turn[k % 2][:, i * P:(i + 1) * P], xin[:, i, k * P:(k + 1) * P], keep.ident[:, :])
                mm.then_inc(turned, 1)

            def up(b, m, first):
                if first and m % TT == 0:
                    pe.wait_ge(w_lo, m // TT * 2 + 1)
                if m >= 2:
                    pe.wait_ge(h_act, b * FT + m - 1)
                cut = slice(m * P, (m + 1) * P)
                split_product(pe, turn[m % 2][:, :], [(w1h[:, k, cut], w1l[:, k, cut], xth[:, k, :], xtl[:, k, :])
                                                      for k in range(KT)]).then_inc(h_mm, 1)

            def down(b, m, first):
                if first and m % TT == 0:
                    pe.wait_ge(w_lo, m // TT * 2 + 2)
                pe.wait_ge(h_lo, b * FT + m + 1)
                if m == 0 and not first:
                    pe.wait_ge(y_out, b * TT)
                for i in range(TT):
                    cut = slice(i * P, (i + 1) * P)
                    pe.matmul(acc[i][:, :], hh[m % 2][:, cut], w2h[:, m, :], start=m == 0, stop=False)
                    pe.matmul(acc[i][:, :], hl[m % 2][:, cut], w2h[:, m, :], start=False, stop=False)
                    mm = pe.matmul(acc[i][:, :], hh[m % 2][:, cut], w2l[:, m, :], start=False, stop=m == FT - 1)
                mm.then_inc(y_mm, 1)

            def circuit(b, m, first):
                if m == 2:
                    if not first:
                        pe.wait_ge(up_added, b * TT)
                    wait_apart(pe, passed_pe, (pt_out, b + 1))
                    for i in range(TT):
                        mm = pe.transpose(misc[1][:, i * 2 * WIRES:(i + 1) * 2 * WIRES], pt[:, i * P:(i + 1) * P],
                                          keep.ident[0:2 * WIRES, 0:2 * WIRES])
                    mm.then_inc(p_turned, 1)
                if m == 9:
                    pe.wait_ge(amp_out, b * 4 + 4)
                    for i in range(TT):
                        mm = pe.transpose(misc[0][0:DIM, i * P:(i + 1) * P], amp[:, i, :], keep.ident[:, :])
                    mm.then_inc(amp_turned, 1)
                if m == 11:
                    wait_apart(pe, passed_pe, (ampt_out, b + 1))
                    pe.matmul(misc[1][0:2 * DIM, :], keep.circuit[:, :], ampt[:, :], start=True, stop=True)\
                        .then_inc(state_mm, 1)
                if m >= 12:
                    i = m - 12
                    if i == 0:
                        pe.wait_ge(prob_out, b + 1)
                    if i >= 2:
                        pe.wait_ge(up_added, b * TT + i - 1)
                    pe.matmul(misc[i % 2][:, :], prob[:, i * P:(i + 1) * P], keep.zpu[:, :], start=True, stop=True)\
                        .then_inc(up_mm, 1)

            def body(b, first, last):
                pe.wait_ge(xt_lo, b * KT + KT)
                if l0:
                    if first:
                        pe.wait_ge(pd_set, 1)
                    else:
                        pe.wait_ge(up_added, b * TT)
                    for k in range(KT):
                        pe.matmul(misc[0][:, :], pd[:, k, :], xth[:, k, :], start=k == 0, stop=False)
                        mm = pe.matmul(misc[0][:, :], pd[:, k, :], xtl[:, k, :], start=False, stop=k == KT - 1)
                    mm.then_inc(p_mm, 1)
                for m in range(FT):
                    up(b, m, first)
                    if m >= 2:
                        down(b, m - 2, first)
                    if l0:
                        circuit(b, m, first)
                for half in range(2):
                    if not last:
                        turn_in(b + 1, 2 * half, True)
                        turn_in(b + 1, 2 * half + 1, True)
                    down(b, FT - 2 + half, first)

            for k in range(KT):
                turn_in(0, k, False)
            each_batch(pe, body)


def attention_stage(nc, keep, t, scratch):
    UNITS = H * TT
    SLOTS = 8
    ITEMS = 6 * TT
    IT_Q, IT_K, IT_V, IT_X, IT_C, IT_O = (TT * i for i in range(6))
    HIS = 5 * TT
    VB = TT * H
    VW = 2 * HD + 2
    ORDER = [4 * (pair // 4 * 2 + i) + pair % 4 for pair in range(H // 2) for i in range(2)]
    PAIR = 2 * TT
    with ExitStack() as ctx:
        sb = lambda n, s, d=F32: ctx.enter_context(nc.sbuf_tensor(f"at_{n}", s, d))
        ps = lambda n: ctx.enter_context(nc.psum_tensor(f"at_{n}", [P, 512], F32))
        sem = lambda n: ctx.enter_context(nc.semaphore(f"at_{n}"))
        weight = {n: (sb(f"w{n}h", [P, KT, D], F32R), sb(f"w{n}l", [P, KT, D], F32R)) for n in "qkvo"}
        context = sb("context", [P, TT, D])
        qk = sb("qk", [P, 4, KT, S])
        QH, KH, QL, KL = range(4)
        ahead_x, xres = qk[:, QH:KH + 1, 0:2, :], qk[:, QL:KL + 1, 0:2, :]
        x_tile = lambda buf, i: buf[:, i // 2, i % 2, :]
        qk_tile = lambda k: (k + 2) % KT
        flat = [sb(f"flat{i}", [P, S]) for i in range(2)]
        stack = [sb(f"stack{i}", [P, 2, 2, S], F32R) for i in range(2)]
        v = sb("v", [P, VB * VW + P - VW], F32R)
        v_tiles = v[:, 0:VB * VW].rearrange("p (t h c) -> p t h c", t=TT, c=VW)
        bias = sb("bias", [P, SLOTS, S])
        pt_hi = [sb(f"pt_hi{i}", [P, KT, S], F32R) for i in range(2)]
        pt_lo = [sb(f"pt_lo{i}", [P, KT, S], F32R) for i in range(2)]
        xt, ct = (pt_hi[0], pt_lo[0]), (pt_hi[1], pt_lo[1])
        ctx_flat = sb("ctx_flat", [P, S])
        head_sum = sb("head_sum", [P, TT, HD])
        inv_sum = sb("inv_sum", [P, TT])
        mask8 = sb("mask8", [P, TT, S], U8)
        mask = sb("mask", [P, TT, S], BF16)
        neg_top = sb("neg_top", [P, SLOTS])
        bqc, bkc = sb("bqc", [P, KT]), sb("bkc", [P, KT])
        bvr, bor = sb("bvr", [P, D]), sb("bor", [P, D])
        ones = sb("ones", [P, P])
        score = [ps(f"score{i}") for i in range(3)]
        turn = [ps(f"turn{i}") for i in range(3)]
        head_ps, head_turn = ps("head"), ps("head_turn")
        item_bank = lambda i: score[(i - IT_X) % 3] if i < IT_Q or IT_X <= i < IT_O else (turn + [head_ps])[i % TT]

        consts_in, w_hi, w_lo, ones_set = map(sem, ("consts_in", "w_hi", "w_lo", "ones_set"))
        w_in = [sem(f"w_in{i}") for i in range(2)]
        x_in, xres_in, stored, mask_in, mask_set = map(sem, ("x_in", "xres_in", "stored", "mask_in", "mask_set"))
        item_mm, item_flat, item_hi, item_out, res_ready = map(sem, ("item_mm", "item_flat", "item_hi", "item_out", "res_ready"))
        bias_in = [sem(f"bias_in{i}") for i in range(SLOTS // 2)]
        stack_in = [sem(f"stack_in{i}") for i in range(2)]
        masked, score_mm, scored, exped, turned, p_hi, p_lo = map(sem, (
            "masked", "score_mm", "scored", "exped", "turned", "p_hi", "p_lo"))
        head_mm, head_flat, head_turned, head_summed, head_out, dve_chain = map(sem, (
            "head_mm", "head_flat", "head_turned", "head_summed", "head_out", "dve_chain"))
        inverted = sem("inverted")
        passed_dve, passed_sp = sem("passed_dve"), sem("passed_sp")
        consts = [(bqc[:, :], t["L1_cond_bq"].rearrange("(m p) -> p m", p=P)),
                  (bkc[:, :], t["L1_cond_bk"].rearrange("(m p) -> p m", p=P)),
                  (bvr[:, :], t["L1_cond_bv"].partition_broadcast(P)), (bor[:, :], t["L1_cond_bo"].partition_broadcast(P))]
        passing = [bias[:, 0:TT, :], bias[:, TT:SLOTS, :]]
        chunks = [(t[f"L1_cond_W{n}"].rearrange("(k p) n -> p k n", p=P), *weight[n]) for n in "qkvo"]
        bias_src = t["fside_Bx16xSxS_0"]

        def done(b, i, last, per=ITEMS):
            return TT + b * per + i + 1 - (TT if last and i >= IT_C else 0)

        block = ctx.enter_context(nc.Block())

        @block.sync
        def _(sp):
            def load_x(buf, b, loaded):
                for half in range(2):
                    sp.dma_start(buf[:, half], rows(scratch["x1"][b])[:, 2 * half:2 * half + 2, :]).then_inc(loaded, 16)

            for dst, src in consts:
                sp.dma_start(dst, src).then_inc(consts_in, 16)
            load_x(ahead_x, 0, x_in)
            sp.dma_start(mask8[:, :, :], rows(t["mask_Bx1xSxS_bk0"][0, 0])).then_inc(mask_in, 16)
            for c, (src, _, _) in enumerate(chunks):
                if c >= 2:
                    sp.wait_ge(w_lo, c - 1)
                sp.dma_start(passing[c % 2], src).then_inc(w_in[c % 2], 16)

            def load_bias(b, two, first):
                if two >= SLOTS // 2 or not first:
                    sp.wait_ge(turned, b * UNITS + 2 * two + 2 - SLOTS)
                elif two % 2 == 0:
                    sp.wait_ge(w_lo, 3 + two // 2)
                h, u = divmod(2 * two, TT)
                slot = 2 * two % SLOTS
                sp.dma_start(bias[:, slot:slot + 2, :],
                             bias_src[b, ORDER[h], u * P:(u + 2) * P, :].rearrange("(t p) n -> p t n", p=P))\
                    .then_inc(bias_in[two % (SLOTS // 2)], 16)

            def load_stack(b, pair):
                if pair == 0:
                    sp.wait_ge(item_out, done(b, IT_V - 1, False))
                if pair >= 2:
                    sp.wait_ge(score_mm, b * UNITS + (pair - 1) * PAIR)
                j, k = ORDER[2 * pair] % 4, ORDER[2 * pair] // 4
                src, to = slice(j * HD, (j + 1) * HD), stack[pair % 2][:, :, :, :].bitcast(F32)
                two = slice(k, k + 2)
                for block, dst, part in ((0, slice(0, 2), slice(QH, KH + 1)), (1, slice(0, 2), slice(QH, KL + 1, KL - QH)),
                                         (2, slice(0, 1), slice(QL, QL + 1)), (2, slice(1, 2), slice(KH, KH + 1)),
                                         (3, slice(0, 2), slice(QL, KL + 1))):
                    sp.dma_start(to[block * HD:(block + 1) * HD, dst, :, :], qk[src, part, two, :])\
                        .then_inc(stack_in[pair % 2], 16)

            def body(b, first, last):
                for two in range(SLOTS // 2):
                    load_bias(b, two, first)
                load_stack(b, 0)
                load_stack(b, 1)
                for two in range(SLOTS // 2, UNITS // 2):
                    load_bias(b, two, first)
                    if two % 4 == 2 and two // 4 + 1 < H // 2:
                        load_stack(b, two // 4 + 1)
                    if two == 5 * UNITS // 16:
                        sp.wait_ge(score_mm, b * UNITS + UNITS // 2)
                        load_x(xres, b, xres_in)
                        if not last:
                            load_x(ahead_x, b + 1, x_in)
                if not last:
                    wait_apart(sp, passed_sp, (mask_set, b + 1))
                    sp.dma_start(mask8[:, :, :], rows(t["mask_Bx1xSxS_bk0"][b + 1, 0])).then_inc(mask_in, 16)
                sp.wait_ge(item_out, done(b, ITEMS - 1, last))
                for half in range(2):
                    sp.dma_start(rows(scratch["x2"][b])[:, 2 * half:2 * half + 2, :], xres[:, half]).then_inc(stored, 16)

            each_batch(sp, body)
            sp.wait_ge(stored, 32 * B)

        @block.gpsimd
        def _(pool):
            pool.wait_ge(consts_in, 16 * len(consts))

            def body(b, first, last):
                def head(h):
                    pool.wait_ge(head_summed, b * H + h + 1)
                    nc.gpsimd.tensor_tensor(context[:, :, ORDER[h] * HD:(ORDER[h] + 1) * HD], head_sum[:, :, :],
                                            inv_sum[:, :].unsqueeze(2).to_broadcast([P, TT, HD]), ALU.mult).then_inc(head_out, 1)

                pool.wait_ge(mask_set, b + 1)
                for n in range(UNITS):
                    if n % 2 == 0:
                        pair = n // 2
                        pool.wait_ge(bias_in[pair % 4], b * (UNITS // SLOTS * 16) + 16 * (pair // 4 + 1))
                    tile = bias[:, n % SLOTS, :]
                    nc.gpsimd.tensor_tensor(tile, tile, mask[:, n % TT, :], ALU.add).then_inc(masked, 1)
                    if n >= 14 and (n - 14) % TT == 0:
                        head((n - 14) // TT)
                for h in range((UNITS - 15) // TT + 1, H):
                    head(h)
                pool.wait_ge(xres_in, b * 32 + 32)
                for i in range(TT):
                    nc.gpsimd.tensor_tensor(x_tile(xres, i), x_tile(xres, i), bor[:, :], ALU.add).then_inc(res_ready, 1)

            each_batch(pool, body)

        @block.scalar
        def _(act):
            def split_weights(c):
                act.wait_ge(w_in[c % 2], 16 * (c // 2 + 1))
                nc.scalar.activation(chunks[c][1][:, :, :], passing[c % 2], ACT.Copy).then_inc(w_hi, 1)

            split_weights(0)
            split_weights(1)

            def transpose_hi(b, i, last):
                k = i % TT
                if i >= IT_X:
                    act.wait_ge(head_mm, b * H + (H if i >= IT_C else H - 1))
                act.wait_ge(item_mm, done(b, i, last))
                hi = (ct if i >= IT_C else xt)[0]
                nc.scalar.activation(hi[:, k, :], item_bank(i)[:, :], ACT.Copy).then_inc(item_hi, 1)

            def body(b, first, last):
                def item(i):
                    k = i % TT
                    if first and i in (IT_Q, IT_K):
                        split_weights(2 + i // TT)
                    act.wait_ge(item_flat, b * 3 * TT + i + 1)
                    if i < IT_V:
                        if not first and qk_tile(k) < 2:
                            act.wait_ge(stored, b * 32)
                        dst, src = qk[:, QH if i < IT_K else KH, qk_tile(k), :].bitcast(F32R), flat[k % 2][:, :]
                    else:
                        dst = v_tiles[:, k, :, 0:HD]
                        src = flat[k % 2][:, :].rearrange("p (h d) -> p h d", h=H)
                    nc.scalar.activation(dst, src, ACT.Copy).then_inc(item_hi, 1)

                def exp(n):
                    act.wait_ge(scored, b * UNITS + n + 1)
                    tile = bias[:, n % SLOTS, :]
                    nc.scalar.activation(tile, tile, ACT.Exp, bias=neg_top[:, n % SLOTS:n % SLOTS + 1], scale=-1.0)\
                        .then_inc(exped, 1)

                def hi(n):
                    h, u = divmod(n, TT)
                    act.wait_ge(turned, b * UNITS + n + 1)
                    if h >= 2 and u == 0:
                        act.wait_ge(head_mm, b * H + h - 1)
                    nc.scalar.activation(pt_hi[h % 2][:, :, u * P:(u + 1) * P],
                                         turn[n % 3][:, :].rearrange("p (k q) -> p k q", k=KT), ACT.Copy).then_inc(p_hi, 1)

                def head(h):
                    act.wait_ge(head_mm, b * H + h + 1)
                    if h >= 1:
                        act.wait_ge(head_turned, b * H + h)
                    nc.scalar.activation(ctx_flat[:, :], head_ps[:, :], ACT.Copy).then_inc(head_flat, 1)

                for i in range(IT_X):
                    if i == IT_X - 1:
                        exp(0)
                    item(i)
                for n in range(1, UNITS):
                    exp(n)
                    if n >= 2:
                        hi(n - 2)
                    if n >= 9 and (n - 9) % TT == 0:
                        head((n - 9) // TT)
                hi(UNITS - 2)
                hi(UNITS - 1)
                head(H - 2)
                if not last:
                    for i in range(IT_X, IT_C - 1):
                        transpose_hi(b, i, last)
                head(H - 1)
                for i in range(IT_C if last else IT_C - 1, IT_O):
                    transpose_hi(b, i, last)

            for i in range(-TT, 0):
                transpose_hi(0, i, False)
            each_batch(act, body)

        @block.vector
        def _(dve):
            link = Chain(dve, dve_chain)
            dve.wait_ge(consts_in, 16 * len(consts))
            link(nc.vector.memset(ones[:, :], 1.0))
            link(nc.vector.tensor_copy(v_tiles[:, :, :, 2 * HD:VW].rearrange("p t h c -> p (t h) c"),
                                       ones[:, :].rearrange("p (b c) -> p b c", c=2)))
            link(nc.vector.tensor_copy(v[:, VB * VW:], ones[:, 0:P - VW]))
            ahead = link.n

            def split_weights(c):
                _, hi, lo = chunks[c]
                dve.wait_ge(w_hi, c + 1)
                nc.vector.tensor_tensor(lo[:, :, :], passing[c % 2], hi[:, :, :].bitcast(F32), ALU.subtract).then_inc(w_lo, 1)

            split_weights(0)
            split_weights(1)

            def transpose_lo(b, i, last):
                dve.wait_ge(item_hi, done(b, i, last, HIS))
                hi, lo = ct if i >= IT_C else xt
                k = i % TT
                nc.vector.tensor_tensor(lo[:, k, :], item_bank(i)[:, :], hi[:, k, :].bitcast(F32), ALU.subtract)\
                    .then_inc(item_out, 1)

            def body(b, first, last):
                def item(i):
                    k = i % TT
                    bank = item_bank(i)
                    if first and i in (IT_Q, IT_K):
                        split_weights(2 + i // TT)
                    dve.wait_ge(item_mm, done(b, i, last))
                    if i >= IT_O:
                        dve.wait_ge(res_ready, b * TT + k + 1)
                        nc.vector.tensor_tensor(x_tile(xres, k), bank[:, :], x_tile(xres, k), ALU.add).then_inc(item_out, 1)
                        return
                    tile = flat[k % 2][:, :]
                    if i < IT_K:
                        m = qk_tile(k)
                        ins = nc.vector.tensor_scalar(tile, bank[:, :], bqc[:, m:m + 1], Q_SCALE, ALU.add, ALU.mult)
                    elif i < IT_V:
                        m = qk_tile(k)
                        ins = nc.vector.tensor_scalar(tile, bank[:, :], bkc[:, m:m + 1], None, ALU.add)
                    else:
                        ins = nc.vector.tensor_tensor(tile, bank[:, :], bvr[:, :], ALU.add)
                    ins.then_inc(item_flat, 1)
                    dve.wait_ge(item_hi, done(b, i, last, HIS))
                    if i < IT_V:
                        hi, lo = (QH, QL) if i < IT_K else (KH, KL)
                        hi, lo = qk[:, hi, m, :], qk[:, lo, m, :].bitcast(F32R)
                    else:
                        hi, lo = v_tiles[:, k, :, 0:HD].bitcast(F32), v_tiles[:, k, :, HD:2 * HD]
                        tile = tile.rearrange("p (h d) -> p h d", h=H)
                    nc.vector.tensor_tensor(lo, tile, hi, ALU.subtract).then_inc(item_out, 1)

                def scores(n):
                    slot = n % SLOTS
                    wait_apart(dve, passed_dve, (masked, b * UNITS + n + 1), (score_mm, b * UNITS + n + 1))
                    nc.vector.tensor_tensor_reduce(bias[:, slot, :], score[n % 3][:, :], bias[:, slot, :], -1.0, -MASKED,
                                                   ALU.add, ALU.min, neg_top[:, slot:slot + 1]).then_inc(scored, 1)

                def lo(n):
                    h, u = divmod(n, TT)
                    dve.wait_ge(p_hi, b * UNITS + n + 1)
                    cut = slice(u * P, (u + 1) * P)
                    nc.vector.tensor_tensor(pt_lo[h % 2][:, :, cut], turn[n % 3][:, :].rearrange("p (k q) -> p k q", k=KT),
                                            pt_hi[h % 2][:, :, cut].bitcast(F32), ALU.subtract).then_inc(p_lo, 1)

                def head(h):
                    dve.wait_ge(head_turned, b * H + h + 1)
                    if not (first and h == 0):
                        dve.wait_ge(head_out, b * H + h)
                    tiles = head_turn[:, :].rearrange("p (t c) -> p t c", t=TT)
                    nc.vector.reciprocal(inv_sum[:, :], tiles[:, :, 2 * HD]).then_inc(inverted, 1)
                    nc.vector.tensor_reduce(head_sum[:, :, :], tiles[:, :, 0:2 * HD].rearrange("p t (a d) -> p t d a", a=2),
                                            AX.X, ALU.add).then_inc(head_summed, 1)

                dve.wait_ge(mask_in, b * 16 + 16)
                if not first:
                    dve.wait_ge(masked, b * UNITS)
                nc.vector.tensor_scalar(mask[:, :, :], mask8[:, :, :], MASKED, None, ALU.mult).then_inc(mask_set, 1)
                for i in range(IT_X):
                    if i == IT_X - 1:
                        scores(0)
                    item(i)
                for n in range(1, UNITS):
                    scores(n)
                    if n >= 3:
                        lo(n - 3)
                    if n >= 11 and (n - 11) % TT == 0:
                        head((n - 11) // TT)
                for n in range(UNITS - 3, UNITS):
                    lo(n)
                if last:
                    head(H - 2)
                else:
                    transpose_lo(b, IT_X, last)
                    transpose_lo(b, IT_X + 1, last)
                    head(H - 2)
                    transpose_lo(b, IT_X + 2, last)
                    transpose_lo(b, IT_X + 3, last)
                head(H - 1)
                for i in range(IT_C, IT_O):
                    transpose_lo(b, i, last)
                for i in range(IT_O, ITEMS):
                    item(i)

            for i in range(-TT, 0):
                transpose_lo(0, i, False)
            each_batch(dve, body)

        @block.tensor
        def _(pe):
            def transpose(b, i, last):
                k = i % TT
                if i == -TT:
                    pe.wait_ge(x_in, 32)
                elif i == IT_X:
                    pe.wait_ge(x_in, b * 32 + 64)
                elif i in (IT_C, IT_C + 2):
                    pe.wait_ge(head_out, b * H + (H // 2 if i == IT_C else H))
                if i in (IT_X, IT_C):
                    pe.wait_ge(scored, b * UNITS + UNITS)
                if i == -1 or IT_X + 3 <= i and (not last or i == IT_C + 3):
                    pe.wait_ge(item_out, done(b, i - 3, last))
                for j in range(TT):
                    src = context[:, j, k * P:(k + 1) * P] if i >= IT_C else x_tile(ahead_x, j)[:, k * P:(k + 1) * P]
                    mm = pe.transpose(item_bank(i)[:, j * P:(j + 1) * P], src, keep.ident[:, :])
                mm.then_inc(item_mm, 1)

            def body(b, first, last):
                def item(i):
                    k = i % TT
                    bank = item_bank(i)
                    if i == IT_O:
                        pe.wait_ge(item_out, done(b, i - 1, last))
                    elif first and i < IT_K:
                        if i == 0:
                            pe.wait_ge(item_out, TT)
                    elif i < IT_X:
                        pe.wait_ge(item_out, done(b, i - TT, False))
                    if first and k == 0:
                        pe.wait_ge(w_lo, TT if i == IT_O else i // TT + 1)
                    if i < IT_V:
                        wh, wl = weight["q" if i < IT_K else "k"]
                        cut = slice(qk_tile(k) * P, (qk_tile(k) + 1) * P)
                        mm = split_product(pe, bank[:, :], [(wh[:, j, cut], wl[:, j, cut], xt[0][:, j, :], xt[1][:, j, :])
                                                            for j in range(KT)])
                    else:
                        (wh, wl), (hi, lo) = (weight["v"], xt) if i < IT_X else (weight["o"], ct)
                        cut = slice(k * P, (k + 1) * P)
                        mm = split_product(pe, bank[:, :], [(hi[:, j, cut], lo[:, j, cut], wh[:, j, :], wl[:, j, :])
                                                            for j in range(KT)])
                    mm.then_inc(item_mm, 1)

                def scores(n):
                    h, u = divmod(n, TT)
                    pair = h // 2
                    if n % PAIR == 0:
                        pe.wait_ge(stack_in[pair % 2], b * (H // 4 * 5 * 16) + (pair // 2 + 1) * 5 * 16)
                    if n >= 3:
                        pe.wait_ge(scored, b * UNITS + n - 2)
                    pe.matmul(score[n % 3][:, :], stack[pair % 2][:, 0, h % 2, u * P:(u + 1) * P], stack[pair % 2][:, 1, h % 2, :],
                              start=True, stop=True).then_inc(score_mm, 1)

                def turn_unit(n):
                    pe.wait_ge(exped, b * UNITS + n + 1)
                    if n == 0:
                        pe.wait_ge(item_out, done(b, IT_X - 1, False))
                    if n >= 3:
                        pe.wait_ge(p_lo, b * UNITS + n - 2)
                    for k in range(KT):
                        mm = pe.transpose(turn[n % 3][:, k * P:(k + 1) * P], bias[:, n % SLOTS, k * P:(k + 1) * P],
                                          keep.ident[:, :])
                    mm.then_inc(turned, 1)

                def head(h, half):
                    if half == 0:
                        pe.wait_ge(p_lo, b * UNITS + (h + 1) * TT)
                        if h >= 1:
                            pe.wait_ge(head_flat, b * H + h)
                    for k in (2 * half, 2 * half + 1):
                        start = (k * H + ORDER[h]) * VW
                        vk = v[:, start:start + P]
                        pe.matmul(head_ps[:, :], vk, pt_hi[h % 2][:, k, :], start=k == 0, stop=False)
                        mm = pe.matmul(head_ps[:, :], vk, pt_lo[h % 2][:, k, :], start=False, stop=k == KT - 1)
                    if half == 1:
                        mm.then_inc(head_mm, 1)

                def turn_head(h):
                    pe.wait_ge(head_flat, b * H + h + 1)
                    if h >= 1:
                        pe.wait_ge(head_summed, b * H + h)
                    for i in range(TT):
                        mm = pe.transpose(head_turn[:, i * P:(i + 1) * P], ctx_flat[:, i * P:(i + 1) * P], keep.ident[:, :])
                    mm.then_inc(head_turned, 1)

                for i in range(IT_X):
                    item(i)
                    if i >= IT_X - 2:
                        scores(i - IT_X + 2)
                scores(2)
                for n in range(UNITS):
                    if n + 3 < UNITS:
                        scores(n + 3)
                    turn_unit(n)
                    if n >= 7 and (n - 7) % TT == 0:
                        head((n - 7) // TT, 0)
                    if n >= 8 and (n - 8) % TT == 0:
                        head((n - 8) // TT, 1)
                    if n >= 10 and (n - 10) % TT == 0:
                        turn_head((n - 10) // TT)
                head(H - 2, 1)
                if not last:
                    transpose(b, IT_X, last)
                    transpose(b, IT_X + 1, last)
                turn_head(H - 2)
                if not last:
                    transpose(b, IT_X + 2, last)
                head(H - 1, 0)
                head(H - 1, 1)
                if not last:
                    transpose(b, IT_X + 3, last)
                turn_head(H - 1)
                for i in range(IT_C, IT_O):
                    transpose(b, i, last)
                for i in range(IT_O, ITEMS):
                    item(i)

            for i in range(-TT, 0):
                transpose(0, i, False)
            each_batch(pe, body)


class Keep:

    def __init__(self, nc, ctx):
        sb = lambda n, s: ctx.enter_context(nc.sbuf_tensor(n, s, F32))
        self.ident = sb("ident", [P, P])
        self.circuit = sb("circuit", [DIM, 2 * DIM])
        self.zpu = sb("zpu", [2 * DIM, D])
        self.take_q = sb("take_q", [P, B])
        self.take_f = sb("take_f", [P, B])
        self.q_factor = sb("q_factor", [P, B])


def build(nc, t, consts, out):
    scratch = {"x1": nc.dram_tensor("x1_scratch", (B, S, D), F32, kind="Internal").ap(),
               "x2": nc.dram_tensor("x2_scratch", (B, S, D), F32, kind="Internal").ap(),
               "ada": nc.dram_tensor("ada_scratch", (B, 2 * D), F32, kind="Internal").ap()}
    with ExitStack() as ctx, nc.allow_non_contiguous_dma(reason="small bias vectors as columns"):
        keep = Keep(nc, ctx)
        setup_stage(nc, keep, t, consts, scratch)
        ffn_stage(nc, keep, t, scratch, True, scratch["x1"])
        attention_stage(nc, keep, t, scratch)
        ffn_stage(nc, keep, t, scratch, False, out)


def circuit_constants():
    bit = lambda i, w: i >> (WIRES - 1 - w) & 1

    def permuted(l):
        to = []
        for i in range(DIM):
            v = [bit(i, w) for w in range(WIRES)]
            for c in range(WIRES):
                if v[c]:
                    v[(c + l + 1) % WIRES] ^= 1
            to.append(sum(x << (WIRES - 1 - w) for w, x in enumerate(v)))
        return to

    to1, to2 = permuted(0), permuted(1)
    from1 = [to1.index(k) for k in range(DIM)]
    entry = {(0, 0): np.pi / 2, (0, 1): np.pi, (1, 0): 0.0, (1, 1): np.pi / 2}
    voff = np.zeros((DIM, LAYERS * WIRES * DIM + 4), np.float64)
    vcoef = np.zeros((DIM, 2, LAYERS * WIRES * 3), np.float64)
    for k in range(DIM):
        for w in range(WIRES):
            for i in range(DIM):
                voff[k, w * DIM + i] = entry[bit(from1[k], w), bit(i, w)]
                voff[k, (WIRES + w) * DIM + i] = entry[bit(i, w), bit(k, w)]
            vcoef[k, 0, w * 3 + 2] = 0.5 if bit(from1[k], w) else -0.5
            vcoef[k, 0, (WIRES + w) * 3] = 0.5 if bit(k, w) else -0.5
            vcoef[k, 1, w * 3] = 0.5 if bit(k, w) else -0.5
        n = LAYERS * WIRES * DIM
        ones = bin(k).count("1")
        voff[k, n:] = [0.0, np.pi / 2, -np.pi / 2 * ones, np.pi / 2 - np.pi / 2 * ones]
    sign = np.array([[1.0 - 2.0 * bit(to2[j], w) for j in range(DIM)] for w in range(WIRES)])
    return voff, vcoef, np.concatenate([sign, sign], axis=1)


def constants():
    voff, vcoef, zsign = circuit_constants()
    half = D // 2
    freqs = np.exp(np.arange(half) * (-np.log(10000.0) / (half - 1)))
    c = {"ident": np.eye(P), "freqs": freqs.reshape(2, P).T, "voff": voff, "vcoef": vcoef, "zsign": zsign}
    return {k: np.ascontiguousarray(v, dtype=np.float32) for k, v in c.items()}


_INS = ["x", "condB_vol", "itok_B_34_63", "fside_Bx16xSxS_0", "mask_Bx1xSxS_bk0"] + [
    f"L0_cond_{n}" for n in ("w1", "b1", "w2", "b2", "pd_w", "pd_b", "vqc_w", "pu_w", "pu_b", "q_scale", "ln_g", "ln_b")] + [
    f"L1_cond_{n}" for n in ("W_ada", "b_ada", "Wq", "bq", "Wk", "bk", "Wv", "bv", "Wo", "bo", "W1", "b1", "W2", "b2",
                             "g2", "beta2")]


def kernel(**inputs):
    import concourse.bacc as _bacc
    from concourse.bass_utils import run_bass_kernel_spmd as _run

    nc = _bacc.Bacc("TRN2", target_bir_lowering=False, num_devices=1)
    arrays, t, consts = {}, {}, {}
    for name in _INS:
        a = np.ascontiguousarray(inputs[name])
        arrays[f"in_{name}"] = a
        t[name] = nc.dram_tensor(f"in_{name}", a.shape, mybir.dt.from_np(a.dtype), kind="ExternalInput").ap()
    for name, a in constants().items():
        arrays[f"const_{name}"] = a
        consts[name] = nc.dram_tensor(f"const_{name}", a.shape, mybir.dt.from_np(a.dtype), kind="ExternalInput").ap()
    out = nc.dram_tensor("out", (B, S, D), F32, kind="ExternalOutput").ap()
    build(nc, t, consts, out)
    r = _run(nc, [arrays], core_ids=[0])
    return r.results[0]["out"]
```

```python
from contextlib import ExitStack

import numpy as np

import concourse.bass as bass
from concourse import mybir

F32 = mybir.dt.float32
F32R = mybir.dt.float32r
BF16 = mybir.dt.bfloat16
U8 = mybir.dt.uint8
I32 = mybir.dt.int32
ALU = mybir.AluOpType
ACT = mybir.ActivationFunctionType
AX = mybir.AxisListType

P = 128
B, S, D, F, H = 8, 512, 512, 2048, 16
HD = D // H
KT = D // P
TT = S // P
FT = F // P
WIRES, LAYERS = 4, 2
DIM = 2 ** WIRES
EPS = 1e-5
PI = float(np.pi)
INV_2PI = float(1 / (2 * np.pi))
ROUND = 1.5 * 2.0 ** 23
C1 = 6.28125
C2 = float(np.floor((2 * np.pi - C1) * 2 ** 20) / 2 ** 20)
C3 = float(2 * np.pi - C1 - C2)
PI_BELOW = 3.1415925
MASKED = -3e38
Q_SCALE = float(HD) ** -0.5

DENSE = ["w1", "b1", "w2", "b2"]


def each_batch(eng, body):
    body(0, True, False)
    with eng.Fori(1, B - 1) as b:
        body(b, False, False)
    body(B - 1, False, True)


def rows(t):
    return t.rearrange("(t p) n -> p t n", p=P)


def wait_apart(eng, passed, *waits):
    for sem, value in waits:
        eng.wait_ge(sem, value)
    eng.sem_inc(passed, 1)


class Chain:

    def __init__(self, eng, sem):
        self.eng, self.sem, self.base, self.n = eng, sem, 0, 0

    def at(self, base):
        self.base, self.n = base, 0

    def step(self, ins):
        self.n += 1
        ins.then_inc(self.sem, 1)

    def wait(self):
        self.eng.wait_ge(self.sem, self.base + self.n)

    def __call__(self, ins):
        self.step(ins)
        self.wait()


class Setup:

    LOADS = 9

    def __init__(self, nc, ctx, keep, t, consts, scratch, banks, w_pass, ada_row, ampt, prob):
        sb = lambda n, s, d=F32: ctx.enter_context(nc.sbuf_tensor(f"su_{n}", s, d))
        sem = lambda n: ctx.enter_context(nc.semaphore(f"su_{n}"))
        NV = LAYERS * WIRES * DIM + 4
        self.nc, self.keep, self.t, self.consts, self.scratch = nc, keep, t, consts, scratch
        self.banks, self.wada, self.puw = banks, w_pass, ampt[0:WIRES, :]
        self.ada = ada_row[0:B, :, :]
        self.steps_i, self.steps = sb("steps_i", [P, B], I32), sb("steps", [P, B])
        self.freq = sb("freq", [P, 2])
        self.ang, self.off, self.turns, self.sine, self.sig = (
            sb(f"emb_{n}", [P, KT, B]) for n in ("ang", "off", "turns", "sine", "sig"))
        self.vol, self.qs = sb("vol", [P, B]), sb("qs", [P, 1])
        self.vw = sb("vw", [DIM, LAYERS * WIRES * 3])
        self.vcoef, self.vprod = sb("vcoef", [DIM, 2, LAYERS * WIRES * 3]), sb("vprod", [DIM, 2, LAYERS * WIRES * 3])
        self.voff, self.vang, self.vturn = (prob[0:DIM, i * NV:(i + 1) * NV] for i in range(3))
        self.vsin = self.vturn
        self.pair, self.gates = sb("vpair", [DIM, LAYERS, 2, DIM]), sb("vgates", [DIM, LAYERS, DIM])
        self.rot2, self.part = sb("vrot2", [DIM, 2, DIM]), sb("vpart", [DIM, 2, DIM])
        self.zs = sb("zs", [WIRES, 2 * DIM])
        self.s_in, self.ident_in, self.wada_in, self.bada_in, self.chain, self.reduced, self.sines, self.sigmoid, \
            self.silu, self.gates_set, self.circuit_mm, self.circuit_set, self.ada_mm, self.ada_rows, self.stored = map(sem, (
                "in", "ident_in", "wada_in", "bada_in", "chain", "reduced", "sines", "sigmoid",
                "silu", "gates_set", "circuit_mm", "circuit_set", "ada_mm", "ada_rows", "stored"))

    def load_ident(self, sp):
        sp.dma_start(self.keep.ident[:, :], self.consts["ident"]).then_inc(self.ident_in, 16)

    def load(self, sp):
        t, c = self.t, self.consts
        loads = [
            (self.freq[:, :], c["freqs"]), (self.voff[:, :], c["voff"]), (self.vcoef[:, :, :], c["vcoef"]),
            (self.zs[:, :], c["zsign"]),
            (self.steps_i[:, :], t["itok_B_34_63"].partition_broadcast(P)),
            (self.vol[:, :], t["condB_vol"].partition_broadcast(P)),
            (self.qs[:, :], t["L0_cond_q_scale"].partition_broadcast(P)),
            (self.vw[:, :], t["L0_cond_vqc_w"].rearrange("l w a -> (l w a)").partition_broadcast(DIM)),
            (self.puw, t["L0_cond_pu_w"]),
        ]
        assert len(loads) == self.LOADS
        for dst, src in loads:
            sp.dma_start(dst, src).then_inc(self.s_in, 16)
        sp.dma_start(self.ada.rearrange("p a n -> p (a n)"), t["L1_cond_b_ada"].partition_broadcast(B)).then_inc(self.bada_in, 16)

    def load_wada(self, sp, half):
        if half == 1:
            sp.wait_ge(self.ada_mm, 1)
        src = self.t["L1_cond_W_ada"].rearrange("(k p) n -> p k n", p=P)[:, :, half * D:(half + 1) * D]
        sp.dma_start(self.wada[:, :, :], src).then_inc(self.wada_in, 16)

    def store_rows(self, sp):
        sp.wait_ge(self.ada_rows, 2)
        sp.dma_start(self.scratch["ada"], self.ada.rearrange("p a n -> p (a n)")).then_inc(self.stored, 16)
        sp.wait_ge(self.stored, 16)

    def reduce_angle(self, link, ang, off, turns):
        nc = self.nc
        link(nc.vector.tensor_tensor(turns, ang, off, ALU.add))
        link(nc.vector.tensor_scalar(turns, turns, INV_2PI, None, ALU.mult))
        link(nc.vector.tensor_scalar(turns, turns, ROUND, None, ALU.add))
        link(nc.vector.tensor_scalar(turns, turns, ROUND, None, ALU.subtract))
        for c in (C1, C2, C3):
            link(nc.vector.scalar_tensor_tensor(ang, turns, -c, ang, ALU.mult, ALU.add))
        link(nc.vector.tensor_tensor(ang, ang, off, ALU.add))
        return nc.vector.tensor_scalar(ang, ang, PI_BELOW, -PI_BELOW, ALU.min, ALU.max)

    def choices(self, dve, link):
        nc, keep = self.nc, self.keep
        dve.wait_ge(self.s_in, 16 * self.LOADS)
        link(nc.vector.tensor_scalar(keep.take_q[:, :], self.vol[:, :], 0.5, None, ALU.is_gt))
        link(nc.vector.tensor_scalar(keep.take_f[:, :], keep.take_q[:, :], -1.0, 1.0, ALU.mult, ALU.add))
        link(nc.vector.scalar_tensor_tensor(self.qs[:, :], self.qs[:, :], -1.0, self.qs[:, :], ALU.mult, ALU.max))
        link(nc.vector.tensor_scalar(keep.q_factor[:, :], keep.take_q[:, :], self.qs[:, 0:1], None, ALU.mult))

    def embedding_angles(self, dve, link):
        nc = self.nc
        link(nc.vector.tensor_copy(self.steps[:, :], self.steps_i[:, :]))
        link(nc.vector.tensor_scalar(self.steps[:, :], self.steps[:, :], 4000.0 / 100.0, None, ALU.mult))
        for k in range(KT):
            link.step(nc.vector.tensor_scalar(self.ang[:, k, :], self.steps[:, :], self.freq[:, k % 2:k % 2 + 1], None, ALU.mult))
        link.step(nc.vector.memset(self.off[:, 0:2, :], 0.0))
        link(nc.vector.memset(self.off[:, 2:4, :], PI / 2))
        self.reduce_angle(link, self.ang[:, :, :], self.off[:, :, :], self.turns[:, :, :]).then_inc(self.reduced, 1)

    def circuit_phases(self, dve, link):
        nc, vang = self.nc, self.vang
        n = LAYERS * WIRES * DIM
        theta = self.vw[:, :].rearrange("p (g a) -> p g a", a=3)[:, :, 1:2].to_broadcast([DIM, LAYERS * WIRES, DIM])
        link.step(nc.vector.tensor_scalar(vang[:, 0:n].rearrange("p (g b) -> p g b", b=DIM), theta, 0.5, None, ALU.mult))
        for c in range(2):
            link(nc.vector.tensor_tensor(self.vprod[:, c, :], self.vcoef[:, c, :], self.vw[:, :], ALU.mult))
        for c in range(2):
            for d in range(2):
                link(nc.vector.tensor_reduce(vang[:, n + 2 * c + d:n + 2 * c + d + 1], self.vprod[:, c, :], AX.X, ALU.add))
        self.reduce_angle(link, vang[:, :], self.voff[:, :], self.vturn[:, :]).then_inc(self.reduced, 1)

    def gate_products(self, dve, link):
        nc = self.nc
        n = LAYERS * WIRES * DIM
        dve.wait_ge(self.sines, 2)
        g = self.vsin[:, 0:n].rearrange("p (l u v b) -> p l u v b", l=LAYERS, u=2, v=2)
        for l in range(LAYERS):
            link(nc.vector.tensor_tensor(self.pair[:, l, :, :], g[:, l, :, 0, :], g[:, l, :, 1, :], ALU.mult))
        link(nc.vector.tensor_tensor(self.gates[:, :, :], self.pair[:, :, 0, :], self.pair[:, :, 1, :], ALU.mult))
        for c in range(2):
            nc.vector.tensor_scalar(self.rot2[:, c, :], self.gates[:, 1, :], self.vsin[:, n + 1 - c:n + 2 - c], None, ALU.mult)\
                .then_inc(self.gates_set, 1)

    def embedding_silu(self, dve):
        dve.wait_ge(self.sigmoid, 1)
        self.nc.vector.tensor_tensor(self.sig[:, :, :], self.sig[:, :, :], self.sine[:, :, :], ALU.mult).then_inc(self.silu, 1)

    def circuit_out(self, dve, link):
        nc, keep, part = self.nc, self.keep, self.part
        n = LAYERS * WIRES * DIM
        dve.wait_ge(self.circuit_mm, 2)
        re, im = self.banks[1][0:DIM, 0:DIM], self.banks[1][0:DIM, DIM:2 * DIM]
        sin_b, cos_b = self.vsin[:, n + 2:n + 3], self.vsin[:, n + 3:n + 4]
        link.step(nc.vector.tensor_scalar(part[:, 0, :], im, sin_b, None, ALU.mult))
        link(nc.vector.tensor_scalar(part[:, 1, :], im, cos_b, None, ALU.mult))
        for column, phase, op in ((0, cos_b, ALU.subtract), (1, sin_b, ALU.add)):
            nc.vector.scalar_tensor_tensor(keep.circuit[:, column * DIM:(column + 1) * DIM], re, phase, part[:, column, :],
                                           ALU.mult, op).then_inc(self.circuit_set, 1)
        nc.vector.tensor_copy(keep.zpu[:, :], self.banks[0][0:2 * DIM, :]).then_inc(self.circuit_set, 1)

    def ada_out(self, dve, link, half):
        nc, ada = self.nc, self.ada
        dve.wait_ge(self.bada_in, 16)
        dve.wait_ge(self.ada_mm, half + 1)
        bank = self.banks[1 - half][0:B, :]
        if half == 0:
            link(nc.vector.tensor_tensor(ada[:, 0, :], bank, ada[:, 0, :], ALU.add))
            nc.vector.tensor_scalar(ada[:, 0, :], ada[:, 0, :], 1.0, None, ALU.add).then_inc(self.ada_rows, 1)
        else:
            nc.vector.tensor_tensor(ada[:, 1, :], bank, ada[:, 1, :], ALU.add).then_inc(self.ada_rows, 1)

    def take_sines(self, act):
        nc = self.nc
        act.wait_ge(self.reduced, 2)
        nc.scalar.activation(self.sine[:, :, :], self.ang[:, :, :], ACT.Sin).then_inc(self.sines, 1)
        nc.scalar.activation(self.vsin[:, :], self.vang[:, :], ACT.Sin).then_inc(self.sines, 1)

    def take_sigmoid(self, act):
        act.wait_ge(self.sines, 1)
        self.nc.scalar.activation(self.sig[:, :, :], self.sine[:, :, :], ACT.Sigmoid).then_inc(self.sigmoid, 1)

    def circuit_products(self, pe, p_out):
        nc = self.nc
        pe.wait_ge(self.gates_set, 2)
        pe.wait_ge(p_out, 1)
        nc.tensor.matmul(self.banks[1][0:DIM, 0:2 * DIM], self.gates[:, 0, :], self.rot2[:, :, :].rearrange("p c j -> p (c j)"),
                         start=True, stop=True).then_inc(self.circuit_mm, 1)
        nc.tensor.matmul(self.banks[0][0:2 * DIM, :], self.zs[:, :], self.puw, start=True, stop=True).then_inc(self.circuit_mm, 1)

    def ada_product(self, pe, half):
        pe.wait_ge(self.silu, 1)
        pe.wait_ge(self.wada_in, 16 * half + 16)
        for k in range(KT):
            mm = self.nc.tensor.matmul(self.banks[1 - half][0:B, :], self.sig[:, k, :], self.wada[:, k, :],
                                       start=k == 0, stop=k == KT - 1)
        mm.then_inc(self.ada_mm, 1)


def split_product(pe, out, pairs, last_stop=True):
    n = len(pairs)
    for i, (ah, al, bh, bl) in enumerate(pairs):
        nc_mm = pe.matmul(out, ah, bh, start=i == 0, stop=False)
        nc_mm = pe.matmul(out, al, bh, start=False, stop=False)
        nc_mm = pe.matmul(out, ah, bl, start=False, stop=i == n - 1)
    return nc_mm


def ffn_stage(nc, keep, t, table, scratch, l0, out):
    L = "L0" if l0 else "L1"
    name = (lambda n: f"L0_cond_{n}") if l0 else (lambda n: f"L1_cond_{n.replace('w', 'W')}")
    w1, b1, w2, b2 = (t[name(n)] for n in ("w1", "b1", "w2", "b2"))
    func = ACT.Gelu if l0 else ACT.Gelu_apprx_sigmoid
    x_src = t["x"] if l0 else scratch["x2"]
    with ExitStack() as ctx:
        sb = lambda n, s, d=F32: ctx.enter_context(nc.sbuf_tensor(f"{L}_{n}", s, d))
        ps = lambda n: ctx.enter_context(nc.psum_tensor(f"{L}_{n}", [P, 512], F32))
        sem = lambda n: ctx.enter_context(nc.semaphore(f"{L}_{n}"))
        w1h, w1l = sb("w1h", [P, KT, F], F32R), sb("w1l", [P, KT, F], F32R)
        w2h, w2l = sb("w2h", [P, FT, D], F32R), sb("w2l", [P, FT, D], F32R)
        xin = sb("xin", [P, TT, D])
        xres = sb("xres", [P, TT, D])
        w_pass = sb("w_pass", [P, TT, D])
        xth, xtl = sb("xth", [P, KT, S], F32R), sb("xtl", [P, KT, S], F32R)
        hid = [sb(f"hid{i}", [P, S]) for i in range(2)]
        hh = [sb(f"hh{i}", [P, S], F32R) for i in range(2)]
        hl = [sb(f"hl{i}", [P, S], F32R) for i in range(2)]
        b1c = sb("b1c", [P, FT])
        b2r = sb("b2r", [P, D])
        gain, offset = sb("gain", [P, D]), sb("offset", [P, D])
        stat, mv = sb("stat", [P, TT, 6]), sb("mv", [P, TT, 2])
        power, rstd, shift = sb("power", [P, TT]), sb("rstd", [P, TT]), sb("shift", [P, TT])
        turn = [ps(f"turn{i}") for i in range(2)]
        acc = [ps(f"acc{i}") for i in range(TT)]

        consts_in, w_hi, w_lo, power_set = map(sem, ("consts_in", "w_hi", "w_lo", "power_set"))
        w_in = [sem(f"w_in{i}") for i in range(2)]
        x_in, xres_in, stored = map(sem, ("x_in", "xres_in", "stored"))
        turned, xt_hi, xt_lo = map(sem, ("turned", "xt_hi", "xt_lo"))
        h_mm, h_act, h_hi, h_lo, y_mm, y_out = map(sem, ("h_mm", "h_act", "h_hi", "h_lo", "y_mm", "y_out"))
        row_added, n_var, n_rstd, n_shift, normed = map(sem, ("row_added", "n_var", "n_rstd", "n_shift", "normed"))
        gained, affine_done, dve_chain = map(sem, ("gained", "affine_done", "dve_chain"))
        passed_dve, passed_pe = sem("passed_dve"), sem("passed_pe")
        if l0:
            pub_row, row = sb("pub_row", [P, D]), sb("row", [P, D])
            ada_row = sb("ada_row", [P, 2, D])
            pdw = sb("pdw", [P, KT, WIRES])
            pd = sb("pd", [P, KT, P], F32R)
            pd_zero = row[:, :].rearrange("p (k n) -> p k n", k=KT)
            pdb = sb("pdb", [P, WIRES])
            pt = sb("pt", [2 * WIRES, S])
            angle = sb("angle", [P, TT, WIRES])
            cos_sin = sb("cos_sin", [P, 2, TT, WIRES])
            pairs = sb("pairs", [P, 2, TT, 4])
            amp = sb("amp", [P, TT, DIM])
            ampt = sb("ampt", [DIM, S])
            prob = sb("prob", [2 * DIM, S])
            misc = [ps(f"misc{i}") for i in range(2)]
            setup = Setup(nc, ctx, keep, t, table, scratch, misc, w_pass, ada_row, ampt, prob)
            pd_set, p_mm, pt_out, p_turned, p_out, p_sig, halved, cs_out, amp_out, amp_turned, ampt_out, state_mm, \
                prob_out, up_mm, up_added, row_set, ada_in = map(sem, (
                    "pd_set", "p_mm", "pt_out", "p_turned", "p_out", "p_sig", "halved", "cs_out", "amp_out", "amp_turned",
                    "ampt_out", "state_mm", "prob_out", "up_mm", "up_added", "row_set", "ada_in"))
        across = lambda n: t[n].partition_broadcast(P)
        consts = [(b1c[:, :], b1.rearrange("(m p) -> p m", p=P)), (b2r[:, :], b2.partition_broadcast(P)),
                  (gain[:, :], across("L0_cond_ln_g" if l0 else "L1_cond_g2")),
                  (offset[:, :], across("L0_cond_ln_b" if l0 else "L1_cond_beta2"))]
        if l0:
            consts += [(pub_row[:, :], across("L0_cond_pu_b")), (pdb[:, :], across("L0_cond_pd_b")),
                       (pdw[:, :, :], t["L0_cond_pd_w"].rearrange("(k p) n -> p k n", p=P))]
        passing = [w_pass, xres]
        chunks = []
        for m in range(0, FT, TT):
            cut = slice(m * P, (m + TT) * P)
            chunks.append((w1.rearrange("(k p) n -> p k n", p=P)[:, :, cut], w1h[:, :, cut], w1l[:, :, cut]))
            chunks.append((w2[cut, :].rearrange("(m p) n -> p m n", p=P), w2h[:, m:m + TT, :], w2l[:, m:m + TT, :]))
        CH = len(chunks)
        ALONE = 0 if l0 else 1
        block = ctx.enter_context(nc.Block())

        @block.sync
        def _(sp):
            if l0:
                setup.load_ident(sp)
            sp.dma_start(xin[:, :, :], rows(x_src[0])).then_inc(x_in, 16)
            sp.dma_start(passing[0][:, :, :], chunks[0][0]).then_inc(w_in[0], 16)
            for dst, src in consts:
                sp.dma_start(dst, src).then_inc(consts_in, 16)
            for c, (src, _, _) in enumerate(chunks[1:], 1):
                if c >= 2:
                    sp.wait_ge(w_lo, c - 1)
                sp.dma_start(passing[c % 2][:, :, :], src).then_inc(w_in[c % 2], 16)
                if l0 and c == 1:
                    setup.load(sp)
            if l0:
                sp.wait_ge(w_lo, CH - 1)
                setup.load_wada(sp, 0)

            def body(b, first, last):
                if not last:
                    sp.wait_ge(turned, b * KT + KT)
                    sp.dma_start(xin[:, :, :], rows(x_src[b + 1])).then_inc(x_in, 16)
                if not first:
                    store(b - 1)
                    sp.wait_ge(stored, b * 16)
                else:
                    sp.wait_ge(w_lo, CH)
                sp.dma_start(xres[:, :, :], rows(x_src[b])).then_inc(xres_in, 16)
                if l0 and first:
                    setup.load_wada(sp, 1)
                    setup.store_rows(sp)
                if l0:
                    sp.dma_start(ada_row[:, :, :].rearrange("p a n -> p (a n)"),
                                 scratch["ada"][b].partition_broadcast(P)).then_inc(ada_in, 16)

            def wait_tiles(b, n):
                if l0:
                    sp.wait_ge(affine_done, b * 2 * TT + TT + n)
                else:
                    sp.wait_ge(y_out, b * TT + n)

            def store(b):
                wait_tiles(b, TT)
                sp.dma_start(rows(out[b]), xres[:, :, :]).then_inc(stored, 16)

            each_batch(sp, body)
            for i in range(TT):
                wait_tiles(B - 1, i + 1)
                sp.dma_start(rows(out[B - 1])[:, i, :], xres[:, i, :]).then_inc(stored, 16)
            sp.wait_ge(stored, 16 * (B - 1 + TT))

        @block.gpsimd
        def _(pool):
            nc.gpsimd.memset(power[:, :], -0.5).then_inc(power_set, 1)
            pool.wait_ge(power_set, 1)
            pool.wait_ge(consts_in, 16 * len(consts))

            def norm_rstd(n):
                pool.wait_ge(n_var, n + 1)
                nc.gpsimd.tensor_tensor(rstd[:, :], mv[:, :, 1], power[:, :], ALU.pow).then_inc(n_rstd, 1)

            def norm(buf, n, g, o):
                norm_rstd(n)
                n = n - ALONE
                for i in range(TT):
                    pool.wait_ge(normed, n * TT + i + 1)
                    nc.gpsimd.tensor_tensor(buf[:, i, :], buf[:, i, :], g, ALU.mult).then_inc(gained, 1)
                    pool.wait_ge(gained, n * TT + i + 1)
                    nc.gpsimd.tensor_tensor(buf[:, i, :], buf[:, i, :], o, ALU.add).then_inc(affine_done, 1)

            def tail(b):
                norm(xres, 2 * b, gain[:, :], offset[:, :])
                pool.wait_ge(ada_in, b * 16 + 16)
                norm(xres, 2 * b + 1, ada_row[:, 0, :], ada_row[:, 1, :])

            def body(b, first, last):
                if l0 and not first:
                    tail(b - 1)
                pool.wait_ge(xres_in, b * 16 + 16)
                if l0:
                    pool.wait_ge(row_set, b + 1)
                for i in range(TT):
                    nc.gpsimd.tensor_tensor(xres[:, i, :], xres[:, i, :], (row if l0 else b2r)[:, :], ALU.add)\
                        .then_inc(row_added, 1)
                if not l0 and not last:
                    norm(xin, b + 1, gain[:, :], offset[:, :])

            if not l0:
                norm_rstd(0)
            each_batch(pool, body)
            if l0:
                norm_rstd(2 * B - 2)
                norm_rstd(2 * B - 1)

        @block.scalar
        def _(act):
            def split_weights(c):
                act.wait_ge(w_in[c % 2], 16 * (c // 2 + 1))
                nc.scalar.activation(chunks[c][1], passing[c % 2][:, :, :], ACT.Copy).then_inc(w_hi, 1)

            def norm(buf, n):
                act.wait_ge(n_shift, n + 1 - ALONE)
                for i in range(TT):
                    nc.scalar.activation(buf[:, i, :], buf[:, i, :], ACT.Identity, bias=shift[:, i:i + 1],
                                         scale=rstd[:, i:i + 1]).then_inc(normed, 1)

            def turn_out(b):
                for k in range(KT):
                    act.wait_ge(turned, b * KT + k + 1)
                    nc.scalar.activation(xth[:, k, :], turn[k % 2][:, :], ACT.Copy).then_inc(xt_hi, 1)

            def body(b, first, last):
                if l0:
                    act.wait_ge(p_mm, b + 1)
                    nc.scalar.activation(pt[:, :], misc[0][0:2 * WIRES, :], ACT.Copy).then_inc(pt_out, 1)
                for m in range(FT):
                    act.wait_ge(h_mm, b * FT + m + 1)
                    if not (first and m < 2):
                        act.wait_ge(h_lo, b * FT + m - 1)
                    nc.scalar.activation(hid[m % 2][:, :], turn[m % 2][:, :], func, bias=b1c[:, m:m + 1]).then_inc(h_act, 1)
                    if first and m < CH - 2:
                        split_weights(m + 2)
                    if l0 and first and m == 1:
                        setup.take_sines(act)
                    if l0 and first and m == 5:
                        setup.take_sigmoid(act)
                    if l0 and not first and m == 3:
                        norm(xres, 2 * b - 2)
                    if l0 and not first and m == 7:
                        norm(xres, 2 * b - 1)
                    if l0 and m == 5:
                        act.wait_ge(p_out, b + 1)
                        nc.scalar.activation(angle[:, :, :], angle[:, :, :], ACT.Sigmoid).then_inc(p_sig, 1)
                    if l0 and m == 6:
                        act.wait_ge(halved, b + 1)
                        nc.scalar.activation(cos_sin[:, :, :, :], cos_sin[:, :, :, :], ACT.Sin).then_inc(cs_out, 1)
                    if l0 and m == 10:
                        act.wait_ge(amp_turned, b + 1)
                        nc.scalar.activation(ampt[:, :], misc[0][0:DIM, :], ACT.Copy).then_inc(ampt_out, 1)
                    if l0 and m == 11:
                        act.wait_ge(state_mm, b + 1)
                        nc.scalar.activation(prob[:, :], misc[1][0:2 * DIM, :], ACT.Square).then_inc(prob_out, 1)
                    if not l0 and not last and m == 6:
                        norm(xin, b + 1)
                if not last:
                    turn_out(b + 1)

            split_weights(0)
            turn_out(0)
            split_weights(1)
            each_batch(act, body)

        @block.vector
        def _(dve):
            link = Chain(dve, dve_chain)
            setup_link = Chain(dve, setup.chain) if l0 else None
            dve.wait_ge(consts_in, 16 * len(consts))
            if l0:
                link(nc.vector.memset(pd_zero[:, :, :], 0.0))
                link(nc.vector.tensor_copy(pd[:, :, :], pd_zero[:, :, :]))
                link(nc.vector.tensor_copy(pd[:, :, 0:WIRES], pdw[:, :, :]))
                nc.vector.tensor_tensor(pd[:, :, WIRES:2 * WIRES], pdw[:, :, :], pd[:, :, 0:WIRES].bitcast(F32),
                                        ALU.subtract).then_inc(pd_set, 1)

            def split_weights(c):
                _, hi, lo = chunks[c]
                dve.wait_ge(w_hi, c + 1)
                nc.vector.tensor_tensor(lo, passing[c % 2][:, :, :], hi.bitcast(F32), ALU.subtract).then_inc(w_lo, 1)

            def norm_stats(buf, n):
                for i in range(TT):
                    link.step(nc.vector.bn_stats(stat[:, i, :], buf[:, i, :]))
                wait_apart(dve, passed_dve, (dve_chain, link.base + link.n))
                for i in range(TT):
                    link.step(nc.vector.bn_aggr(mv[:, i, :], stat[:, i, :]))
                link.wait()
                nc.vector.tensor_scalar(mv[:, :, 1], mv[:, :, 1], EPS, None, ALU.add).then_inc(n_var, 1)

            def norm_shift(n):
                dve.wait_ge(n_rstd, n + 1)
                nc.vector.scalar_tensor_tensor(shift[:, :], mv[:, :, 0], -1.0, rstd[:, :], ALU.mult, ALU.mult)\
                    .then_inc(n_shift, 1)

            def norm_alone(buf, n, g, o, written):
                norm_stats(buf, n)
                for i in range(TT):
                    link.step(nc.vector.scalar_tensor_tensor(buf[:, i, :], buf[:, i, :], mv[:, i, 0:1], g,
                                                             ALU.subtract, ALU.mult))
                dve.wait_ge(n_rstd, n + 1)
                link.wait()
                for i in range(TT):
                    nc.vector.scalar_tensor_tensor(buf[:, i, :], buf[:, i, :], rstd[:, i:i + 1], o,
                                                   ALU.mult, ALU.add).then_inc(affine_done, 1)
                if not written:
                    dve.wait_ge(affine_done, n * TT + TT)

            def turn_out(b):
                for k in range(KT):
                    dve.wait_ge(xt_hi, b * KT + k + 1)
                    nc.vector.tensor_tensor(xtl[:, k, :], turn[k % 2][:, :], xth[:, k, :].bitcast(F32), ALU.subtract)\
                        .then_inc(xt_lo, 1)

            def circuit_row(b, first):
                if not first:
                    dve.wait_ge(row_added, b * TT)
                link(nc.vector.tensor_scalar(row[:, :], b2r[:, :], keep.take_f[:, bass.ds(b, 1)], None, ALU.mult))
                nc.vector.scalar_tensor_tensor(row[:, :], pub_row[:, :], keep.q_factor[:, bass.ds(b, 1)], row[:, :],
                                               ALU.mult, ALU.add).then_inc(row_set, 1)

            def circuit_inputs(b):
                dve.wait_ge(p_turned, b + 1)
                halves = misc[1][:, 0:TT * 2 * WIRES].rearrange("p (t a w) -> p t w a", t=TT, a=2)
                link(nc.vector.tensor_reduce(angle[:, :, :], halves, AX.X, ALU.add))
                link(nc.vector.tensor_tensor(angle[:, :, :], angle[:, :, :],
                                             pdb[:, :].unsqueeze(1).to_broadcast([P, TT, WIRES]), ALU.add))
                nc.vector.tensor_scalar(angle[:, :, :], angle[:, :, :], 10.0, -10.0, ALU.min, ALU.max).then_inc(p_out, 1)

            def circuit_angles(b):
                dve.wait_ge(p_sig, b + 1)
                link(nc.vector.tensor_scalar(cos_sin[:, 1, :, :], angle[:, :, :], PI, 0.5, ALU.mult, ALU.mult))
                nc.vector.tensor_scalar(cos_sin[:, 0, :, :], cos_sin[:, 1, :, :], -1.0, PI / 2, ALU.mult, ALU.add)\
                    .then_inc(halved, 1)

            def circuit_amplitudes(b):
                dve.wait_ge(cs_out, b + 1)
                for h in range(2):
                    for i in range(2):
                        one = cos_sin[:, i, :, 2 * h:2 * h + 1].to_broadcast([P, TT, 2])
                        two = cos_sin[:, :, :, 2 * h + 1].rearrange("p c t -> p t c")
                        link(nc.vector.tensor_tensor(pairs[:, h, :, 2 * i:2 * i + 2], one, two, ALU.mult))
                for i in range(4):
                    ins = nc.vector.tensor_tensor(amp[:, :, 4 * i:4 * i + 4],
                                                  pairs[:, 0, :, i:i + 1].to_broadcast([P, TT, 4]),
                                                  pairs[:, 1, :, :], ALU.mult)
                    ins.then_inc(amp_out, 1)

            def circuit_add(b, i):
                dve.wait_ge(up_mm, b * TT + i + 1)
                dve.wait_ge(row_added, b * TT + i + 1)
                nc.vector.scalar_tensor_tensor(xres[:, i, :], misc[i % 2][:, :], keep.q_factor[:, bass.ds(b, 1)],
                                               xres[:, i, :], ALU.mult, ALU.add).then_inc(up_added, 1)

            def setup_step(m):
                if m == 0:
                    setup.choices(dve, setup_link)
                    circuit_row(0, True)
                    setup.embedding_angles(dve, setup_link)
                if m == 1:
                    setup.circuit_phases(dve, setup_link)
                if m == 3:
                    setup.gate_products(dve, setup_link)
                if m == 6:
                    setup.embedding_silu(dve)
                if m == 7:
                    setup.circuit_out(dve, setup_link)
                if m == 9:
                    setup.ada_out(dve, setup_link, 0)
                if m == 11:
                    setup.ada_out(dve, setup_link, 1)

            def body(b, first, last):
                if l0:
                    links = 1 + 2 + 1 + 4 + (0 if first else 4 * TT)
                    link.at(ahead if first else ahead + 8 + (b - 1) * (8 + 4 * TT))
                else:
                    links = 0 if last else 2 * TT
                    link.at(ahead + b * 2 * TT)
                if l0 and not first:
                    circuit_row(b, first)
                for m in range(FT):
                    dve.wait_ge(h_act, b * FT + m + 1)
                    if not (first and m < 2):
                        dve.wait_ge(y_mm, b * FT + m - 1)
                    nc.vector.tensor_copy(hh[m % 2][:, :], hid[m % 2][:, :]).then_inc(h_hi, 1)
                    dve.wait_ge(h_hi, b * FT + m + 1)
                    nc.vector.tensor_tensor(hl[m % 2][:, :], hid[m % 2][:, :], hh[m % 2][:, :].bitcast(F32), ALU.subtract)\
                        .then_inc(h_lo, 1)
                    if first and m < CH - 2:
                        split_weights(m + 2)
                    if l0 and first:
                        setup_step(m)
                    if l0 and not first:
                        if m == 0:
                            dve.wait_ge(y_out, b * TT)
                            norm_stats(xres, 2 * b - 2)
                        if m == 2:
                            norm_shift(2 * b - 2)
                        if m == 5:
                            dve.wait_ge(affine_done, b * 2 * TT - TT)
                            norm_stats(xres, 2 * b - 1)
                        if m == 6:
                            norm_shift(2 * b - 1)
                    if l0:
                        if m == 3:
                            circuit_inputs(b)
                        if m == 5:
                            circuit_angles(b)
                        if m == 7:
                            circuit_amplitudes(b)
                        if m >= 12:
                            circuit_add(b, m - 12)
                    if not l0 and not last:
                        if m == 3:
                            dve.wait_ge(x_in, b * 16 + 32)
                            norm_stats(xin, b + 1)
                        if m == 5:
                            norm_shift(b + 1)
                if not last:
                    turn_out(b + 1)
                dve.wait_ge(y_mm, b * FT + FT)
                for i in range(TT):
                    if l0:
                        dve.wait_ge(up_added, b * TT + i + 1)
                        nc.vector.scalar_tensor_tensor(xres[:, i, :], acc[i][:, :], keep.take_f[:, bass.ds(b, 1)],
                                                       xres[:, i, :], ALU.mult, ALU.add).then_inc(y_out, 1)
                    else:
                        dve.wait_ge(row_added, b * TT + i + 1)
                        nc.vector.tensor_tensor(xres[:, i, :], acc[i][:, :], xres[:, i, :], ALU.add).then_inc(y_out, 1)
                assert link.n == links, (link.n, links)

            if not l0:
                dve.wait_ge(x_in, 16)
                norm_alone(xin, 0, gain[:, :], offset[:, :], True)
            ahead = link.n
            split_weights(0)
            turn_out(0)
            split_weights(1)
            each_batch(dve, body)
            if l0:
                link.at(ahead + 8 + (B - 1) * (8 + 4 * TT))
                dve.wait_ge(y_out, B * TT)
                norm_alone(xres, 2 * B - 2, gain[:, :], offset[:, :], False)
                dve.wait_ge(ada_in, B * 16)
                norm_alone(xres, 2 * B - 1, ada_row[:, 0, :], ada_row[:, 1, :], True)

        @block.tensor
        def _(pe):
            def turn_in(b, k, ahead):
                if k == 0:
                    if l0:
                        pe.wait_ge(x_in, b * 16 + 16)
                    else:
                        pe.wait_ge(affine_done, b * TT + TT)
                if ahead and k < 2:
                    pe.wait_ge(h_act, b * FT - 1 + k)
                if k >= 2:
                    pe.wait_ge(xt_lo, b * KT + k - 1)
                for i in range(TT):
                    mm = pe.transpose(turn[k % 2][:, i * P:(i + 1) * P], xin[:, i, k * P:(k + 1) * P], keep.ident[:, :])
                mm.then_inc(turned, 1)

            def up(b, m, first):
                if first and m % TT == 0:
                    pe.wait_ge(w_lo, m // TT * 2 + 1)
                if m >= 2:
                    pe.wait_ge(h_act, b * FT + m - 1)
                cut = slice(m * P, (m + 1) * P)
                split_product(pe, turn[m % 2][:, :], [(w1h[:, k, cut], w1l[:, k, cut], xth[:, k, :], xtl[:, k, :])
                                                      for k in range(KT)]).then_inc(h_mm, 1)

            def down(b, m, first):
                if first and m % TT == 0:
                    pe.wait_ge(w_lo, m // TT * 2 + 2)
                pe.wait_ge(h_lo, b * FT + m + 1)
                if m == 0 and not first:
                    pe.wait_ge(y_out, b * TT)
                for i in range(TT):
                    cut = slice(i * P, (i + 1) * P)
                    pe.matmul(acc[i][:, :], hh[m % 2][:, cut], w2h[:, m, :], start=m == 0, stop=False)
                    pe.matmul(acc[i][:, :], hl[m % 2][:, cut], w2h[:, m, :], start=False, stop=False)
                    mm = pe.matmul(acc[i][:, :], hh[m % 2][:, cut], w2l[:, m, :], start=False, stop=m == FT - 1)
                mm.then_inc(y_mm, 1)

            def circuit(b, m, first):
                if m == 2:
                    if not first:
                        pe.wait_ge(up_added, b * TT)
                    wait_apart(pe, passed_pe, (pt_out, b + 1))
                    for i in range(TT):
                        mm = pe.transpose(misc[1][:, i * 2 * WIRES:(i + 1) * 2 * WIRES], pt[:, i * P:(i + 1) * P],
                                          keep.ident[0:2 * WIRES, 0:2 * WIRES])
                    mm.then_inc(p_turned, 1)
                if m == 9:
                    pe.wait_ge(amp_out, b * 4 + 4)
                    for i in range(TT):
                        mm = pe.transpose(misc[0][0:DIM, i * P:(i + 1) * P], amp[:, i, :], keep.ident[:, :])
                    mm.then_inc(amp_turned, 1)
                if m == 11:
                    wait_apart(pe, passed_pe, (ampt_out, b + 1))
                    pe.matmul(misc[1][0:2 * DIM, :], keep.circuit[:, :], ampt[:, :], start=True, stop=True)\
                        .then_inc(state_mm, 1)
                if m >= 12:
                    i = m - 12
                    if i == 0:
                        pe.wait_ge(prob_out, b + 1)
                    if i >= 2:
                        pe.wait_ge(up_added, b * TT + i - 1)
                    pe.matmul(misc[i % 2][:, :], prob[:, i * P:(i + 1) * P], keep.zpu[:, :], start=True, stop=True)\
                        .then_inc(up_mm, 1)

            def setup_step(m):
                if m == 6:
                    setup.circuit_products(pe, p_out)
                if m == 8:
                    pe.wait_ge(setup.circuit_set, 3)
                    setup.ada_product(pe, 0)
                if m == 10:
                    pe.wait_ge(setup.ada_rows, 1)
                if m == 11:
                    setup.ada_product(pe, 1)
                    pe.wait_ge(setup.ada_rows, 2)

            def body(b, first, last):
                pe.wait_ge(xt_lo, b * KT + KT)
                if l0:
                    if first:
                        pe.wait_ge(pd_set, 1)
                    else:
                        pe.wait_ge(up_added, b * TT)
                    for k in range(KT):
                        pe.matmul(misc[0][:, :], pd[:, k, :], xth[:, k, :], start=k == 0, stop=False)
                        mm = pe.matmul(misc[0][:, :], pd[:, k, :], xtl[:, k, :], start=False, stop=k == KT - 1)
                    mm.then_inc(p_mm, 1)
                for m in range(FT):
                    up(b, m, first)
                    if m >= 2:
                        down(b, m - 2, first)
                    if l0:
                        circuit(b, m, first)
                    if l0 and first:
                        setup_step(m)
                for half in range(2):
                    if not last:
                        turn_in(b + 1, 2 * half, True)
                        turn_in(b + 1, 2 * half + 1, True)
                    down(b, FT - 2 + half, first)

            if l0:
                pe.wait_ge(setup.ident_in, 16)
            for k in range(KT):
                turn_in(0, k, False)
            each_batch(pe, body)


def attention_stage(nc, keep, t, scratch):
    UNITS = H * TT
    SLOTS = 8
    IT_Q, IT_K, IT_V, IT_L = (TT * i for i in range(4))
    LATE = [("context", 0), ("context", 1), ("x", 0), ("context", 2), ("context", 3), ("x", 1),
            ("output", 0), ("x", 2), ("output", 1), ("x", 3), ("output", 2), ("output", 3)]
    ITEMS = IT_L + len(LATE)
    HIS = ITEMS - TT
    VB = TT * H
    VW = 2 * HD + 2
    ORDER = [4 * (pair // 4 * 2 + i) + pair % 4 for pair in range(H // 2) for i in range(2)]
    PAIR = 2 * TT
    with ExitStack() as ctx:
        sb = lambda n, s, d=F32: ctx.enter_context(nc.sbuf_tensor(f"at_{n}", s, d))
        ps = lambda n: ctx.enter_context(nc.psum_tensor(f"at_{n}", [P, 512], F32))
        sem = lambda n: ctx.enter_context(nc.semaphore(f"at_{n}"))
        weight = {n: (sb(f"w{n}h", [P, KT, D], F32R), sb(f"w{n}l", [P, KT, D], F32R)) for n in "qkvo"}
        context = sb("context", [P, TT, D])
        qk = sb("qk", [P, 4, KT, S])
        QH, KH, QL, KL = range(4)
        ahead_x, xres = qk[:, QH:KH + 1, 0:2, :], qk[:, QL:KL + 1, 0:2, :]
        x_tile = lambda buf, i: buf[:, i // 2, i % 2, :]
        qk_tile = lambda k: (k + 2) % KT
        flat = [sb(f"flat{i}", [P, S]) for i in range(2)]
        stack = [sb(f"stack{i}", [P, 2, 2, S], F32R) for i in range(2)]
        v = sb("v", [P, VB * VW + P - VW], F32R)
        v_tiles = v[:, 0:VB * VW].rearrange("p (t h c) -> p t h c", t=TT, c=VW)
        bias = sb("bias", [P, SLOTS, S])
        pt_hi = [sb(f"pt_hi{i}", [P, KT, S], F32R) for i in range(2)]
        pt_lo = [sb(f"pt_lo{i}", [P, KT, S], F32R) for i in range(2)]
        ct, xt = (pt_hi[0], pt_lo[0]), (pt_hi[1], pt_lo[1])
        ctx_flat = sb("ctx_flat", [P, S])
        head_sum = sb("head_sum", [P, TT, HD])
        inv_sum = sb("inv_sum", [P, TT])
        mask8 = sb("mask8", [P, TT, S], U8)
        mask = sb("mask", [P, TT, S], BF16)
        neg_top = sb("neg_top", [P, SLOTS])
        bqc, bkc = sb("bqc", [P, KT]), sb("bkc", [P, KT])
        bvr, bor = sb("bvr", [P, D]), sb("bor", [P, D])
        ones = sb("ones", [P, P])
        score = [ps(f"score{i}") for i in range(3)]
        turn = [ps(f"turn{i}") for i in range(3)]
        head_ps, head_turn = ps("head"), ps("head_turn")

        def late(i):
            return LATE[i - IT_L] if i >= IT_L else ("x", i % TT)

        def is_turn(i):
            return i < IT_Q or i >= IT_L and late(i)[0] != "output"

        def before(i):
            return [j for j in range(-TT, i) if is_turn(j)][-2]

        def item_bank(i):
            if is_turn(i):
                return score[sum(is_turn(j) for j in range(IT_L if i >= IT_L else -TT, i)) % 2]
            return (turn + [score[2] if i >= IT_L else head_ps])[late(i)[1] if i >= IT_L else i % TT]

        def lates(last):
            return [i for i in range(IT_L, ITEMS) if not last or late(i)[0] != "x"]

        consts_in, w_hi, w_lo, ones_set = map(sem, ("consts_in", "w_hi", "w_lo", "ones_set"))
        w_in = [sem(f"w_in{i}") for i in range(2)]
        x_in, xres_in, stored, mask_in, mask_set = map(sem, ("x_in", "xres_in", "stored", "mask_in", "mask_set"))
        item_mm, item_flat, item_hi, item_out, res_ready = map(sem, ("item_mm", "item_flat", "item_hi", "item_out", "res_ready"))
        bias_in = [sem(f"bias_in{i}") for i in range(SLOTS // 2)]
        stack_in = [sem(f"stack_in{i}") for i in range(2)]
        masked, score_mm, scored, exped, turned, p_hi, p_lo = map(sem, (
            "masked", "score_mm", "scored", "exped", "turned", "p_hi", "p_lo"))
        head_mm, head_flat, head_turned, head_summed, head_out, dve_chain = map(sem, (
            "head_mm", "head_flat", "head_turned", "head_summed", "head_out", "dve_chain"))
        inverted = sem("inverted")
        passed_dve, passed_sp = sem("passed_dve"), sem("passed_sp")
        consts = [(bqc[:, :], t["L1_cond_bq"].rearrange("(m p) -> p m", p=P)),
                  (bkc[:, :], t["L1_cond_bk"].rearrange("(m p) -> p m", p=P)),
                  (bvr[:, :], t["L1_cond_bv"].partition_broadcast(P)), (bor[:, :], t["L1_cond_bo"].partition_broadcast(P))]
        passing = [bias[:, 0:TT, :], bias[:, TT:SLOTS, :]]
        chunks = [(t[f"L1_cond_W{n}"].rearrange("(k p) n -> p k n", p=P), *weight[n]) for n in "qkvo"]
        bias_src = t["fside_Bx16xSxS_0"]

        def done(b, i, last):
            return TT + b * ITEMS + min(i + 1, IT_L) + sum(j <= i for j in lates(last))

        def done_hi(b, i, last):
            return TT + b * HIS + min(i + 1, IT_L) + sum(j <= i and is_turn(j) for j in lates(last))

        block = ctx.enter_context(nc.Block())

        @block.sync
        def _(sp):
            def load_x(buf, b, half, loaded):
                sp.dma_start(buf[:, half], rows(scratch["x1"][b])[:, 2 * half:2 * half + 2, :]).then_inc(loaded, 16)

            for dst, src in consts:
                sp.dma_start(dst, src).then_inc(consts_in, 16)
            load_x(ahead_x, 0, 0, x_in)
            load_x(ahead_x, 0, 1, x_in)
            sp.dma_start(mask8[:, :, :], rows(t["mask_Bx1xSxS_bk0"][0, 0])).then_inc(mask_in, 16)
            for c, (src, _, _) in enumerate(chunks):
                if c >= 2:
                    sp.wait_ge(w_lo, c - 1)
                sp.dma_start(passing[c % 2], src).then_inc(w_in[c % 2], 16)

            def load_bias(b, two, first):
                if two >= SLOTS // 2 or not first:
                    sp.wait_ge(turned, b * UNITS + 2 * two + 2 - SLOTS)
                elif two % 2 == 0:
                    sp.wait_ge(w_lo, 3 + two // 2)
                h, u = divmod(2 * two, TT)
                slot = 2 * two % SLOTS
                sp.dma_start(bias[:, slot:slot + 2, :],
                             bias_src[b, ORDER[h], u * P:(u + 2) * P, :].rearrange("(t p) n -> p t n", p=P))\
                    .then_inc(bias_in[two % (SLOTS // 2)], 16)

            def load_stack(b, pair):
                if pair == 0:
                    sp.wait_ge(item_out, done(b, IT_V - 1, False))
                if pair >= 2:
                    sp.wait_ge(score_mm, b * UNITS + (pair - 1) * PAIR)
                j, k = ORDER[2 * pair] % 4, ORDER[2 * pair] // 4
                src, to = slice(j * HD, (j + 1) * HD), stack[pair % 2][:, :, :, :].bitcast(F32)
                two = slice(k, k + 2)
                for block, dst, part in ((0, slice(0, 2), slice(QH, KH + 1)), (1, slice(0, 2), slice(QH, KL + 1, KL - QH)),
                                         (2, slice(0, 1), slice(QL, QL + 1)), (2, slice(1, 2), slice(KH, KH + 1)),
                                         (3, slice(0, 2), slice(QL, KL + 1))):
                    sp.dma_start(to[block * HD:(block + 1) * HD, dst, :, :], qk[src, part, two, :])\
                        .then_inc(stack_in[pair % 2], 16)

            def body(b, first, last):
                for two in range(SLOTS // 2):
                    load_bias(b, two, first)
                load_stack(b, 0)
                load_stack(b, 1)
                for two in range(SLOTS // 2, UNITS // 2):
                    load_bias(b, two, first)
                    if two % 4 == 2 and two // 4 + 1 < H // 2:
                        load_stack(b, two // 4 + 1)
                    if two == 20:
                        sp.wait_ge(score_mm, b * UNITS + UNITS // 2)
                    if two in (20, 21):
                        load_x(xres, b, two - 20, xres_in)
                    if not last and two in (24, 25):
                        load_x(ahead_x, b + 1, two - 24, x_in)
                if not last:
                    wait_apart(sp, passed_sp, (mask_set, b + 1))
                    sp.dma_start(mask8[:, :, :], rows(t["mask_Bx1xSxS_bk0"][b + 1, 0])).then_inc(mask_in, 16)
                for half in range(2):
                    sp.wait_ge(item_out, done(b, IT_L + LATE.index(("output", 2 * half + 1)), last))
                    sp.dma_start(rows(scratch["x2"][b])[:, 2 * half:2 * half + 2, :], xres[:, half]).then_inc(stored, 16)

            each_batch(sp, body)
            sp.wait_ge(stored, 32 * B)

        @block.gpsimd
        def _(pool):
            pool.wait_ge(consts_in, 16 * len(consts))

            def body(b, first, last):
                def head(h):
                    pool.wait_ge(head_summed, b * H + h + 1)
                    nc.gpsimd.tensor_tensor(context[:, :, ORDER[h] * HD:(ORDER[h] + 1) * HD], head_sum[:, :, :],
                                            inv_sum[:, :].unsqueeze(2).to_broadcast([P, TT, HD]), ALU.mult).then_inc(head_out, 1)

                pool.wait_ge(mask_set, b + 1)
                for n in range(UNITS):
                    if n % 2 == 0:
                        pair = n // 2
                        pool.wait_ge(bias_in[pair % 4], b * (UNITS // SLOTS * 16) + 16 * (pair // 4 + 1))
                    tile = bias[:, n % SLOTS, :]
                    nc.gpsimd.tensor_tensor(tile, tile, mask[:, n % TT, :], ALU.add).then_inc(masked, 1)
                    if n >= 14 and (n - 14) % TT == 0:
                        head((n - 14) // TT)
                pool.wait_ge(xres_in, b * 32 + 32)
                for i in range(TT):
                    nc.gpsimd.tensor_tensor(x_tile(xres, i), x_tile(xres, i), bor[:, :], ALU.add).then_inc(res_ready, 1)
                for h in range((UNITS - 15) // TT + 1, H):
                    head(h)

            each_batch(pool, body)

        @block.scalar
        def _(act):
            def split_weights(c):
                act.wait_ge(w_in[c % 2], 16 * (c // 2 + 1))
                nc.scalar.activation(chunks[c][1][:, :, :], passing[c % 2], ACT.Copy).then_inc(w_hi, 1)

            split_weights(0)
            split_weights(1)

            def transpose_hi(b, i, last):
                what, k = late(i)
                if i >= IT_L:
                    act.wait_ge(head_mm, b * H + (H - 1 if what == "context" else H))
                act.wait_ge(item_mm, done(b, i, last))
                hi = (ct if what == "context" else xt)[0]
                nc.scalar.activation(hi[:, k, :], item_bank(i)[:, :], ACT.Copy).then_inc(item_hi, 1)

            def body(b, first, last):
                def item(i):
                    k = i % TT
                    if first and i in (IT_Q, IT_K):
                        split_weights(2 + i // TT)
                    act.wait_ge(item_flat, b * 3 * TT + i + 1)
                    if i < IT_V:
                        if not first and qk_tile(k) < 2:
                            act.wait_ge(stored, b * 32)
                        dst, src = qk[:, QH if i < IT_K else KH, qk_tile(k), :].bitcast(F32R), flat[k % 2][:, :]
                    else:
                        dst = v_tiles[:, k, :, 0:HD]
                        src = flat[k % 2][:, :].rearrange("p (h d) -> p h d", h=H)
                    nc.scalar.activation(dst, src, ACT.Copy).then_inc(item_hi, 1)

                def exp(n):
                    act.wait_ge(scored, b * UNITS + n + 1)
                    tile = bias[:, n % SLOTS, :]
                    nc.scalar.activation(tile, tile, ACT.Exp, bias=neg_top[:, n % SLOTS:n % SLOTS + 1], scale=-1.0)\
                        .then_inc(exped, 1)

                def hi(n):
                    h, u = divmod(n, TT)
                    act.wait_ge(turned, b * UNITS + n + 1)
                    if h >= 2 and u == 0:
                        act.wait_ge(head_mm, b * H + h - 1)
                    nc.scalar.activation(pt_hi[h % 2][:, :, u * P:(u + 1) * P],
                                         turn[n % 3][:, :].rearrange("p (k q) -> p k q", k=KT), ACT.Copy).then_inc(p_hi, 1)

                def head(h):
                    act.wait_ge(head_mm, b * H + h + 1)
                    if h >= 1:
                        act.wait_ge(head_turned, b * H + h)
                    nc.scalar.activation(ctx_flat[:, :], head_ps[:, :], ACT.Copy).then_inc(head_flat, 1)

                for i in range(IT_L):
                    if i == IT_L - 1:
                        exp(0)
                        exp(1)
                    item(i)
                for n in range(2, UNITS):
                    exp(n)
                    if n >= 2:
                        hi(n - 2)
                    if n >= 9 and (n - 9) % TT == 0:
                        head((n - 9) // TT)
                hi(UNITS - 2)
                hi(UNITS - 1)
                head(H - 2)
                for n, i in enumerate(filter(is_turn, lates(last))):
                    if n == 2:
                        head(H - 1)
                    transpose_hi(b, i, last)

            for i in range(-TT, 0):
                transpose_hi(0, i, False)
            each_batch(act, body)

        @block.vector
        def _(dve):
            link = Chain(dve, dve_chain)
            dve.wait_ge(consts_in, 16 * len(consts))
            link(nc.vector.memset(ones[:, :], 1.0))
            link(nc.vector.tensor_copy(v_tiles[:, :, :, 2 * HD:VW].rearrange("p t h c -> p (t h) c"),
                                       ones[:, :].rearrange("p (b c) -> p b c", c=2)))
            link(nc.vector.tensor_copy(v[:, VB * VW:], ones[:, 0:P - VW]))
            ahead = link.n

            def split_weights(c):
                _, hi, lo = chunks[c]
                dve.wait_ge(w_hi, c + 1)
                nc.vector.tensor_tensor(lo[:, :, :], passing[c % 2], hi[:, :, :].bitcast(F32), ALU.subtract).then_inc(w_lo, 1)

            split_weights(0)
            split_weights(1)

            def transpose_lo(b, i, last):
                dve.wait_ge(item_hi, done_hi(b, i, last))
                what, k = late(i)
                hi, lo = ct if what == "context" else xt
                nc.vector.tensor_tensor(lo[:, k, :], item_bank(i)[:, :], hi[:, k, :].bitcast(F32), ALU.subtract)\
                    .then_inc(item_out, 1)

            def body(b, first, last):
                def item(i):
                    k = late(i)[1] if i >= IT_L else i % TT
                    bank = item_bank(i)
                    if first and i in (IT_Q, IT_K):
                        split_weights(2 + i // TT)
                    dve.wait_ge(item_mm, done(b, i, last))
                    if i >= IT_L:
                        dve.wait_ge(res_ready, b * TT + k + 1)
                        nc.vector.tensor_tensor(x_tile(xres, k), bank[:, :], x_tile(xres, k), ALU.add).then_inc(item_out, 1)
                        return
                    tile = flat[k % 2][:, :]
                    if i < IT_K:
                        m = qk_tile(k)
                        ins = nc.vector.tensor_scalar(tile, bank[:, :], bqc[:, m:m + 1], Q_SCALE, ALU.add, ALU.mult)
                    elif i < IT_V:
                        m = qk_tile(k)
                        ins = nc.vector.tensor_scalar(tile, bank[:, :], bkc[:, m:m + 1], None, ALU.add)
                    else:
                        ins = nc.vector.tensor_tensor(tile, bank[:, :], bvr[:, :], ALU.add)
                    ins.then_inc(item_flat, 1)
                    dve.wait_ge(item_hi, done_hi(b, i, last))
                    if i < IT_V:
                        hi, lo = (QH, QL) if i < IT_K else (KH, KL)
                        hi, lo = qk[:, hi, m, :], qk[:, lo, m, :].bitcast(F32R)
                    else:
                        hi, lo = v_tiles[:, k, :, 0:HD].bitcast(F32), v_tiles[:, k, :, HD:2 * HD]
                        tile = tile.rearrange("p (h d) -> p h d", h=H)
                    nc.vector.tensor_tensor(lo, tile, hi, ALU.subtract).then_inc(item_out, 1)

                def scores(n):
                    slot = n % SLOTS
                    wait_apart(dve, passed_dve, (masked, b * UNITS + n + 1), (score_mm, b * UNITS + n + 1))
                    nc.vector.tensor_tensor_reduce(bias[:, slot, :], score[n % 3][:, :], bias[:, slot, :], -1.0, -MASKED,
                                                   ALU.add, ALU.min, neg_top[:, slot:slot + 1]).then_inc(scored, 1)

                def lo(n):
                    h, u = divmod(n, TT)
                    dve.wait_ge(p_hi, b * UNITS + n + 1)
                    cut = slice(u * P, (u + 1) * P)
                    nc.vector.tensor_tensor(pt_lo[h % 2][:, :, cut], turn[n % 3][:, :].rearrange("p (k q) -> p k q", k=KT),
                                            pt_hi[h % 2][:, :, cut].bitcast(F32), ALU.subtract).then_inc(p_lo, 1)

                def head(h):
                    dve.wait_ge(head_turned, b * H + h + 1)
                    if not (first and h == 0):
                        dve.wait_ge(head_out, b * H + h)
                    tiles = head_turn[:, :].rearrange("p (t c) -> p t c", t=TT)
                    nc.vector.reciprocal(inv_sum[:, :], tiles[:, :, 2 * HD]).then_inc(inverted, 1)
                    nc.vector.tensor_reduce(head_sum[:, :, :], tiles[:, :, 0:2 * HD].rearrange("p t (a d) -> p t d a", a=2),
                                            AX.X, ALU.add).then_inc(head_summed, 1)

                dve.wait_ge(mask_in, b * 16 + 16)
                if not first:
                    dve.wait_ge(masked, b * UNITS)
                nc.vector.tensor_scalar(mask[:, :, :], mask8[:, :, :], MASKED, None, ALU.mult).then_inc(mask_set, 1)
                for i in range(IT_L):
                    if i == IT_L - 1:
                        scores(0)
                        scores(1)
                    item(i)
                for n in range(2, UNITS):
                    scores(n)
                    if n >= 3:
                        lo(n - 3)
                    if n >= 11 and (n - 11) % TT == 0:
                        head((n - 11) // TT)
                for n in range(UNITS - 3, UNITS):
                    lo(n)
                for n, i in enumerate(lates(last)):
                    if n == 2:
                        head(H - 2)
                        head(H - 1)
                    if is_turn(i):
                        transpose_lo(b, i, last)
                    else:
                        item(i)

            for i in range(-TT, 0):
                transpose_lo(0, i, False)
            each_batch(dve, body)

        @block.tensor
        def _(pe):
            def transpose(b, i, last):
                what, k = late(i)
                if i == -TT:
                    pe.wait_ge(x_in, 32)
                elif i >= IT_L and (what, k) == ("x", 0):
                    pe.wait_ge(x_in, b * 32 + 64)
                elif what == "context" and k % 2 == 0:
                    pe.wait_ge(head_out, b * H + (H // 2 if k == 0 else H))
                if i == IT_L:
                    pe.wait_ge(scored, b * UNITS + UNITS)
                if i in (-2, -1) or i >= IT_L + 2:
                    pe.wait_ge(item_out, done(b, before(i), last))
                for j in range(TT):
                    src = (context[:, j] if what == "context" else x_tile(ahead_x, j))[:, k * P:(k + 1) * P]
                    mm = pe.transpose(item_bank(i)[:, j * P:(j + 1) * P], src, keep.ident[:, :])
                mm.then_inc(item_mm, 1)

            def body(b, first, last):
                def item(i):
                    k = i % TT
                    bank = item_bank(i)
                    if i == 0:
                        pe.wait_ge(item_out, TT if first else done(b - 1, LATE.index(("x", 3)) + IT_L, False))
                    elif not first or i >= IT_K:
                        pe.wait_ge(item_out, done(b, i - TT, False))
                    if first and k == 0:
                        pe.wait_ge(w_lo, i // TT + 1)
                    if i < IT_V:
                        wh, wl = weight["q" if i < IT_K else "k"]
                        cut = slice(qk_tile(k) * P, (qk_tile(k) + 1) * P)
                        mm = split_product(pe, bank[:, :], [(wh[:, j, cut], wl[:, j, cut], xt[0][:, j, :], xt[1][:, j, :])
                                                            for j in range(KT)])
                    else:
                        (wh, wl), (hi, lo) = weight["v"], xt
                        cut = slice(k * P, (k + 1) * P)
                        mm = split_product(pe, bank[:, :], [(hi[:, j, cut], lo[:, j, cut], wh[:, j, :], wl[:, j, :])
                                                            for j in range(KT)])
                    mm.then_inc(item_mm, 1)

                def output(k, half):
                    if k == 0:
                        pe.wait_ge(item_out, done(b, IT_L + LATE.index(("context", 2 * half + 1)), last))
                    if first and k == 0:
                        pe.wait_ge(w_lo, TT)
                    (wh, wl), (hi, lo), cut, bank = weight["o"], ct, slice(k * P, (k + 1) * P), \
                        item_bank(IT_L + LATE.index(("output", k)))
                    for j in (2 * half, 2 * half + 1):
                        pe.matmul(bank[:, :], hi[:, j, cut], wh[:, j, :], start=j == 0, stop=False)
                        pe.matmul(bank[:, :], lo[:, j, cut], wh[:, j, :], start=False, stop=False)
                        mm = pe.matmul(bank[:, :], hi[:, j, cut], wl[:, j, :], start=False, stop=j == KT - 1)
                    if half == 1:
                        mm.then_inc(item_mm, 1)

                def scores(n):
                    h, u = divmod(n, TT)
                    pair = h // 2
                    if n % PAIR == 0:
                        pe.wait_ge(stack_in[pair % 2], b * (H // 4 * 5 * 16) + (pair // 2 + 1) * 5 * 16)
                    if n >= 3:
                        pe.wait_ge(scored, b * UNITS + n - 2)
                    pe.matmul(score[n % 3][:, :], stack[pair % 2][:, 0, h % 2, u * P:(u + 1) * P], stack[pair % 2][:, 1, h % 2, :],
                              start=True, stop=True).then_inc(score_mm, 1)

                def turn_unit(n):
                    pe.wait_ge(exped, b * UNITS + n + 1)
                    if n < 3:
                        pe.wait_ge(item_out, done(b, IT_V + n, False))
                    if n >= 3:
                        pe.wait_ge(p_lo, b * UNITS + n - 2)
                    for k in range(KT):
                        mm = pe.transpose(turn[n % 3][:, k * P:(k + 1) * P], bias[:, n % SLOTS, k * P:(k + 1) * P],
                                          keep.ident[:, :])
                    mm.then_inc(turned, 1)

                def head(h, half):
                    if half == 0:
                        pe.wait_ge(p_lo, b * UNITS + (h + 1) * TT)
                        if h == 0:
                            pe.wait_ge(item_out, done(b, IT_L - 1, False))
                        if h >= 1:
                            pe.wait_ge(head_flat, b * H + h)
                    for k in (2 * half, 2 * half + 1):
                        start = (k * H + ORDER[h]) * VW
                        vk = v[:, start:start + P]
                        pe.matmul(head_ps[:, :], vk, pt_hi[h % 2][:, k, :], start=k == 0, stop=False)
                        mm = pe.matmul(head_ps[:, :], vk, pt_lo[h % 2][:, k, :], start=False, stop=k == KT - 1)
                    if half == 1:
                        mm.then_inc(head_mm, 1)

                def turn_head(h):
                    pe.wait_ge(head_flat, b * H + h + 1)
                    if h >= 1:
                        pe.wait_ge(head_summed, b * H + h)
                    for i in range(TT):
                        mm = pe.transpose(head_turn[:, i * P:(i + 1) * P], ctx_flat[:, i * P:(i + 1) * P], keep.ident[:, :])
                    mm.then_inc(head_turned, 1)

                for i in range(IT_L):
                    if i == IT_L - 1:
                        scores(0)
                        scores(1)
                    item(i)
                scores(2)
                for n in range(UNITS):
                    if n + 3 < UNITS:
                        scores(n + 3)
                    turn_unit(n)
                    if n >= 7 and (n - 7) % TT == 0:
                        head((n - 7) // TT, 0)
                    if n >= 8 and (n - 8) % TT == 0:
                        head((n - 8) // TT, 1)
                    if n >= 10 and (n - 10) % TT == 0:
                        turn_head((n - 10) // TT)
                head(H - 2, 1)
                transpose(b, IT_L, last)
                transpose(b, IT_L + 1, last)
                turn_head(H - 2)
                head(H - 1, 0)
                head(H - 1, 1)
                output(0, 0)
                turn_head(H - 1)
                output(1, 0)
                todo = lates(last)[2:]
                if not last:
                    transpose(b, todo.pop(0), last)
                output(2, 0)
                transpose(b, todo.pop(0), last)
                transpose(b, todo.pop(0), last)
                output(3, 0)
                for i in todo:
                    if is_turn(i):
                        transpose(b, i, last)
                    else:
                        output(late(i)[1], 1)

            for i in range(-TT, 0):
                transpose(0, i, False)
            each_batch(pe, body)


class Keep:

    def __init__(self, nc, ctx):
        sb = lambda n, s: ctx.enter_context(nc.sbuf_tensor(n, s, F32))
        self.ident = sb("ident", [P, P])
        self.circuit = sb("circuit", [DIM, 2 * DIM])
        self.zpu = sb("zpu", [2 * DIM, D])
        self.take_q = sb("take_q", [P, B])
        self.take_f = sb("take_f", [P, B])
        self.q_factor = sb("q_factor", [P, B])


def build(nc, t, consts, out):
    scratch = {"x1": nc.dram_tensor("x1_scratch", (B, S, D), F32, kind="Internal").ap(),
               "x2": nc.dram_tensor("x2_scratch", (B, S, D), F32, kind="Internal").ap(),
               "ada": nc.dram_tensor("ada_scratch", (B, 2 * D), F32, kind="Internal").ap()}
    with ExitStack() as ctx, nc.allow_non_contiguous_dma(reason="small bias vectors as columns"):
        keep = Keep(nc, ctx)
        ffn_stage(nc, keep, t, consts, scratch, True, scratch["x1"])
        attention_stage(nc, keep, t, scratch)
        ffn_stage(nc, keep, t, consts, scratch, False, out)


def circuit_constants():
    bit = lambda i, w: i >> (WIRES - 1 - w) & 1

    def permuted(l):
        to = []
        for i in range(DIM):
            v = [bit(i, w) for w in range(WIRES)]
            for c in range(WIRES):
                if v[c]:
                    v[(c + l + 1) % WIRES] ^= 1
            to.append(sum(x << (WIRES - 1 - w) for w, x in enumerate(v)))
        return to

    to1, to2 = permuted(0), permuted(1)
    from1 = [to1.index(k) for k in range(DIM)]
    entry = {(0, 0): np.pi / 2, (0, 1): np.pi, (1, 0): 0.0, (1, 1): np.pi / 2}
    voff = np.zeros((DIM, LAYERS * WIRES * DIM + 4), np.float64)
    vcoef = np.zeros((DIM, 2, LAYERS * WIRES * 3), np.float64)
    for k in range(DIM):
        for w in range(WIRES):
            for i in range(DIM):
                voff[k, w * DIM + i] = entry[bit(from1[k], w), bit(i, w)]
                voff[k, (WIRES + w) * DIM + i] = entry[bit(i, w), bit(k, w)]
            vcoef[k, 0, w * 3 + 2] = 0.5 if bit(from1[k], w) else -0.5
            vcoef[k, 0, (WIRES + w) * 3] = 0.5 if bit(k, w) else -0.5
            vcoef[k, 1, w * 3] = 0.5 if bit(k, w) else -0.5
        n = LAYERS * WIRES * DIM
        ones = bin(k).count("1")
        voff[k, n:] = [0.0, np.pi / 2, -np.pi / 2 * ones, np.pi / 2 - np.pi / 2 * ones]
    sign = np.array([[1.0 - 2.0 * bit(to2[j], w) for j in range(DIM)] for w in range(WIRES)])
    return voff, vcoef, np.concatenate([sign, sign], axis=1)


def constants():
    voff, vcoef, zsign = circuit_constants()
    half = D // 2
    freqs = np.exp(np.arange(half) * (-np.log(10000.0) / (half - 1)))
    c = {"ident": np.eye(P), "freqs": freqs.reshape(2, P).T, "voff": voff, "vcoef": vcoef, "zsign": zsign}
    return {k: np.ascontiguousarray(v, dtype=np.float32) for k, v in c.items()}


_INS = ["x", "condB_vol", "itok_B_34_63", "fside_Bx16xSxS_0", "mask_Bx1xSxS_bk0"] + [
    f"L0_cond_{n}" for n in ("w1", "b1", "w2", "b2", "pd_w", "pd_b", "vqc_w", "pu_w", "pu_b", "q_scale", "ln_g", "ln_b")] + [
    f"L1_cond_{n}" for n in ("W_ada", "b_ada", "Wq", "bq", "Wk", "bk", "Wv", "bv", "Wo", "bo", "W1", "b1", "W2", "b2",
                             "g2", "beta2")]


def kernel(**inputs):
    import concourse.bacc as _bacc
    from concourse.bass_utils import run_bass_kernel_spmd as _run

    nc = _bacc.Bacc("TRN2", target_bir_lowering=False, num_devices=1)
    arrays, t, consts = {}, {}, {}
    for name in _INS:
        a = np.ascontiguousarray(inputs[name])
        arrays[f"in_{name}"] = a
        t[name] = nc.dram_tensor(f"in_{name}", a.shape, mybir.dt.from_np(a.dtype), kind="ExternalInput").ap()
    for name, a in constants().items():
        arrays[f"const_{name}"] = a
        consts[name] = nc.dram_tensor(f"const_{name}", a.shape, mybir.dt.from_np(a.dtype), kind="ExternalInput").ap()
    out = nc.dram_tensor("out", (B, S, D), F32, kind="ExternalOutput").ap()
    build(nc, t, consts, out)
    r = _run(nc, [arrays], core_ids=[0])
    return r.results[0]["out"]
```
